# Optimizing a Trainium2 kernel written in Bass

```python
import numpy as np
import jax
import jax.numpy as jnp

def _softmax(x, axis=-1):
    return jax.nn.softmax(x, axis=axis)

def _gelu(x):
    return jax.nn.gelu(x, approximate=True)

def _silu(x):
    return jax.nn.silu(x)

def _sigmoid(x):
    return jax.nn.sigmoid(x)

def _layernorm(x, axis=-1, eps=1e-05):
    m = jnp.mean(x, axis=axis, keepdims=True)
    v = jnp.var(x, axis=axis, keepdims=True)
    return (x - m) / jnp.sqrt(v + eps)

def _scatter_add(tgt, idx, src, axis=0):
    return tgt.at[idx].add(src)

def _segment_sum(src, seg, n):
    return jax.ops.segment_sum(src, seg, n)
kernel_name = 'mk_gnn_ffn_d2_gnn_r8_f908ac'

def setup_inputs(seed: int=0):
    np.random.seed(seed)
    _w = jnp.asarray

    def _rec_inputs():
        import jax
        import jax.numpy as jnp
        _gk = jax.random.key(seed)
        x = -7.329e-05 + 0.9999 * jax.random.normal(jax.random.fold_in(_gk, 1), (1250, 1024), jnp.float32)
        _s = jax.random.randint(jax.random.fold_in(_gk, 2), (10000,), 0, 1250, jnp.int32)
        _d = jax.random.randint(jax.random.fold_in(_gk, 3), (10000,), 0, 1250, jnp.int32)
        _loop = jnp.arange(1250, dtype=jnp.int32)
        src = jnp.concatenate([_s, _d, _loop])
        dst = jnp.concatenate([_d, _s, _loop])
        _o = jnp.argsort(dst, stable=True)
        src = src[_o]
        dst = dst[_o]
        edge_weight = -0.000130211 + 0.031236 * jax.random.normal(jax.random.fold_in(_gk, 12), (21250,), jnp.float32)
        return (x, src, dst, edge_weight)
    x, src, dst, edge_weight = _rec_inputs()

    def _L0_gnn_setup():
        import jax, jax.numpy as jnp
        import numpy as np
        INDIM = 1024
        OUTDIM = 1024
        NNZ = 8192
        N = 6250
        key = jax.random.key(seed)
        k1, k2, k3, k4, k5 = jax.random.split(key, 5)
        x = jax.random.normal(k1, (N, INDIM), dtype=jnp.float32)
        stdv = np.sqrt(6.0 / (INDIM + OUTDIM))
        nnz_weight = jax.random.uniform(k2, (NNZ,), dtype=jnp.float32, minval=-stdv, maxval=stdv)
        bias = jax.random.normal(k3, (OUTDIM,), dtype=jnp.float32) * 0.02
        row = jax.random.randint(k4, (NNZ,), 0, OUTDIM, dtype=jnp.int64)
        col = jax.random.randint(k5, (NNZ,), 0, INDIM, dtype=jnp.int64)
        edge_index = jnp.stack([row, col])
        return {'x': x, 'nnz_weight': nnz_weight, 'bias': bias, 'edge_index': edge_index}
    _L0_gnn_all = _L0_gnn_setup()
    _L0_gnn_in = {k: v for k, v in _L0_gnn_all.items() if k in ('bias',)}
    del _L0_gnn_all

    def _L0_ffn_setup():
        import jax, jax.numpy as jnp
        import numpy as np
        B, S, D, H, M, E, K = (4, 256, 1024, 256, 64, 8, 2)

        def _layernorm(x, g, b, eps=1e-05):
            mu = x.mean(-1, keepdims=True)
            var = ((x - mu) ** 2).mean(-1, keepdims=True)
            return (x - mu) * jax.lax.rsqrt(var + eps) * g + b

        def _forward(inputs_embeds, enc_W, enc_b, s2c_W, s2c_b, rW1, rb1, rW2, rb2, We1, be1, We2, be2, c2s_W, c2s_b, dec_W, dec_b, ln_g, ln_b):
            b, s, _ = inputs_embeds.shape
            spikes_enc = jax.nn.sigmoid(inputs_embeds @ enc_W + enc_b)
            flat = spikes_enc.reshape(b * s, H)
            cont = flat @ s2c_W + s2c_b
            logits = jnp.tanh(cont @ rW1 + rb1) @ rW2 + rb2
            probs = jax.nn.softmax(logits, axis=-1)
            topw, topi = jax.lax.top_k(probs, K)
            w = topw / topw.sum(-1, keepdims=True)
            gates = (jax.nn.one_hot(topi, E, dtype=cont.dtype) * w[..., None]).sum(1)
            h = jax.nn.relu(jnp.einsum('nm,emh->enh', cont, We1) + be1[:, None, :])
            expert_out = jnp.einsum('enh,ehm->enm', h, We2) + be2[:, None, :]
            output_flat = jnp.einsum('enm,ne->nm', expert_out, gates)
            spikes_moe = jax.nn.sigmoid(output_flat @ c2s_W + c2s_b).reshape(b, s, H)
            decoded = jax.nn.sigmoid(spikes_moe @ dec_W + dec_b)
            return _layernorm(decoded, ln_g, ln_b)
        key = jax.random.key(seed)
        ks = jax.random.split(key, 10)
        r = lambda k, shape: jax.random.normal(k, shape, dtype=jnp.float32) * 0.02
        return {'inputs_embeds': jax.random.normal(ks[0], (B, S, D), dtype=jnp.float32), 'enc_W': r(ks[1], (D, H)), 'enc_b': jnp.zeros((H,), jnp.float32), 's2c_W': r(ks[2], (H, M)), 's2c_b': jnp.zeros((M,), jnp.float32), 'rW1': r(ks[3], (M, 64)), 'rb1': jnp.zeros((64,), jnp.float32), 'rW2': r(ks[4], (64, E)), 'rb2': jnp.zeros((E,), jnp.float32), 'We1': r(ks[5], (E, M, H // 2)), 'be1': jnp.zeros((E, H // 2), jnp.float32), 'We2': r(ks[6], (E, H // 2, M)), 'be2': jnp.zeros((E, M), jnp.float32), 'c2s_W': r(ks[7], (M, H)), 'c2s_b': jnp.zeros((H,), jnp.float32), 'dec_W': r(ks[8], (H, D)), 'dec_b': jnp.zeros((D,), jnp.float32), 'ln_g': jnp.ones((D,), jnp.float32), 'ln_b': jnp.zeros((D,), jnp.float32)}
    _L0_ffn_all = _L0_ffn_setup()
    _L0_ffn_in = {k: v for k, v in _L0_ffn_all.items() if k in ('enc_W', 'enc_b', 's2c_W', 's2c_b', 'rW1', 'rb1', 'rW2', 'rb2', 'We1', 'be1', 'We2', 'be2', 'c2s_W', 'c2s_b', 'dec_W', 'dec_b', 'ln_g', 'ln_b')}
    del _L0_ffn_all

    def _L1_gnn_setup():
        import jax, jax.numpy as jnp
        import numpy as np
        N_NODES = 1250
        N_EDGES = 20000
        DIM = 1024
        key = jax.random.key(seed)
        k1, k2, k3 = jax.random.split(key, 3)
        x = jax.random.normal(k1, (N_NODES, DIM), dtype=jnp.float32)
        edge_index = jax.random.randint(k2, (2, N_EDGES), 0, N_NODES, dtype=jnp.int64)
        W = jax.random.normal(k3, (DIM, DIM), dtype=jnp.float32) * (1.0 / np.sqrt(DIM))
        b = jnp.zeros((DIM,), dtype=jnp.float32)
        return {'x': x, 'edge_index': edge_index, 'W': W, 'b': b}
    _L1_gnn_all = _L1_gnn_setup()
    _L1_gnn_in = {k: v for k, v in _L1_gnn_all.items() if k in ('W', 'b')}
    del _L1_gnn_all

    def _L1_ffn_setup():
        import jax, jax.numpy as jnp
        import numpy as np
        BLOCK = 32
        W_BITS = 4
        ACT_BITS = 16

        def act_qdq(x):
            qmax = 2.0 ** (ACT_BITS - 1) - 1.0
            scale = jnp.maximum(jnp.max(jnp.abs(x)) / qmax, 1e-12)
            return jnp.clip(jnp.round(x / scale), -qmax - 1.0, qmax) * scale

        def fixed_qdq_u16(x):
            scale = 1.0 / 65536.0
            return jnp.clip(jnp.round(x / scale), 0.0, 65535.0) * scale

        def lpbq_dequant(w):
            O, I = w.shape
            qmax = 2.0 ** (W_BITS - 1) - 1.0
            wb = w.reshape(O, I // BLOCK, BLOCK)
            s = jnp.maximum(jnp.max(jnp.abs(wb), axis=-1, keepdims=True) / qmax, 1e-12)
            wq = jnp.clip(jnp.round(wb / s), -qmax - 1.0, qmax) * s
            return wq.reshape(O, I)
        key = jax.random.key(seed)
        k1, k2, k3, k4 = jax.random.split(key, 4)
        B, S, H, I = (2, 512, 1024, 384)
        x = jax.random.normal(k1, (B, S, H), jnp.float32)
        w_gate = jax.random.normal(k2, (I, H), jnp.float32) * 0.02
        w_up = jax.random.normal(k3, (I, H), jnp.float32) * 0.02
        w_down = jax.random.normal(k4, (H, I), jnp.float32) * 0.02
        return {'x': x, 'w_gate': w_gate, 'w_up': w_up, 'w_down': w_down}
    _L1_ffn_all = _L1_ffn_setup()
    _L1_ffn_in = {k: v for k, v in _L1_ffn_all.items() if k in ('w_gate', 'w_up', 'w_down')}
    del _L1_ffn_all
    return {'x': x, 'src': src, 'dst': dst, 'edge_weight': edge_weight, 'L0_gnn_bias': _L0_gnn_in['bias'], 'L0_ffn_enc_W': _L0_ffn_in['enc_W'], 'L0_ffn_enc_b': _L0_ffn_in['enc_b'], 'L0_ffn_s2c_W': _L0_ffn_in['s2c_W'], 'L0_ffn_s2c_b': _L0_ffn_in['s2c_b'], 'L0_ffn_rW1': _L0_ffn_in['rW1'], 'L0_ffn_rb1': _L0_ffn_in['rb1'], 'L0_ffn_rW2': _L0_ffn_in['rW2'], 'L0_ffn_rb2': _L0_ffn_in['rb2'], 'L0_ffn_We1': _L0_ffn_in['We1'], 'L0_ffn_be1': _L0_ffn_in['be1'], 'L0_ffn_We2': _L0_ffn_in['We2'], 'L0_ffn_be2': _L0_ffn_in['be2'], 'L0_ffn_c2s_W': _L0_ffn_in['c2s_W'], 'L0_ffn_c2s_b': _L0_ffn_in['c2s_b'], 'L0_ffn_dec_W': _L0_ffn_in['dec_W'], 'L0_ffn_dec_b': _L0_ffn_in['dec_b'], 'L0_ffn_ln_g': _L0_ffn_in['ln_g'], 'L0_ffn_ln_b': _L0_ffn_in['ln_b'], 'L1_gnn_W': _L1_gnn_in['W'], 'L1_gnn_b': _L1_gnn_in['b'], 'L1_ffn_w_gate': _L1_ffn_in['w_gate'], 'L1_ffn_w_up': _L1_ffn_in['w_up'], 'L1_ffn_w_down': _L1_ffn_in['w_down']}

def reference(x, src, dst, edge_weight, L0_gnn_bias, L0_ffn_enc_W, L0_ffn_enc_b, L0_ffn_s2c_W, L0_ffn_s2c_b, L0_ffn_rW1, L0_ffn_rb1, L0_ffn_rW2, L0_ffn_rb2, L0_ffn_We1, L0_ffn_be1, L0_ffn_We2, L0_ffn_be2, L0_ffn_c2s_W, L0_ffn_c2s_b, L0_ffn_dec_W, L0_ffn_dec_b, L0_ffn_ln_g, L0_ffn_ln_b, L1_gnn_W, L1_gnn_b, L1_ffn_w_gate, L1_ffn_w_up, L1_ffn_w_down):
    import jax
    import jax.numpy as jnp

    def _L0_gnn_ref(x, nnz_weight, bias, edge_index):
        import jax, jax.numpy as jnp
        import numpy as np
        INDIM = 1024
        OUTDIM = 1024
        NNZ = 8192
        N = 6250
        row, col = (edge_index[0], edge_index[1])
        W = jnp.zeros((OUTDIM, INDIM), dtype=nnz_weight.dtype).at[row, col].add(nnz_weight)
        return x @ W.T + bias

    def _L0_ffn_ref(inputs_embeds, enc_W, enc_b, s2c_W, s2c_b, rW1, rb1, rW2, rb2, We1, be1, We2, be2, c2s_W, c2s_b, dec_W, dec_b, ln_g, ln_b):
        import jax, jax.numpy as jnp
        import numpy as np
        B, S, D, H, M, E, K = (4, 256, 1024, 256, 64, 8, 2)

        def _layernorm(x, g, b, eps=1e-05):
            mu = x.mean(-1, keepdims=True)
            var = ((x - mu) ** 2).mean(-1, keepdims=True)
            return (x - mu) * jax.lax.rsqrt(var + eps) * g + b

        def _forward(inputs_embeds, enc_W, enc_b, s2c_W, s2c_b, rW1, rb1, rW2, rb2, We1, be1, We2, be2, c2s_W, c2s_b, dec_W, dec_b, ln_g, ln_b):
            b, s, _ = inputs_embeds.shape
            spikes_enc = jax.nn.sigmoid(inputs_embeds @ enc_W + enc_b)
            flat = spikes_enc.reshape(b * s, H)
            cont = flat @ s2c_W + s2c_b
            logits = jnp.tanh(cont @ rW1 + rb1) @ rW2 + rb2
            probs = jax.nn.softmax(logits, axis=-1)
            topw, topi = jax.lax.top_k(probs, K)
            w = topw / topw.sum(-1, keepdims=True)
            gates = (jax.nn.one_hot(topi, E, dtype=cont.dtype) * w[..., None]).sum(1)
            h = jax.nn.relu(jnp.einsum('nm,emh->enh', cont, We1) + be1[:, None, :])
            expert_out = jnp.einsum('enh,ehm->enm', h, We2) + be2[:, None, :]
            output_flat = jnp.einsum('enm,ne->nm', expert_out, gates)
            spikes_moe = jax.nn.sigmoid(output_flat @ c2s_W + c2s_b).reshape(b, s, H)
            decoded = jax.nn.sigmoid(spikes_moe @ dec_W + dec_b)
            return _layernorm(decoded, ln_g, ln_b)
        return _forward(inputs_embeds, enc_W, enc_b, s2c_W, s2c_b, rW1, rb1, rW2, rb2, We1, be1, We2, be2, c2s_W, c2s_b, dec_W, dec_b, ln_g, ln_b)

    def _L1_gnn_ref(x, edge_index, W, b):
        import jax, jax.numpy as jnp
        import numpy as np
        N_NODES = 1250
        N_EDGES = 20000
        DIM = 1024
        'GCNConv (add_self_loops=True, symmetric norm) -> Dropout(eval=identity) -> ReLU.'
        n = x.shape[0]
        loops = jnp.arange(n, dtype=edge_index.dtype)
        src = jnp.concatenate([edge_index[0], loops])
        dst = jnp.concatenate([edge_index[1], loops])
        deg = jax.ops.segment_sum(jnp.ones_like(dst, dtype=x.dtype), dst, num_segments=n)
        dinv = jnp.where(deg > 0, jax.lax.rsqrt(deg), jnp.zeros_like(deg))
        norm = dinv[src] * dinv[dst]
        h = x @ W
        msg = h[src] * norm[:, None]
        out = jax.ops.segment_sum(msg, dst, num_segments=n) + b
        return jax.nn.relu(out)

    def _L1_ffn_ref(x, w_gate, w_up, w_down):
        import jax, jax.numpy as jnp
        import numpy as np
        BLOCK = 32
        W_BITS = 4
        ACT_BITS = 16

        def act_qdq(x):
            qmax = 2.0 ** (ACT_BITS - 1) - 1.0
            scale = jnp.maximum(jnp.max(jnp.abs(x)) / qmax, 1e-12)
            return jnp.clip(jnp.round(x / scale), -qmax - 1.0, qmax) * scale

        def fixed_qdq_u16(x):
            scale = 1.0 / 65536.0
            return jnp.clip(jnp.round(x / scale), 0.0, 65535.0) * scale

        def lpbq_dequant(w):
            O, I = w.shape
            qmax = 2.0 ** (W_BITS - 1) - 1.0
            wb = w.reshape(O, I // BLOCK, BLOCK)
            s = jnp.maximum(jnp.max(jnp.abs(wb), axis=-1, keepdims=True) / qmax, 1e-12)
            wq = jnp.clip(jnp.round(wb / s), -qmax - 1.0, qmax) * s
            return wq.reshape(O, I)
        x = act_qdq(x)
        up = act_qdq(x @ lpbq_dequant(w_up).T)
        gate = act_qdq(x @ lpbq_dequant(w_gate).T)
        sig = fixed_qdq_u16(jax.nn.sigmoid(gate))
        gate = act_qdq(gate * sig)
        o = act_qdq(gate * up)
        return o @ lpbq_dequant(w_down).T
    edge_index = jnp.stack([src, dst])
    x = x + _L0_gnn_ref(_layernorm(x, axis=-1), edge_weight, L0_gnn_bias, edge_index)
    x = x + _L0_ffn_ref(_layernorm(x, axis=-1)[None], L0_ffn_enc_W, L0_ffn_enc_b, L0_ffn_s2c_W, L0_ffn_s2c_b, L0_ffn_rW1, L0_ffn_rb1, L0_ffn_rW2, L0_ffn_rb2, L0_ffn_We1, L0_ffn_be1, L0_ffn_We2, L0_ffn_be2, L0_ffn_c2s_W, L0_ffn_c2s_b, L0_ffn_dec_W, L0_ffn_dec_b, L0_ffn_ln_g, L0_ffn_ln_b)[0]
    x = x + _L1_gnn_ref(_layernorm(x, axis=-1), edge_index, L1_gnn_W, L1_gnn_b)
    x = x + _L1_ffn_ref(_layernorm(x, axis=-1)[None], L1_ffn_w_gate, L1_ffn_w_up, L1_ffn_w_down)[0]
    return x

_drawn_inputs = setup_inputs


def setup_inputs(seed=0):
    import zlib

    import numpy as np

    out = dict(_drawn_inputs(seed))
    spreads = {'L0_ffn_enc_b': (0.0, 0.8),
     'L0_ffn_s2c_b': (0.0, 0.8),
     'L0_ffn_rb1': (0.0, 0.8),
     'L0_ffn_rb2': (0.0, 0.8),
     'L0_ffn_be1': (0.0, 0.8),
     'L0_ffn_be2': (0.0, 0.8),
     'L0_ffn_c2s_b': (0.0, 0.529),
     'L0_ffn_dec_b': (0.0, 0.1),
     'L0_ffn_ln_g': (1.0, 0.2),
     'L0_ffn_ln_b': (0.0, 0.1),
     'L1_gnn_b': (0.0, 0.1)}
    factors = {'L0_gnn_bias': 3.718,
     'L0_ffn_enc_W': 8.0,
     'L0_ffn_s2c_W': 8.0,
     'L0_ffn_rW1': 8.0,
     'L0_ffn_rW2': 8.0,
     'L0_ffn_We1': 8.0,
     'L0_ffn_We2': 8.0,
     'L0_ffn_c2s_W': 8.0}
    for name, (base, spread) in spreads.items():
        noise = np.random.default_rng([zlib.crc32(name.encode()), seed]).standard_normal(out[name].shape)
        drawn = base * np.exp(spread * noise) if base else spread * noise
        out[name] = jnp.asarray(drawn.astype(out[name].dtype))
    for name, factor in factors.items():
        out[name] = (out[name] * factor).astype(out[name].dtype)
    return out
```

```python
from contextlib import ExitStack

import concourse.bass as bass
import numpy as np
from concourse import mybir

F32 = mybir.dt.float32
F32R = mybir.dt.float32r
BF16 = mybir.dt.bfloat16
F16 = mybir.dt.float16
U16 = mybir.dt.uint16
U32 = mybir.dt.uint32
I32 = mybir.dt.int32
ALU = mybir.AluOpType
ACT = mybir.ActivationFunctionType
AX = mybir.AxisListType
RMAX = bass.bass_isa.ReduceOp.max

N = 1250
D = 1024
E = 21250
P = 125
TILES = N // P
PAIRS = TILES // 2
ET = E // P
EH = ET // 2
WIN = 32
BLOCKS = 40
CHUNKS = 10
WCH = D // 128
KD = D // 128
RING = 4
H1 = 256
M1 = 64
EX = 8
QI = 384
QC = QI // 128
PAIR = 2 * P
EPS = 1e-5
X3_STEPS = 5
LAYER0 = ("gnn_bias", "ffn_enc_W", "ffn_enc_b", "ffn_s2c_W", "ffn_s2c_b", "ffn_rW1", "ffn_rb1", "ffn_rW2",
          "ffn_rb2", "ffn_We1", "ffn_be1", "ffn_We2", "ffn_be2", "ffn_c2s_W", "ffn_c2s_b", "ffn_dec_W",
          "ffn_dec_b", "ffn_ln_g", "ffn_ln_b")
STEPS = 15
MAGIC = 12582912.0


class Link:

    def __init__(self, eng, sem, base=0):
        self.eng, self.sem, self.base, self.n = eng, sem, base, 0

    def __call__(self, ins):
        self.step(ins)
        self.wait()

    def step(self, ins):
        ins.then_inc(self.sem, 1)
        self.n += 1

    def wait(self):
        self.eng.wait_ge(self.sem, self.base + self.n)


def sb(nc, ctx, name, shape, dt=F32):
    return ctx.enter_context(nc.sbuf_tensor(name, shape, dt))


def psum(nc, ctx, name, shape, dt=F32):
    return ctx.enter_context(nc.psum_tensor(name, shape, dt))


def sems(nc, ctx, *names):
    return [ctx.enter_context(nc.semaphore(n)) for n in names]


def build_matrices(nc, src, dst, weight, x, X, ident, WT, CT, dinv, deg_dram):
    with ExitStack() as ctx:
        dst_i = sb(nc, ctx, "dst_i", [EH, 2, P], I32)
        src_i = sb(nc, ctx, "src_i", [EH, 2, P], I32)
        rows = sb(nc, ctx, "rows", [EH, 3, 2, P])
        cols = sb(nc, ctx, "cols", [P, 3, ET])
        coef = sb(nc, ctx, "coef", [P, ET, 4], BF16)
        rest = sb(nc, ctx, "rest", [P, 2, ET])
        iota_i = sb(nc, ctx, "iota_i", [P, BLOCKS * WIN], I32)
        iota_h = sb(nc, ctx, "iota_h", [P, BLOCKS * WIN], F16)
        first_i = sb(nc, ctx, "first_i", [EH, BLOCKS + 4], I32)
        first = sb(nc, ctx, "first", [EH, BLOCKS + 4])
        ends = sb(nc, ctx, "ends", [EH, 4])
        touch = sb(nc, ctx, "touch", [EH, 2, BLOCKS])
        marks = sb(nc, ctx, "marks", [EH, 4, BLOCKS])
        most = sb(nc, ctx, "most", [EH, 4, BLOCKS])
        span = sb(nc, ctx, "span", [1, 2, BLOCKS])
        table = sb(nc, ctx, "table", [1, 2, BLOCKS], I32)
        left = sb(nc, ctx, "left", [P, RING, 128], BF16)
        right = sb(nc, ctx, "right", [P, RING, N], BF16)
        block_out = sb(nc, ctx, "block_out", [128, 4, N])
        degrees = sb(nc, ctx, "degrees", [128, BLOCKS])
        parts = sb(nc, ctx, "parts", [128, 2, 3, D])
        counts = sb(nc, ctx, "counts", [128, 2, N])
        deg = sb(nc, ctx, "deg", [P, TILES])
        mhalf = sb(nc, ctx, "mhalf", [P, TILES])
        held = sb(nc, ctx, "held", [1, 4])
        B = [psum(nc, ctx, f"B{i}", [128, 3 * 512]) for i in range(2)]
        TP = [psum(nc, ctx, f"TP{i}", [128, 512]) for i in range(2)]

        (edges_in, rows_ready, iota_ready, ident_ready, cols_turned, cols_ready, coef_ready, marks_ready,
         most_ready, table_ready, slot_free, pair_ready, block_built, block_copied, w_summed,
         turned, evacuated, loop_link, deg_out, deg_in, dinv_ready, x_in, diag_ready) = sems(
            nc, ctx, "edges_in", "rows_ready", "iota_ready", "ident_ready", "cols_turned", "cols_ready",
            "coef_ready", "marks_ready", "most_ready", "table_ready", "slot_free", "pair_ready",
            "block_built", "block_copied", "w_summed", "turned", "evacuated", "loop_link",
            "deg_out", "deg_in", "dinv_ready", "x_in", "diag_ready")
        moved = [sems(nc, ctx, *(f"moved{par}{q}" for q in range(4))) for par in range(2)]
        dve_link, pool_link = sems(nc, ctx, "dve_link", "pool_link")
        weights_in = sems(nc, ctx, "weights_in")[0]

        def chunk_pairs(eng, body):
            with eng.Fori(0, WCH // 2) as g:
                body(g, True, False)
            body(WCH // 2, False, True)

        block = ctx.enter_context(nc.Block())

        @block.sync
        def _(sp):
            for tile, ap in ((dst_i, dst), (src_i, src)):
                sp.dma_start(tile[:, :, :], ap.rearrange("(h q k) -> q h k", h=2, k=P)).then_inc(edges_in, 16)
            sp.dma_start(rows[:, 2], weight.rearrange("(h q k) -> q h k", h=2, k=P)).then_inc(edges_in, 16)

            copied, summed, read = (sp.alloc_register(n) for n in ("copied", "summed", "read"))
            for register, value in ((copied, 3), (summed, 1), (read, 3)):
                sp.reg_mov(register, value)

            def body(g, with_w, last):
                for par in range(2):
                    for q in range(4):
                        sp.wait_ge(block_copied, copied)
                        if q == 0:
                            sp.wait_ge(w_summed, summed)
                            sp.wait_ge(turned, read)
                        lanes = slice(32 * q, 32 * q + 32)
                        sp.dma_start(counts[lanes, par], block_out[0:32, q]).then_inc(moved[par][q], 16)
                        if with_w:
                            for k in range(3):
                                sp.dma_start(parts[lanes, par, k], block_out[32 * k + 32:32 * k + 64, q, 0:D]
                                             ).then_inc(moved[par][q], 16)
                        sp.reg_add(copied, copied, 1)
                        if q == 3:
                            sp.reg_add(summed, summed, 1)
                            sp.reg_add(read, read, 3)

            chunk_pairs(sp, body)
            sp.dma_start(deg_dram.rearrange("(b p) -> p b", p=WIN), degrees[0:32, :],
                         allow_slow_non_contiguous=True).then_inc(deg_out, 16)
            sp.wait_ge(deg_out, 16)
            sp.dma_start(deg[:, :], deg_dram[0:N].rearrange("(t p) -> p t", p=P),
                         allow_slow_non_contiguous=True).then_inc(deg_in, 16)
            sp.wait_ge(deg_in, 16)

        @block.gpsimd
        def _(pool):
            pool.memset(ident[:, :], 0.0).then_inc(pool_link, 1)
            pool.wait_ge(pool_link, 1)
            pool.affine_select(out=ident[:, :], in_=ident[:, :], compare_op=ALU.not_equal, fill=1.0, base=0,
                               pattern=[[-1, 128]], channel_multiplier=1).then_inc(ident_ready, 1)
            pool.iota(iota_i[:, :], [[1, BLOCKS * WIN]], base=0, channel_multiplier=0).then_inc(iota_ready, 1)
            pool.iota(first_i[:, 0:BLOCKS], [[WIN, BLOCKS]], base=0, channel_multiplier=0).then_inc(iota_ready, 1)
            pool.iota(first_i[:, BLOCKS:BLOCKS + 2], [[EH, 2]], base=1, channel_multiplier=1).then_inc(iota_ready, 1)
            pool.iota(first_i[:, BLOCKS + 2:], [[-EH, 2]], base=ET, channel_multiplier=-1).then_inc(iota_ready, 1)
            pool.memset(mhalf[:, :], -0.5).then_inc(iota_ready, 1)
            pool.wait_ge(marks_ready, 1)
            pool.partition_all_reduce(most[:, :, :], marks[:, :, :], EH, RMAX).then_inc(most_ready, 1)

            def hold(k):
                pool.tensor_tensor(held[:, k:k + 1], mhalf[0:1, 0:1], mhalf[0:1, 0:1], ALU.add)

            with pool.Fori(0, WCH // 2) as g:
                for par in range(2):
                    for q in range(4):
                        pool.wait_ge(moved[par][q], 64 * g + 64)
                    hold(2 * par)
                    c = 2 * g + par
                    out = WT[:, bass.ds(c, 1), :].rearrange("p a d -> p (a d)")
                    pool.tensor_tensor(out, parts[:, par, 0], parts[:, par, 1], ALU.add).then_inc(loop_link, 1)
                    pool.wait_ge(loop_link, c + 1)
                    hold(2 * par + 1)
                    pool.tensor_tensor(out, out, parts[:, par, 2], ALU.add).then_inc(w_summed, 1)
            pool.wait_ge(deg_in, 16)
            pool.tensor_scalar(deg[:, :], deg[:, :], 1.0, None, ALU.add).then_inc(pool_link, 1)
            pool.wait_ge(pool_link, 2)
            pool.wait_ge(iota_ready, 5)
            pool.tensor_tensor(dinv[:, :], deg[:, :], mhalf[:, :], ALU.pow).then_inc(dinv_ready, 1)

        @block.vector
        def _(dve):
            link = Link(dve, dve_link)
            dve.wait_ge(edges_in, 48)
            dve.tensor_copy(rows[:, 0], dst_i[:, :, :]).then_inc(rows_ready, 1)
            dve.tensor_copy(rows[:, 1], src_i[:, :, :]).then_inc(rows_ready, 1)
            dve.wait_ge(iota_ready, 4)
            dve.tensor_copy(iota_h[:, :], iota_i[:, :]).then_inc(dve_link, 1)
            link.n += 1
            dve.wait_ge(rows_ready, 1)
            link(dve.tensor_reduce(ends[:, 0:2], rows[:, 0], AX.X, ALU.min))
            link(dve.tensor_reduce(ends[:, 2:4], rows[:, 0], AX.X, ALU.max))
            link(dve.tensor_copy(first[:, :], first_i[:, :]))
            link(dve.tensor_scalar(ends[:, 0:2], ends[:, 0:2], -float(WIN), None, ALU.add))
            for h in range(2):
                link(dve.tensor_scalar(touch[:, h], first[:, 0:BLOCKS], ends[:, h:h + 1], None, ALU.is_gt))
                link(dve.scalar_tensor_tensor(touch[:, h], first[:, 0:BLOCKS], ends[:, 2 + h:3 + h], touch[:, h],
                                              ALU.is_le, ALU.mult))
                link(dve.tensor_scalar(marks[:, h], touch[:, h], first[:, BLOCKS + h:BLOCKS + h + 1], None,
                                       ALU.mult))
                ins = dve.tensor_scalar(marks[:, 2 + h], touch[:, h], first[:, BLOCKS + 2 + h:BLOCKS + 3 + h],
                                        None, ALU.mult)
                if h == 0:
                    link(ins)
            ins.then_inc(marks_ready, 1)
            dve.wait_ge(cols_turned, 1)
            dve.tensor_copy(cols[:, :, :].rearrange("p a t -> p (a t)"), TP[0][0:P, 0:3 * ET]).then_inc(cols_ready, 1)
            dve.memset(coef[:, :, 0], 1.0)
            dve.wait_ge(cols_ready, 1)
            link(dve.tensor_copy(coef[:, :, 1], cols[:, 2]))
            link(dve.tensor_tensor(rest[:, 0], cols[:, 2], coef[:, :, 1], ALU.subtract))
            link(dve.tensor_copy(coef[:, :, 2], rest[:, 0]))
            link(dve.tensor_tensor(rest[:, 1], rest[:, 0], coef[:, :, 2], ALU.subtract))
            dve.tensor_copy(coef[:, :, 3], rest[:, 1]).then_inc(coef_ready, 1)
            dve.wait_ge(most_ready, 1)
            link(dve.tensor_tensor(span[:, 1], most[0:1, 0], most[0:1, 1], ALU.max))
            link(dve.tensor_tensor(span[:, 0], most[0:1, 2], most[0:1, 3], ALU.max))
            link(dve.tensor_scalar(span[:, 0], span[:, 0], -1.0, float(ET), ALU.mult, ALU.add))
            link(dve.tensor_scalar(span[:, 0], span[:, 0], float(ET - 3), None, ALU.min))
            link(dve.scalar_tensor_tensor(span[:, 1], span[:, 0], 3.0, span[:, 1], ALU.add, ALU.max))
            dve.tensor_copy(table[:, :, :], span[:, :, :]).then_inc(table_ready, 1)
            dve.wait_ge(table_ready, 1)
            dve.wait_ge(coef_ready, 1)

            done = dve.alloc_register("onehots_made")
            dve.reg_mov(done, 0)

            def body(g, with_w, last):
                for k in range(8):
                    b = 8 * g + k
                    lo = dve.value_load(table[0:1, 0, bass.ds(b, 1)], min_val=0, max_val=ET - 3)
                    hi = dve.value_load(table[0:1, 1, bass.ds(b, 1)], min_val=3, max_val=ET)
                    with dve.Fori(lo, hi) as t:
                        n = dve.snap(done, min_val=0, max_val=BLOCKS * ET)
                        slot = n % RING
                        dve.wait_ge(slot_free, n + 1)
                        dve.scalar_tensor_tensor(
                            left[:, bass.ds(slot, 1), :].rearrange("p a (k d) -> p (a k) d", k=4),
                            iota_h[:, bass.ds(WIN * b, WIN)].unsqueeze(1).broadcast_to([P, 4, WIN]),
                            cols[:, 0, bass.ds(t, 1)],
                            coef[:, bass.ds(t, 1), :].rearrange("p a k -> p (a k)").unsqueeze(2).broadcast_to([P, 4, WIN]),
                            ALU.is_equal, ALU.mult)
                        dve.tensor_scalar(right[:, bass.ds(slot, 1), :].rearrange("p a d -> p (a d)"),
                                          iota_h[:, 0:N], cols[:, 1, bass.ds(t, 1)], None,
                                          ALU.is_equal).then_inc(pair_ready, 1)
                        dve.reg_add(done, done, 1)

            chunk_pairs(dve, body)
            for j in range(TILES):
                dve.wait_ge(evacuated, 3 * CHUNKS + 2)
                ins = dve.tensor_tensor(CT[0:P, j, P * j:P * j + P], CT[0:P, j, P * j:P * j + P], ident[0:P, 0:P], ALU.add)
            ins.then_inc(diag_ready, 1)
            dve.wait_ge(diag_ready, 1)

        @block.tensor
        def _(pe):
            pe.sem_inc(slot_free, RING)
            for free in (block_copied, evacuated, w_summed):
                pe.sem_inc(free, 2)
            pe.sem_inc(turned, 6)
            pe.wait_ge(edges_in, 48)
            pe.wait_ge(rows_ready, 2)
            pe.wait_ge(ident_ready, 1)
            for k in range(3):
                for h in range(2):
                    at = (2 * k + h) * EH
                    ins = pe.transpose(TP[0][0:P, at:at + EH], rows[:, k, h], ident[0:EH, 0:EH])
            ins.then_inc(cols_turned, 1)
            pe.wait_ge(cols_ready, 1)
            pe.wait_ge(table_ready, 1)
            used = pe.alloc_register("onehots_used")
            pe.reg_mov(used, 0)

            def one_hot_products(out, start, stop):
                n = pe.snap(used, min_val=0, max_val=BLOCKS * ET)
                slot = n % RING
                pe.wait_ge(pair_ready, n + 1)
                lhs = left[:, bass.ds(slot, 1), :].rearrange("p a d -> p (a d)")
                for at in range(0, N, 512):
                    size = min(512, N - at)
                    ins = pe.matmul(out[:, at:at + size], lhs,
                                    right[:, bass.ds(slot, 1), at:at + size].rearrange("p a d -> p (a d)"),
                                    start=start, stop=stop)
                ins.then_inc(slot_free, 1)
                if stop:
                    pe.matmul(out[:, 1535:1536], coef[:, 0:32, :].rearrange("p t k -> p (t k)"),
                              coef[:, 0, 0:1], start=True, stop=True).then_inc(block_built, 1)
                pe.reg_add(used, used, 1)

            def build(g, k):
                b = 8 * g + k
                pe.wait_ge(block_copied, b + 1)
                lo = pe.value_load(table[0:1, 0, bass.ds(b, 1)], min_val=0, max_val=ET - 3)
                hi = pe.value_load(table[0:1, 1, bass.ds(b, 1)], min_val=3, max_val=ET)
                one_hot_products(B[k % 2], True, False)
                with pe.Fori(lo + 1, hi - 1) as t:
                    one_hot_products(B[k % 2], False, False)
                one_hot_products(B[k % 2], False, True)

            def turn(g, par, per):
                for q in range(4):
                    pe.wait_ge(moved[par][q], per)
                for k in range(3):
                    pe.wait_ge(evacuated, 6 * g + 3 * par + k + 1)
                    for j in range(4 * k, min(4 * k + 4, TILES)):
                        ins = pe.transpose(TP[(k + par) % 2][0:P, 128 * (j % 4):128 * (j % 4) + 128],
                                           counts[:, par, P * j:P * j + P], ident[:, :])
                    ins.then_inc(turned, 1)

            def body(g, with_w, last):
                got = 64 * g + 64 if with_w else 64 * g + 16
                for k in (2, 3, 4, 5):
                    build(g, k)
                turn(g, 0, got)
                for k in (6, 7) + (() if last else (8, 9)):
                    build(g, k)
                turn(g, 1, got)

            build(0, 0)
            build(0, 1)
            chunk_pairs(pe, body)

        @block.scalar
        def _(act):
            for t in range(TILES):
                act.dma_start(X[:, t], x[P * t:P * t + P, :]).then_inc(x_in, 16)

            def copy(g, k, last_pair=False):
                b, q = 8 * g + k, k % 4
                act.wait_ge(block_built, b + 1)
                if k >= 8:
                    act.wait_ge(moved[1][q], 64 * g + 64)
                elif k >= 4:
                    act.wait_ge(moved[0][q], 64 * g + (64 if not last_pair else 16))
                act.activation(block_out[:, q], B[k % 2][:, 0:N], ACT.Copy,
                               accum_out=degrees[:, bass.ds(b, 1)]).then_inc(block_copied, 1)

            def evacuate(g, par):
                for k in range(3):
                    j, m = 4 * k, min(4, TILES - 4 * k)
                    act.wait_ge(turned, 6 * g + 3 * par + k + 7)
                    act.activation(CT[0:P, j:j + m, bass.ds(128 * (2 * g + par), 128)],
                                   TP[(k + par) % 2][0:P, 0:128 * m].rearrange("p (j d) -> p j d", j=m),
                                   ACT.Copy).then_inc(evacuated, 1)

            def body(g, with_w, last):
                for k in (2, 3, 4, 5):
                    copy(g, k, last)
                evacuate(g, 0)
                for k in (6, 7) + (() if last else (8, 9)):
                    copy(g, k, last)
                evacuate(g, 1)

            copy(0, 0)
            copy(0, 1)
            chunk_pairs(act, body)
            act.wait_ge(x_in, 16 * TILES)


def wait_at(eng, sem, value, carrier):
    eng.wait_ge(sem, value)
    if not isinstance(value, int):
        eng.nop(nofuse=True)


class Steps:

    def __init__(self, eng, sem, base, carrier):
        self.eng, self.sem, self.base, self.carrier, self.n = eng, sem, base, carrier, 0

    def __call__(self, ins):
        ins.then_inc(self.sem, 1)
        self.n += 1
        wait_at(self.eng, self.sem, self.base + self.n, self.carrier)


def tile_of(X, i):
    return X[:, bass.ds(i, 1), :].rearrange("p a d -> p (a d)")


def layer0(nc, weights, X, ident, WT, scale4, shift4, dinv):
    (bias0, enc_W, enc_b, s2c_W, s2c_b, rW1, rb1, rW2, rb2, We1, be1, We2, be2, c2s_W, c2s_b,
     dec_W, dec_b, ln_g, ln_b) = weights
    with ExitStack() as ctx:
        encW = sb(nc, ctx, "encW", [128, KD, H1])
        decW = sb(nc, ctx, "decW", [128, 2, D])
        s2cW = sb(nc, ctx, "s2cW", [128, 2, M1])
        rW1s = sb(nc, ctx, "rW1s", [M1, M1])
        rW2s = sb(nc, ctx, "rW2s", [M1, EX])
        We1s = sb(nc, ctx, "We1s", [M1, EX, 128])
        We2s = sb(nc, ctx, "We2s", [128, EX, M1])
        c2sW = sb(nc, ctx, "c2sW", [M1, H1])
        encb = sb(nc, ctx, "encb", [128, 2])
        s2cb = sb(nc, ctx, "s2cb", [M1, 1])
        rb1s = sb(nc, ctx, "rb1s", [M1, 1])
        be1s = sb(nc, ctx, "be1s", [128, EX])
        c2sb = sb(nc, ctx, "c2sb", [128, 2])
        rb2r = sb(nc, ctx, "rb2r", [P, EX])
        be2r = sb(nc, ctx, "be2r", [P, EX * M1])
        bias0r = sb(nc, ctx, "bias0r", [P, D])
        decbr = sb(nc, ctx, "decbr", [P, D])
        lngr = sb(nc, ctx, "lngr", [P, D])
        lnbr = sb(nc, ctx, "lnbr", [P, D])
        xn1 = sb(nc, ctx, "xn1", [P, 2, D])
        xn2 = sb(nc, ctx, "xn2", [P, 2, D])
        xT1 = sb(nc, ctx, "xT1", [128, KD, PAIR])
        xT2 = sb(nc, ctx, "xT2", [128, KD, PAIR])
        flatT = sb(nc, ctx, "flatT", [128, 2, PAIR])
        contT = sb(nc, ctx, "contT", [M1, PAIR])
        routT = sb(nc, ctx, "routT", [M1, PAIR])
        hT = sb(nc, ctx, "hT", [128, EX, PAIR])
        logits = sb(nc, ctx, "logits", [P, 2, EX])
        top8 = sb(nc, ctx, "top8", [P, 2, EX])
        top_i = sb(nc, ctx, "top_i", [P, 2, EX], U32)
        top_f = sb(nc, ctx, "top_f", [P, 2, EX])
        lead = sb(nc, ctx, "lead", [P, 2, 2])
        share = sb(nc, ctx, "share", [P, 2, 2])
        iota8i = sb(nc, ctx, "iota8i", [P, EX], I32)
        iota8 = sb(nc, ctx, "iota8", [P, EX])
        first = sb(nc, ctx, "first_gate", [P, 2, EX])
        gates = sb(nc, ctx, "gates", [P, 2, EX])
        mixed = sb(nc, ctx, "mixed", [P, 2, EX * M1])
        moe = sb(nc, ctx, "moe", [P, 2, M1])
        moeT = sb(nc, ctx, "moeT", [M1, PAIR])
        spikT = sb(nc, ctx, "spikT", [128, 2, PAIR])
        dec = sb(nc, ctx, "dec", [P, 2, D])
        stats = sb(nc, ctx, "stats", [P, 4, 2, 2, 6])
        mv = sb(nc, ctx, "mv", [P, 4, 2, 2])
        veps = sb(nc, ctx, "veps", [P, 4, 2])
        rstd = sb(nc, ctx, "rstd", [P, 4, 2])
        mhalf = sb(nc, ctx, "mhalf2", [P, 2])
        nmean = sb(nc, ctx, "nmean", [P, 2])
        TR = [psum(nc, ctx, f"TR{i}", [128, 512]) for i in range(2)]
        Y = [psum(nc, ctx, f"Y{i}", [128, 512]) for i in range(2)]
        DP = [psum(nc, ctx, f"DP{i}", [128, 512]) for i in range(2)]
        F = [psum(nc, ctx, f"F{i}", [128, 512]) for i in range(2)]
        (w_in, consts, tr_ready, tr_free, y_ready, y_free, f_ready, lead_ready, share_ready, moe_ready,
         dec_ready, dec_free, dec_done, x_biased, x_shifted, normed, gained, x2_ready, scaled, pool_steps,
         steps_first, steps_loop, steps_last) = sems(
            nc, ctx, "w_in", "consts", "tr_ready", "tr_free", "y_ready", "y_free", "f_ready", "lead_ready",
            "share_ready", "moe_ready", "dec_ready", "dec_free", "dec_done", "x_biased", "x_shifted", "normed",
            "gained", "x2_ready", "scaled", "pool_steps", "steps_first", "steps_loop", "steps_last")
        f_done = sems(nc, ctx, "f_done0", "f_done1")
        xn_ready = sems(nc, ctx, "xn1_ready", "xn2_ready")
        var_ready = sems(nc, ctx, *(f"var_ready{k}" for k in range(1, 5)))
        rstd_ready = sems(nc, ctx, *(f"rstd_ready{k}" for k in range(1, 5)))
        LAST = PAIRS - 1
        LOADS = 19

        def pairs(eng, prologue, body):
            prologue()
            with eng.Fori(0, LAST) as p:
                body(p, p + 1)
            body(LAST, None)

        def fill(p, k):
            return 8 * p + 4 * (k - 1)

        block = ctx.enter_context(nc.Block())

        @block.sync
        def _(sp):
            loads = []

            def load(tile, ap, slow=False):
                loads.append(1)
                sp.dma_start(tile, ap, allow_slow_non_contiguous=slow).then_inc(w_in, 16)

            def row(v, n):
                return v.rearrange("(a n) -> a n", a=1).broadcast_to([P, n])

            load(bias0r[:, :], row(bias0, D))
            load(encW[:, :, :], enc_W.rearrange("(k p) m -> p k m", p=128))
            load(encb[:, :], enc_b.rearrange("(c p) -> p c", p=128), True)
            load(s2cW[:, :, :], s2c_W.rearrange("(k p) m -> p k m", p=128))
            load(s2cb[:, :], s2c_b.rearrange("(p a) -> p a", a=1), True)
            load(rW1s[:, :], rW1)
            load(rb1s[:, :], rb1.rearrange("(p a) -> p a", a=1), True)
            load(rW2s[:, :], rW2)
            load(rb2r[:, :], row(rb2, EX))
            load(We1s[:, :, :], We1.rearrange("e m h -> m e h"))
            load(be1s[:, :], be1.rearrange("e h -> h e"), True)
            load(We2s[:, :, :], We2.rearrange("e h m -> h e m"))
            load(be2r[:, :], row(be2.rearrange("e m -> (e m)"), EX * M1))
            load(c2sW[:, :], c2s_W)
            load(c2sb[:, :], c2s_b.rearrange("(c p) -> p c", p=128), True)
            load(decW[:, :, :], dec_W.rearrange("(k p) d -> p k d", p=128))
            load(decbr[:, :], row(dec_b, D))
            load(lngr[:, :], row(ln_g, D))
            load(lnbr[:, :], row(ln_b, D))
            assert len(loads) == LOADS
            sp.wait_ge(w_in, 16 * LOADS)

        @block.tensor
        def _(pe):
            hold = pe.alloc_register("pe_hold0")
            pe.reg_mov(hold, 0)
            for free, n in ((tr_free, 2), (y_free, 2), (dec_free, 2), (f_done[0], 1), (f_done[1], 1), (f_ready, 12)):
                pe.sem_inc(free, n)

            def turn(p, k):
                xn = (xn1, xn2)[k - 1]
                wait_at(pe, xn_ready[k - 1], p + 1, hold)
                for j in range(4):
                    wait_at(pe, tr_free, fill(p, k) + j + 1, hold)
                    for c in range(2):
                        for s in range(2):
                            at, f = PAIR * c + P * s, 128 * (2 * j + c)
                            ins = pe.transpose(TR[j % 2][:, at:at + P], xn[:, s, f:f + 128], ident[0:P, 0:P])
                    ins.then_inc(tr_ready, 1)

            def gnn(p, part):
                s, half = part // 2, part % 2
                if part == 0:
                    wait_at(pe, tr_free, fill(p, 1) + 4 + 2, hold)
                wait_at(pe, y_free, 4 * p + part + 1, hold)
                for k in range(KD):
                    ins = pe.matmul(Y[half][0:P, :], xT1[:, k, P * s:P * s + P], WT[:, k, 512 * half:512 * half + 512],
                                    start=(k == 0), stop=(k == KD - 1))
                ins.then_inc(y_ready, 1)

            def use(p, u):
                wait_at(pe, f_done[u % 2], 6 * p + u // 2 + 1, hold)
                return F[u % 2]

            def left_bank(p, u):
                wait_at(pe, f_done[u % 2], 6 * p + u // 2 + 2, hold)

            def prologue():
                turn(0, 1)
                for part in range(4):
                    gnn(0, part)

            def body(p, n):
                turn(p, 2)
                pe.wait_ge(w_in, 16 * LOADS)
                wait_at(pe, tr_free, fill(p, 2) + 4 + 2, hold)
                f = use(p, 0)
                for m in range(2):
                    for k in range(KD):
                        ins = pe.matmul(f[:, PAIR * m:PAIR * m + PAIR], encW[:, k, 128 * m:128 * m + 128], xT2[:, k, :],
                                        start=(k == 0), stop=(k == KD - 1))
                ins.then_inc(f_ready, 1)
                if n is not None:
                    turn(n, 1)
                left_bank(p, 0)
                f = use(p, 1)
                for k in range(2):
                    ins = pe.matmul(f[0:M1, 0:PAIR], s2cW[:, k, :], flatT[:, k, :], start=(k == 0), stop=(k == 1))
                ins.then_inc(f_ready, 1)
                if n is not None:
                    gnn(n, 0)
                left_bank(p, 1)
                f = use(p, 2)
                pe.matmul(f[0:M1, 0:PAIR], rW1s[:, :], contT[:, :], start=True, stop=True).then_inc(f_ready, 1)
                for u in range(4):
                    f = use(p, 3 + u)
                    for e in range(2):
                        ins = pe.matmul(f[:, PAIR * e:PAIR * e + PAIR], We1s[:, 2 * u + e, :], contT[:, :],
                                        start=True, stop=True)
                    ins.then_inc(f_ready, 1)
                if n is not None:
                    gnn(n, 1)
                left_bank(p, 2)
                f = use(p, 7)
                for s in range(2):
                    ins = pe.matmul(f[0:P, EX * s:EX * s + EX], routT[:, P * s:P * s + P], rW2s[:, :],
                                    start=True, stop=True)
                ins.then_inc(f_ready, 1)
                left_bank(p, 5)
                left_bank(p, 6)
                for s in range(2):
                    f = use(p, 8 + s)
                    for e in range(EX):
                        ins = pe.matmul(f[0:P, M1 * e:M1 * e + M1], hT[:, e, P * s:P * s + P], We2s[:, e, :],
                                        start=True, stop=True)
                    ins.then_inc(f_ready, 1)
                if n is not None:
                    gnn(n, 2)
                wait_at(pe, moe_ready, 2 * p + 2, hold)
                f = use(p, 10)
                for s in range(2):
                    ins = pe.transpose(f[0:M1, P * s:P * s + P], moe[:, s, :], ident[0:P, 0:P])
                ins.then_inc(f_ready, 1)
                if n is not None:
                    gnn(n, 3)
                left_bank(p, 10)
                f = use(p, 11)
                for m in range(2):
                    ins = pe.matmul(f[:, PAIR * m:PAIR * m + PAIR], c2sW[:, 128 * m:128 * m + 128], moeT[:, :],
                                    start=True, stop=True)
                ins.then_inc(f_ready, 1)
                left_bank(p, 11)
                for part in range(4):
                    s, half = part // 2, part % 2
                    wait_at(pe, dec_free, 4 * p + part + 1, hold)
                    for k in range(2):
                        ins = pe.matmul(DP[half][0:P, :], spikT[:, k, P * s:P * s + P],
                                        decW[:, k, 512 * half:512 * half + 512], start=(k == 0), stop=(k == 1))
                    ins.then_inc(dec_ready, 1)

            pairs(pe, prologue, body)

        @block.scalar
        def _(act):
            hold = act.alloc_register("act_hold0")
            act.reg_mov(hold, 0)

            def evacuate(p, k):
                if k == 2:
                    wait_at(act, f_ready, 12 * p + 1, hold)
                elif not isinstance(p, int):
                    wait_at(act, y_ready, 4 * p, hold)
                for j in range(4):
                    wait_at(act, tr_ready, fill(p, k) + j + 1, hold)
                    act.activation((xT1, xT2)[k - 1][:, 2 * j:2 * j + 2, :].rearrange("p a n -> p (a n)"),
                                   TR[j % 2][:, 0:2 * PAIR], ACT.Copy).then_inc(tr_free, 1)

            def computed(p, u):
                wait_at(act, f_ready, 12 * p + u + 13, hold)
                return F[u % 2]

            def prologue():
                evacuate(0, 1)

            def body(p, n):
                evacuate(p, 2)
                act.wait_ge(w_in, 16 * LOADS)
                f = computed(p, 0)
                for m in range(2):
                    ins = act.activation(flatT[:, m, :], f[:, PAIR * m:PAIR * m + PAIR], ACT.Sigmoid,
                                         bias=encb[:, m:m + 1])
                ins.then_inc(f_done[0], 1)
                if n is not None:
                    evacuate(n, 1)
                f = computed(p, 1)
                act.activation(contT[:, :], f[0:M1, 0:PAIR], ACT.Identity, bias=s2cb[:, :]).then_inc(f_done[1], 1)
                f = computed(p, 2)
                act.activation(routT[:, :], f[0:M1, 0:PAIR], ACT.Tanh, bias=rb1s[:, :]).then_inc(f_done[0], 1)
                for u in range(4):
                    f = computed(p, 3 + u)
                    for e in range(2):
                        ins = act.activation(hT[:, 2 * u + e, :], f[:, PAIR * e:PAIR * e + PAIR], ACT.Relu,
                                             bias=be1s[:, 2 * u + e:2 * u + e + 1])
                    ins.then_inc(f_done[(3 + u) % 2], 1)
                wait_at(act, lead_ready, p + 1, hold)
                act.activation(share[:, :, :], lead[:, :, :], ACT.Sigmoid).then_inc(share_ready, 1)
                f = computed(p, 11)
                for m in range(2):
                    ins = act.activation(spikT[:, m, :], f[:, PAIR * m:PAIR * m + PAIR], ACT.Sigmoid,
                                         bias=c2sb[:, m:m + 1])
                ins.then_inc(f_done[1], 1)
                for part in range(4):
                    wait_at(act, dec_free, 4 * p + part + 3, hold)
                    at = dec[:, part // 2, 512 * (part % 2):512 * (part % 2) + 512]
                    act.activation(at, at, ACT.Sigmoid).then_inc(dec_done, 1)

            pairs(act, prologue, body)

        @block.gpsimd
        def _(pool):
            hold = pool.alloc_register("pool_hold0")
            pool.reg_mov(hold, 0)
            pool.memset(mhalf[:, :], -0.5).then_inc(consts, 1)
            pool.iota(iota8i[:, :], [[1, EX]], base=0, channel_multiplier=0).then_inc(consts, 1)
            pool.wait_ge(consts, 2)
            pool.wait_ge(w_in, 16 * LOADS)

            def inverse_root(p, k):
                wait_at(pool, var_ready[k - 1], p + 1, hold)
                return pool.tensor_tensor(rstd[:, k - 1], veps[:, k - 1], mhalf[:, :], ALU.pow)

            def first_norms(p):
                for k, vector, added in ((1, bias0r, x_biased), (2, lnbr, x_shifted)):
                    inverse_root(p, k).then_inc(rstd_ready[k - 1], 1)
                    wait_at(pool, xn_ready[k - 1], p + 1, hold)
                    for s in range(2):
                        t = tile_of(X, 2 * p + s)
                        ins = pool.tensor_tensor(t, t, vector[:, :], ALU.add)
                    ins.then_inc(added, 1)

            def body(p, n):
                if n is not None:
                    first_norms(n)
                inverse_root(p, 3).then_inc(rstd_ready[2], 1)
                wait_at(pool, normed, p + 1, hold)
                for s in range(2):
                    ins = pool.tensor_tensor(dec[:, s, :], dec[:, s, :], lngr[:, :], ALU.mult)
                ins.then_inc(gained, 1)
                inverse_root(p, 4).then_inc(pool_steps, 1)
                pool.tensor_scalar(nmean[:, :], mv[:, 3, :, 0], -1.0, None, ALU.mult).then_inc(pool_steps, 1)
                wait_at(pool, pool_steps, 3 * p + 2, hold)
                pool.tensor_tensor(scale4[:, bass.ds(2 * p, 2)], rstd[:, 3], dinv[:, bass.ds(2 * p, 2)], ALU.mult
                                   ).then_inc(pool_steps, 1)
                wait_at(pool, pool_steps, 3 * p + 3, hold)
                pool.tensor_tensor(shift4[:, bass.ds(2 * p, 2)], nmean[:, :], scale4[:, bass.ds(2 * p, 2)], ALU.mult
                                   ).then_inc(scaled, 1)

            pairs(pool, lambda: first_norms(0), body)

        @block.vector
        def _(dve):
            hold = dve.alloc_register("dve_hold0")
            dve.reg_mov(hold, 0)
            dve.wait_ge(consts, 2)
            dve.tensor_copy(iota8[:, :], iota8i[:, :]).then_inc(consts, 1)
            dve.wait_ge(consts, 3)
            dve.wait_ge(w_in, 16 * LOADS)
            dve.wait_ge(consts, 3)

            def norm(step, p, k, rows):
                k -= 1
                for s in range(2):
                    for half in range(2):
                        ins = dve.bn_stats(stats[:, k, s, half], rows(s)[:, 512 * half:512 * half + 512])
                step(ins)
                for s in range(2):
                    ins = dve.bn_aggr(mv[:, k, s], stats[:, k, s].rearrange("p a b -> p (a b)"))
                step(ins)
                dve.tensor_scalar(veps[:, k], mv[:, k, :, 1], EPS, None, ALU.add).then_inc(var_ready[k], 1)

            def apply(p, k, s, out, rows):
                return dve.tensor_scalar(out, rows, mv[:, k - 1, s, 0:1], rstd[:, k - 1, s:s + 1],
                                         ALU.subtract, ALU.mult)

            def normalise(step, p, k):
                xn = (xn1, xn2)[k - 1]
                norm(step, p, k, lambda s: tile_of(X, 2 * p + s))
                if not isinstance(p, int):
                    wait_at(dve, tr_ready, fill(p, k) - 4, hold)
                wait_at(dve, rstd_ready[k - 1], p + 1, hold)
                for s in range(2):
                    ins = apply(p, k, s, xn[:, s, :], tile_of(X, 2 * p + s))
                ins.then_inc(xn_ready[k - 1], 1)

            def add_gnn(p, part):
                s, half = part // 2, part % 2
                wait_at(dve, y_ready, 4 * p + part + 1, hold)
                if part == 0:
                    wait_at(dve, x_biased, p + 1, hold)
                t = tile_of(X, 2 * p + s)[:, 512 * half:512 * half + 512]
                return dve.tensor_tensor(t, Y[half][0:P, :], t, ALU.add).then_inc(y_free, 1)

            def added(p):
                wait_at(dve, y_free, 4 * p + 4 + 2, hold)

            def computed(p, u):
                wait_at(dve, f_ready, 12 * p + u + 13, hold)
                return F[u % 2]

            def prologue():
                step = Steps(dve, steps_first, 0, hold)
                normalise(step, 0, 1)
                for part in range(4):
                    add_gnn(0, part)
                added(0)
                normalise(step, 0, 2)

            def body(p, n):
                step = Steps(dve, steps_loop, STEPS * p, hold) if n is not None else Steps(dve, steps_last, 0, hold)
                if n is not None:
                    normalise(step, n, 1)
                    add_gnn(n, 0)
                    add_gnn(n, 1)
                f = computed(p, 7)
                dve.tensor_tensor(logits[:, :, :], f[0:P, 0:2 * EX].rearrange("p (s e) -> p s e", s=2),
                                  rb2r[:, :].unsqueeze(1).broadcast_to([P, 2, EX]), ALU.add).then_inc(f_done[1], 1)
                wait_at(dve, f_done[1], 6 * p + 3 + 2, hold)
                for s in range(2):
                    ins = dve.max(top8[:, s], logits[:, s])
                step(ins)
                for s in range(2):
                    last_index = dve.max_index(top_i[:, s], top8[:, s], logits[:, s])
                step(last_index)
                dve.tensor_tensor(lead[:, :, 0], top8[:, :, 0], top8[:, :, 1], ALU.subtract)
                dve.tensor_tensor(lead[:, :, 1], top8[:, :, 1], top8[:, :, 0], ALU.subtract).then_inc(lead_ready, 1)
                step(dve.tensor_copy(top_f[:, :, :], top_i[:, :, :]))
                wait_at(dve, share_ready, p + 1, hold)
                for s in range(2):
                    for out, k in ((first, 0), (gates, 1)):
                        ins = dve.tensor_scalar(out[:, s], iota8[:, :], top_f[:, s, k:k + 1], share[:, s, k:k + 1],
                                                ALU.is_equal, ALU.mult)
                step(ins)
                step(dve.tensor_tensor(gates[:, :, :], gates[:, :, :], first[:, :, :], ALU.add))
                for s in range(2):
                    f = computed(p, 8 + s)
                    ins = dve.tensor_tensor(mixed[:, s], f[0:P, :], be2r[:, :], ALU.add).then_inc(f_done[s], 1)
                wait_at(dve, f_done[0], 6 * p + 4 + 2, hold)
                wait_at(dve, f_done[1], 6 * p + 4 + 2, hold)
                for s in range(2):
                    m = mixed[:, s].rearrange("p (e m) -> p e m", e=EX)
                    ins = dve.tensor_tensor(m, m, gates[:, s].unsqueeze(2).broadcast_to([P, EX, M1]), ALU.mult)
                step(ins)
                for s in range(2):
                    dve.tensor_reduce(moe[:, s], mixed[:, s].rearrange("p (e m) -> p m e", e=EX), AX.X, ALU.add
                                      ).then_inc(moe_ready, 1)
                if n is not None:
                    add_gnn(n, 2)
                f = computed(p, 10)
                dve.tensor_copy(moeT[:, :], f[0:M1, 0:PAIR]).then_inc(f_done[0], 1)
                if n is not None:
                    add_gnn(n, 3)
                    added(n)
                    normalise(step, n, 2)
                for part in range(4):
                    s, half = part // 2, part % 2
                    wait_at(dve, dec_ready, 4 * p + part + 1, hold)
                    dve.tensor_tensor(dec[:, s, 512 * half:512 * half + 512], DP[half][0:P, :],
                                      decbr[:, 512 * half:512 * half + 512], ALU.add).then_inc(dec_free, 1)
                wait_at(dve, dec_done, 4 * p + 4, hold)
                norm(step, p, 3, lambda s: dec[:, s, :])
                wait_at(dve, rstd_ready[2], p + 1, hold)
                for s in range(2):
                    ins = apply(p, 3, s, dec[:, s, :], dec[:, s, :])
                ins.then_inc(normed, 1)
                wait_at(dve, gained, p + 1, hold)
                wait_at(dve, x_shifted, p + 1, hold)
                for s in range(2):
                    t = tile_of(X, 2 * p + s)
                    ins = dve.tensor_tensor(t, t, dec[:, s, :], ALU.add)
                step(ins)
                norm(step, p, 4, lambda s: tile_of(X, 2 * p + s))
                assert n is None or step.n == STEPS, step.n

            pairs(dve, prologue, body)
            dve.wait_ge(scaled, PAIRS)


QUANT_STEPS = 4


def dequantise(dve, step, w, blocks, largest, scale, inverse):
    of_block = [128, blocks, 32]
    step(dve.tensor_reduce(largest, w, AX.X, ALU.max, apply_absolute_value=True))
    step(dve.tensor_scalar(scale, largest, 1.0 / 7.0, 1e-12, ALU.mult, ALU.max))
    step(dve.reciprocal(inverse, scale))
    step(dve.tensor_tensor(w, w, inverse.unsqueeze(2).broadcast_to(of_block), ALU.mult))
    step(dve.tensor_scalar(w, w, MAGIC, None, ALU.add))
    step(dve.tensor_scalar(w, w, -MAGIC, 7.0, ALU.add, ALU.min))
    step(dve.tensor_tensor(w, w, scale.unsqueeze(2).broadcast_to(of_block), ALU.mult))


def aggregate(nc, X, CT, W1, AG, scale4, shift4, w_layer1, w_gate, w_up):
    with ExitStack() as ctx:
        CTf = sb(nc, ctx, "CTf", [P, TILES, N])
        staged = sb(nc, ctx, "staged", [P, 2, TILES, 128])
        wbig = sb(nc, ctx, "wbig", [128, 3, 32])
        A = [psum(nc, ctx, f"A{i}", [128, 3 * 512]) for i in range(2)]
        (w1_in, quant_in, counts_ready, staged_ready, agg_ready, agg_done, shifts, quant_steps) = sems(
            nc, ctx, "w1_in", "quant_in", "counts_ready", "staged_ready", "agg_ready", "agg_done", "shifts",
            "quant_steps")
        GU = CT[:, :, :].rearrange("p t d -> p (t d)").bitcast(F32)[:, 0:2 * QC * D].rearrange(
            "p (m d) -> p m d", d=D)
        block = ctx.enter_context(nc.Block())

        @block.sync
        def _(sp):
            sp.dma_start(W1[:, :, :], w_layer1.rearrange("(k p) d -> p k d", p=128)).then_inc(w1_in, 16)
            sp.wait_ge(counts_ready, 3)
            sp.dma_start(GU[:, 0:QC], w_gate.rearrange("(m p) d -> p m d", p=128)).then_inc(quant_in, 16)
            sp.dma_start(GU[:, QC:2 * QC], w_up.rearrange("(m p) d -> p m d", p=128)).then_inc(quant_in, 16)
            sp.wait_ge(w1_in, 16)
            sp.wait_ge(quant_in, 32)

        @block.gpsimd
        def _(pool):
            for i in range(0, 2):
                ins = pool.tensor_copy(CTf[:, i, :], CT[0:P, i, 0:N])
            ins.then_inc(counts_ready, 1)

        @block.scalar
        def _(act):
            hold = None
            for i in range(2, 6):
                ins = act.activation(CTf[:, i, :], CT[0:P, i, 0:N], ACT.Copy)
            ins.then_inc(counts_ready, 1)
            with act.Fori(0, KD // 2) as g:
                for par in range(2):
                    f = 2 * g + par
                    wait_at(act, agg_ready, f + 3, hold)
                    act.activation(AG[:, bass.ds(f, 1), :].rearrange("p a n -> p (a n)"), A[par][:, 0:N], ACT.Copy
                                   ).then_inc(agg_done, 1)

        @block.vector
        def _(dve):
            hold = None

            def stage(f, par):
                x = X[:, :, bass.ds(128 * f, 128)]
                wait_at(dve, agg_ready, f + 1, hold)
                dve.tensor_tensor(staged[:, par], x, scale4[:, :].unsqueeze(2).broadcast_to([P, TILES, 128]),
                                  ALU.mult).then_inc(shifts, 1)
                wait_at(dve, shifts, f + 1, hold)
                dve.tensor_tensor(staged[:, par], staged[:, par],
                                  shift4[:, :].unsqueeze(2).broadcast_to([P, TILES, 128]), ALU.add
                                  ).then_inc(staged_ready, 1)

            for i in range(6, TILES):
                ins = dve.tensor_copy(CTf[:, i, :], CT[0:P, i, 0:N])
            ins.then_inc(counts_ready, 1)
            with dve.Fori(0, KD // 2) as g:
                for par in range(2):
                    stage(2 * g + par, par)
            dve.wait_ge(quant_in, 32)
            step = Steps(dve, quant_steps, 0, hold)
            for m in range(2 * QC):
                dequantise(dve, step, GU[:, m].rearrange("p (b k) -> p b k", k=32), 32, wbig[:, 0], wbig[:, 1],
                           wbig[:, 2])

        @block.tensor
        def _(pe):
            hold = None
            pe.sem_inc(agg_ready, 2)
            pe.sem_inc(agg_done, 2)
            pe.wait_ge(counts_ready, 3)
            with pe.Fori(0, KD // 2) as g:
                for par in range(2):
                    f = 2 * g + par
                    wait_at(pe, staged_ready, f + 1, hold)
                    wait_at(pe, agg_done, f + 1, hold)
                    for i in range(TILES):
                        for at in range(0, N, 512):
                            size = min(512, N - at)
                            ins = pe.matmul(A[par][:, at:at + size], staged[:, par, i, :], CTf[:, i, at:at + size],
                                            start=(i == 0), stop=(i == TILES - 1))
                    ins.then_inc(agg_ready, 1)


def layer1_gnn(nc, X, CT, W1, AG, ident, guT, wdT, dinv, scale5, shift5, largest, bias1, w_down):
    with ExitStack() as ctx:
        wd = sb(nc, ctx, "wd", [128, KD, QI])
        biasr = sb(nc, ctx, "biasr", [P, D])
        agT = sb(nc, ctx, "agT", [128, 2, KD, P])
        z = sb(nc, ctx, "z", [P, 2, D])
        wbig = sb(nc, ctx, "wbig2", [128, 3, 12])
        stats = sb(nc, ctx, "stats5", [P, 2, 2, 6])
        mv = sb(nc, ctx, "mv5", [P, 2, 2])
        veps = sb(nc, ctx, "veps5", [P, 2])
        rstd = sb(nc, ctx, "rstd5", [P, 2])
        nmean = sb(nc, ctx, "nmean5", [P, 2])
        mhalf = sb(nc, ctx, "mhalf5", [P, 2])
        Z = [psum(nc, ctx, f"Z{i}", [128, 512]) for i in range(4)]
        TW = [psum(nc, ctx, f"TW{i}", [128, 512]) for i in range(2)]
        (wd_in, bias_in, wd_ready, tw_ready, tw_done, copied, z_ready, z_free, zeroed, var_ready, rstd_ready,
         x3_steps, quant_steps, pool_steps) = sems(
            nc, ctx, "wd_in", "bias_in", "wd_ready", "tw_ready", "tw_done", "copied", "z_ready", "z_free",
            "zeroed", "var_ready5", "rstd_ready5", "x3_steps", "quant_steps2", "pool_steps5")
        GU = CT[:, :, :].rearrange("p t d -> p (t d)").bitcast(F32)[:, 0:2 * QC * D].rearrange(
            "p (m d) -> p m d", d=D)
        FILLS = 4 * QC + KD
        block = ctx.enter_context(nc.Block())

        @block.sync
        def _(sp):
            sp.dma_start(wd[:, :, :], w_down.rearrange("(c p) k -> p c k", p=128)).then_inc(wd_in, 16)
            sp.dma_start(biasr[:, :], bias1.rearrange("(a n) -> a n", a=1).broadcast_to([P, D])).then_inc(bias_in, 16)
            sp.wait_ge(wd_in, 16)
            sp.wait_ge(bias_in, 16)

        @block.gpsimd
        def _(pool):
            pool.memset(mhalf[:, :], -0.5).then_inc(zeroed, 1)
            pool.memset(largest[:, :], 0.0).then_inc(zeroed, 1)
            pool.wait_ge(zeroed, 2)

            def copy(i, s):
                pool.tensor_copy(agT[:, s], AG[:, :, bass.ds(P * i, P)]).then_inc(copied, 1)

            copy(0, 0)
            copy(1, 1)
            with pool.Fori(0, PAIRS) as g:
                wait_at(pool, var_ready, g + 1, None)
                pool.tensor_tensor(rstd[:, :], veps[:, :], mhalf[:, :], ALU.pow).then_inc(rstd_ready, 1)
                pool.tensor_scalar(nmean[:, :], mv[:, :, 0], -1.0, None, ALU.mult).then_inc(pool_steps, 1)
                wait_at(pool, pool_steps, 2 * g + 1, None)
                pool.tensor_copy(scale5[:, bass.ds(2 * g, 2)], rstd[:, :])
                pool.tensor_tensor(shift5[:, bass.ds(2 * g, 2)], nmean[:, :], rstd[:, :], ALU.mult
                                   ).then_inc(pool_steps, 1)
                wait_at(pool, pool_steps, 2 * g + 2, None)
                for s in range(2):
                    wait_at(pool, z_ready, 4 * g + 2 * s + 2, None)
                    copy((2 * g + 2) % TILES + s, s)

        @block.tensor
        def _(pe):
            pe.sem_inc(tw_done, 2)
            pe.sem_inc(z_free, 4)
            fill = 0
            for m in range(2 * QC):
                for j in range(2):
                    pe.wait_ge(tw_done, fill + 1)
                    for k in range(4):
                        ins = pe.transpose(TW[fill % 2][:, 128 * k:128 * k + 128],
                                           GU[:, m, 128 * (4 * j + k):128 * (4 * j + k) + 128], ident[:, :])
                    ins.then_inc(tw_ready, 1)
                    fill += 1
            pe.wait_ge(wd_ready, KD)
            for c in range(KD):
                pe.wait_ge(tw_done, fill + 1)
                for k in range(QC):
                    ins = pe.transpose(TW[fill % 2][:, 128 * k:128 * k + 128], wd[:, c, 128 * k:128 * k + 128],
                                       ident[:, :])
                ins.then_inc(tw_ready, 1)
                fill += 1
            assert fill == FILLS
            with pe.Fori(0, PAIRS) as g:
                for s in range(2):
                    wait_at(pe, copied, 2 * g + s + 1, None)
                    for half in range(2):
                        part = 2 * s + half
                        wait_at(pe, z_free, 4 * g + part + 1, None)
                        for k in range(KD):
                            ins = pe.matmul(Z[part][0:P, :], agT[:, s, k, :], W1[:, k, 512 * half:512 * half + 512],
                                            start=(k == 0), stop=(k == KD - 1))
                        ins.then_inc(z_ready, 1)

        @block.scalar
        def _(act):
            fill = 0
            for m in range(2 * QC):
                for j in range(2):
                    act.wait_ge(tw_ready, fill + 1)
                    act.activation(guT[:, 4 * j:4 * j + 4, 128 * m:128 * m + 128],
                                   TW[fill % 2][:, :].rearrange("p (k n) -> p k n", k=4), ACT.Copy
                                   ).then_inc(tw_done, 1)
                    fill += 1
            for c in range(KD):
                act.wait_ge(tw_ready, fill + 1)
                act.activation(wdT[:, :, 128 * c:128 * c + 128],
                               TW[fill % 2][:, 0:128 * QC].rearrange("p (k n) -> p k n", k=QC), ACT.Copy
                               ).then_inc(tw_done, 1)
                fill += 1
            act.wait_ge(tw_done, FILLS + 2)

        @block.vector
        def _(dve):
            dve.wait_ge(wd_in, 16)
            step = Steps(dve, quant_steps, 0, None)
            for c in range(KD):
                dequantise(dve, step, wd[:, c].rearrange("p (b k) -> p b k", k=32), 12, wbig[:, 0], wbig[:, 1],
                           wbig[:, 2])
                dve.sem_inc(wd_ready, 1)
            dve.wait_ge(bias_in, 16)
            dve.wait_ge(zeroed, 2)
            with dve.Fori(0, PAIRS) as g:
                step = Steps(dve, x3_steps, X3_STEPS * g, None)
                for s in range(2):
                    for half in range(2):
                        part = 2 * s + half
                        wait_at(dve, z_ready, 4 * g + part + 1, None)
                        at = slice(512 * half, 512 * half + 512)
                        dve.scalar_tensor_tensor(z[:, s, at], Z[part][0:P, :], dinv[:, bass.ds(2 * g + s, 1)],
                                                 biasr[:, at], ALU.mult, ALU.add).then_inc(z_free, 1)
                wait_at(dve, z_free, 4 * g + 8, None)
                for s in range(2):
                    t = tile_of(X, 2 * g + s)
                    ins = dve.scalar_tensor_tensor(t, z[:, s], 0.0, t, ALU.max, ALU.add)
                step(ins)
                for s in range(2):
                    for half in range(2):
                        ins = dve.bn_stats(stats[:, s, half], tile_of(X, 2 * g + s)[:, 512 * half:512 * half + 512])
                step(ins)
                for s in range(2):
                    ins = dve.bn_aggr(mv[:, s], stats[:, s].rearrange("p a b -> p (a b)"))
                step(ins)
                dve.tensor_scalar(veps[:, :], mv[:, :, 1], EPS, None, ALU.add).then_inc(var_ready, 1)
                wait_at(dve, rstd_ready, g + 1, None)
                for s in range(2):
                    ins = dve.tensor_scalar(z[:, s], tile_of(X, 2 * g + s), mv[:, s, 0:1], rstd[:, s:s + 1],
                                            ALU.subtract, ALU.mult)
                step(ins)
                ins = dve.tensor_reduce(largest[0:P, bass.ds(2 * g, 2)], z[:, :, :], AX.X, ALU.max,
                                        apply_absolute_value=True)
                step(ins)
                wait_at(dve, pool_steps, 2 * g + 2, None)
                assert step.n == X3_STEPS


def quantised_ffn(nc, X, AG, guT, wdT, ident, scale5, shift5, largest, out):
    with ExitStack() as ctx:
        q = sb(nc, ctx, "q", [P, 2, D])
        qT = sb(nc, ctx, "qT", [128, KD, PAIR])
        oq = sb(nc, ctx, "oq", [128, 2, QC, PAIR])
        big = sb(nc, ctx, "big", [128, 16])
        red = sb(nc, ctx, "red", [128, 16])
        sc = sb(nc, ctx, "sc", [128, 16])
        coef = sb(nc, ctx, "coef5", [P, 2, TILES])
        big2 = sb(nc, ctx, "big2", [128, 2, PAIRS])
        big3 = sb(nc, ctx, "big3", [128, 2, QC])
        TQ = [psum(nc, ctx, f"TQ{i}", [128, 512]) for i in range(2)]
        H = [psum(nc, ctx, f"H{i}", [128, 512]) for i in range(3)]
        O = [psum(nc, ctx, f"O{i}", [128, 512]) for i in range(2)]
        (steps, reduced, q_ready, tq_ready, tq_done, h_ready, h_done, sig_in, sig_out, down_ready, oq_ready,
         o_ready, o_done, stored, loop_steps, coef_ready, found) = sems(
            nc, ctx, "steps6", "reduced", "q_ready", "tq_ready", "tq_done", "h_ready6", "h_done", "sig_in",
            "sig_out", "down_ready", "oq_ready", "o_ready", "o_done", "stored", "loop_steps", "coef_ready", "found")
        G, U = AG[:, 0:QC], AG[:, QC:2 * QC]
        S = AG[:, 2 * QC:2 * QC + 2]
        block = ctx.enter_context(nc.Block())

        def scales(dve, step, a, n, factor=None):
            step(dve.tensor_scalar(sc[:, a:a + n], red[:, a:a + n], 1.0 / 32767.0, 1e-12, ALU.mult, ALU.max))
            step(dve.reciprocal(sc[:, a + 8:a + 8 + n], sc[:, a:a + n]))

        @block.gpsimd
        def _(pool):
            for n, (a, k) in enumerate(((0, 1), (1, 2), (3, 1), (4, 1))):
                pool.wait_ge(found, n + 1)
                pool.partition_all_reduce(red[:, a:a + k], big[:, a:a + k], 128, RMAX).then_inc(reduced, 1)

        @block.vector
        def _(dve):
            step = Steps(dve, steps, 0, None)
            dve.tensor_reduce(big[:, 0:1], largest[:, :], AX.X, ALU.max).then_inc(found, 1)
            dve.wait_ge(reduced, 1)
            scales(dve, step, 0, 1)
            for k, c in ((0, scale5), (1, shift5)):
                ins = dve.tensor_scalar(coef[:, k], c[:, :], sc[0:P, 8:9], None, ALU.mult)
            ins.then_inc(coef_ready, 1)
            dve.wait_ge(coef_ready, 1)
            with dve.Fori(0, PAIRS) as g:
                wait_at(dve, tq_ready, 4 * g + 4, None)
                lstep = Steps(dve, loop_steps, 2 * g, None)
                for s in range(2):
                    ins = dve.tensor_scalar(q[:, s], tile_of(X, 2 * g + s), coef[:, 0, bass.ds(2 * g + s, 1)],
                                            coef[:, 1, bass.ds(2 * g + s, 1)], ALU.mult, ALU.add)
                lstep(ins)
                for s in range(2):
                    ins = dve.tensor_scalar(q[:, s], q[:, s], MAGIC, None, ALU.add)
                lstep(ins)
                dve.tensor_scalar(q[:, :, :].rearrange("p s d -> p (s d)"), q[:, :, :].rearrange("p s d -> p (s d)"),
                                  -MAGIC, 32767.0, ALU.add, ALU.min).then_inc(q_ready, 1)
                wait_at(dve, h_done, 3 * g + 3 + 3, None)
                dve.tensor_reduce(big2[:, :, bass.ds(g, 1)],
                                  AG[:, 0:2 * QC, bass.ds(PAIR * g, PAIR)].rearrange("p (a m) n -> p a m n", a=2),
                                  AX.XY, ALU.max, apply_absolute_value=True).then_inc(down_ready, 1)
            dve.wait_ge(down_ready, PAIRS)
            dve.tensor_reduce(big[:, 1:3], big2[:, :, :], AX.X, ALU.max).then_inc(found, 1)
            dve.wait_ge(reduced, 2)
            scales(dve, step, 1, 2)
            for c in range(QC):
                step(dve.tensor_scalar(G[:, c], G[:, c], sc[:, 9:10], MAGIC, ALU.mult, ALU.add))
                step(dve.tensor_scalar(G[:, c], G[:, c], -MAGIC, 32767.0, ALU.add, ALU.min))
                dve.tensor_scalar(G[:, c], G[:, c], sc[:, 1:2], None, ALU.mult).then_inc(sig_in, 1)
            for c in range(QC):
                step(dve.tensor_scalar(U[:, c], U[:, c], sc[:, 10:11], MAGIC, ALU.mult, ALU.add))
                step(dve.tensor_scalar(U[:, c], U[:, c], -MAGIC, 32767.0, ALU.add, ALU.min))
            for c in range(QC):
                dve.wait_ge(sig_out, c + 1)
                s = S[:, c % 2]
                step(dve.tensor_scalar(s, s, 65536.0, MAGIC, ALU.mult, ALU.add))
                step(dve.tensor_scalar(s, s, -MAGIC, 65535.0, ALU.add, ALU.min))
                dve.wait_ge(sig_in, QC)
                dve.scalar_tensor_tensor(G[:, c], s, 1.0 / 65536.0, G[:, c], ALU.mult, ALU.mult).then_inc(oq_ready, 1)
                dve.wait_ge(oq_ready, c + 1)
                step(dve.tensor_reduce(big3[:, 0, c:c + 1], G[:, c], AX.X, ALU.max, apply_absolute_value=True))
            dve.tensor_reduce(big[:, 3:4], big3[:, 0], AX.X, ALU.max).then_inc(found, 1)
            dve.wait_ge(reduced, 3)
            scales(dve, step, 3, 1)
            step(dve.tensor_tensor(sc[:, 5:6], sc[:, 3:4], sc[:, 2:3], ALU.mult))
            for c in range(QC):
                step(dve.tensor_scalar(G[:, c], G[:, c], sc[:, 11:12], MAGIC, ALU.mult, ALU.add))
                step(dve.tensor_scalar(G[:, c], G[:, c], -MAGIC, 32767.0, ALU.add, ALU.min))
                step(dve.tensor_tensor(G[:, c], G[:, c], U[:, c], ALU.mult))
                step(dve.tensor_reduce(big3[:, 1, c:c + 1], G[:, c], AX.X, ALU.max, apply_absolute_value=True))
            step(dve.tensor_reduce(big[:, 5:6], big3[:, 1], AX.X, ALU.max))
            dve.tensor_tensor(big[:, 4:5], big[:, 5:6], sc[:, 5:6], ALU.mult).then_inc(found, 1)
            dve.wait_ge(reduced, 4)
            scales(dve, step, 4, 1)
            step(dve.tensor_tensor(sc[:, 6:7], sc[:, 5:6], sc[:, 12:13], ALU.mult))
            with dve.Fori(0, PAIRS) as g:
                lstep = Steps(dve, loop_steps, 2 * PAIRS + g, None)
                lstep(dve.tensor_scalar(oq[:, 0], G[:, :, bass.ds(PAIR * g, PAIR)], sc[:, 6:7], MAGIC,
                                        ALU.mult, ALU.add))
                wait_at(dve, o_ready, 4 * g + 4, None)
                dve.tensor_scalar(oq[:, 1], oq[:, 0], -MAGIC, 32767.0, ALU.add, ALU.min).then_inc(oq_ready, 1)
                for part in range(4):
                    s, half = part // 2, part % 2
                    wait_at(dve, o_ready, 4 * g + part + 1 + 4, None)
                    t = tile_of(X, 2 * g + s)[:, 512 * half:512 * half + 512]
                    dve.scalar_tensor_tensor(t, O[half][0:P, :], sc[0:P, 4:5], t, ALU.mult, ALU.add).then_inc(o_done, 1)

        @block.scalar
        def _(act):
            act.wait_ge(coef_ready, 1)
            with act.Fori(0, PAIRS) as g:
                for j in range(4):
                    wait_at(act, tq_ready, 4 * g + j + 1 + 4, None)
                    if j == 0:
                        wait_at(act, h_ready, 3 * g + 3, None)
                    act.activation(qT[:, 2 * j:2 * j + 2, :].rearrange("p a n -> p (a n)"), TQ[j % 2][:, 0:2 * PAIR],
                                   ACT.Copy).then_inc(tq_done, 1)
                for j in range(QC):
                    wait_at(act, h_ready, 3 * g + j + 1 + 3, None)
                    act.activation(AG[:, 2 * j:2 * j + 2, bass.ds(PAIR * g, PAIR)],
                                   H[j][:, 0:2 * PAIR].rearrange("p (a n) -> p a n", a=2), ACT.Copy,
                                   scale=sc[:, 0:1]).then_inc(h_done, 1)
            for c in range(QC):
                act.wait_ge(sig_in, c + 1)
                if c >= 2:
                    act.wait_ge(oq_ready, c - 1)
                act.activation(S[:, c % 2], G[:, c], ACT.Sigmoid).then_inc(sig_out, 1)

        @block.tensor
        def _(pe):
            for free, n in ((tq_done, 2), (tq_ready, 4), (h_done, 3), (h_ready, 3), (o_done, 2), (o_ready, 4)):
                pe.sem_inc(free, n)
            with pe.Fori(0, PAIRS) as g:
                wait_at(pe, q_ready, g + 1, None)
                for j in range(4):
                    wait_at(pe, tq_done, 4 * g + j + 1, None)
                    for c in range(2):
                        for s in range(2):
                            at, f = PAIR * c + P * s, 128 * (2 * j + c)
                            ins = pe.transpose(TQ[j % 2][:, at:at + P], q[:, s, f:f + 128], ident[0:P, 0:P])
                    ins.then_inc(tq_ready, 1)
                wait_at(pe, tq_done, 4 * g + 4 + 2, None)
                for j in range(QC):
                    wait_at(pe, h_done, 3 * g + j + 1, None)
                    for m in range(2):
                        for k in range(KD):
                            w = guT[:, k, 128 * (2 * j + m):128 * (2 * j + m) + 128]
                            ins = pe.matmul(H[j][:, PAIR * m:PAIR * m + PAIR], w, qT[:, k, :],
                                            start=(k == 0), stop=(k == KD - 1))
                    ins.then_inc(h_ready, 1)
            with pe.Fori(0, PAIRS) as g:
                wait_at(pe, oq_ready, g + QC + 1, None)
                for part in range(4):
                    s, half = part // 2, part % 2
                    wait_at(pe, o_done, 4 * g + part + 1, None)
                    for k in range(QC):
                        ins = pe.matmul(O[half][0:P, :], oq[:, 1, k, P * s:P * s + P],
                                        wdT[:, k, 512 * half:512 * half + 512], start=(k == 0), stop=(k == QC - 1))
                    ins.then_inc(o_ready, 1)

        @block.sync
        def _(sp):
            with sp.Fori(0, PAIRS) as g:
                for s in range(2):
                    sp.wait_ge(o_done, 4 * g + 2 * s + 2 + 2)
                    sp.nop(nofuse=True)
                    sp.dma_start(out.rearrange("(t p) d -> p t d", p=P)[:, bass.ds(2 * g + s, 1), :],
                                 X[:, bass.ds(2 * g + s, 1), :]).then_inc(stored, 16)
            sp.wait_ge(stored, 16 * TILES)


def program(nc, a, out):
    with ExitStack() as top:
        ident = sb(nc, top, "ident", [128, 128])
        X = sb(nc, top, "X", [P, TILES, D])
        CT = sb(nc, top, "CT", [128, TILES, BLOCKS * WIN], U16)
        dinv, scale4, shift4, scale5, shift5 = (
            sb(nc, top, n, [P, TILES]) for n in ("dinv", "scale4", "shift4", "scale5", "shift5"))
        largest = sb(nc, top, "largest", [128, TILES])
        WT = sb(nc, top, "WT", [128, WCH, D])
        deg_dram = nc.dram_tensor("deg_dram", (BLOCKS * WIN,), F32).ap()
        build_matrices(nc, a["src"], a["dst"], a["edge_weight"], a["x"], X, ident, WT, CT, dinv, deg_dram)
        layer0(nc, [a["L0_" + n] for n in LAYER0], X, ident, WT, scale4, shift4, dinv)
        AG = sb(nc, top, "AG", [128, KD, N])
        aggregate(nc, X, CT, WT, AG, scale4, shift4, a["L1_gnn_W"], a["L1_ffn_w_gate"], a["L1_ffn_w_up"])
        guT = sb(nc, top, "guT", [128, KD, 2 * QI])
        wdT = sb(nc, top, "wdT", [128, QC, D])
        layer1_gnn(nc, X, CT, WT, AG, ident, guT, wdT, dinv, scale5, shift5, largest, a["L1_gnn_b"],
                   a["L1_ffn_w_down"])
        quantised_ffn(nc, X, AG, guT, wdT, ident, scale5, shift5, largest, out)


def kernel(**inputs):
    import concourse.bacc as bacc
    from concourse.bass_utils import run_bass_kernel_spmd

    nc = bacc.Bacc("TRN2", target_bir_lowering=False, num_devices=1)
    arrays = {k: np.ascontiguousarray(v) for k, v in inputs.items()}
    args = {k: nc.dram_tensor(f"in_{k}", v.shape, mybir.dt.from_np(v.dtype), kind="ExternalInput").ap()
            for k, v in arrays.items()}
    out = nc.dram_tensor("out", (N, D), F32, kind="ExternalOutput").ap()
    program(nc, args, out)
    r = run_bass_kernel_spmd(nc, [{f"in_{k}": v for k, v in arrays.items()}], core_ids=[0])
    return r.results[0]["out"]
```

```python
from contextlib import ExitStack

import concourse.bass as bass
import numpy as np
from concourse import mybir

F32 = mybir.dt.float32
F32R = mybir.dt.float32r
BF16 = mybir.dt.bfloat16
F16 = mybir.dt.float16
I16 = mybir.dt.int16
U32 = mybir.dt.uint32
I32 = mybir.dt.int32
ALU = mybir.AluOpType
ACT = mybir.ActivationFunctionType
AX = mybir.AxisListType
RMAX = bass.bass_isa.ReduceOp.max

N = 1250
D = 1024
E = 21250
P = 125
TILES = N // P
PAIRS = TILES // 2
ET = E // P
EH = ET // 2
WIN = 32
BLOCKS = 40
CHUNKS = 10
WCH = D // 128
KD = D // 128
ENDS = 4
MIDDLE = 2
H1 = 256
M1 = 64
EX = 8
QI = 384
QC = QI // 128
PAIR = 2 * P
EPS = 1e-5
RAW = 2
LAYER0 = ("gnn_bias", "ffn_enc_W", "ffn_enc_b", "ffn_s2c_W", "ffn_s2c_b", "ffn_rW1", "ffn_rb1", "ffn_rW2",
          "ffn_rb2", "ffn_We1", "ffn_be1", "ffn_We2", "ffn_be2", "ffn_c2s_W", "ffn_c2s_b", "ffn_dec_W",
          "ffn_dec_b", "ffn_ln_g", "ffn_ln_b")
STEPS = 15
COUNT_PART = 4096
PARTS = ((0, 0), (1, 0), (0, 1))
MAGIC = 12582912.0


class Link:

    def __init__(self, eng, sem, base=0):
        self.eng, self.sem, self.base, self.n = eng, sem, base, 0

    def __call__(self, ins):
        self.step(ins)
        self.wait()

    def step(self, ins):
        ins.then_inc(self.sem, 1)
        self.n += 1

    def wait(self):
        self.eng.wait_ge(self.sem, self.base + self.n)


def sb(nc, ctx, name, shape, dt=F32):
    return ctx.enter_context(nc.sbuf_tensor(name, shape, dt))


def psum(nc, ctx, name, shape, dt=F32):
    return ctx.enter_context(nc.psum_tensor(name, shape, dt))


def sems(nc, ctx, *names):
    return [ctx.enter_context(nc.semaphore(n)) for n in names]


def build_matrices(nc, src, dst, weight, x, X, ident, WT, CT, deg, dinv, deg_dram):
    with ExitStack() as ctx:
        dst_i = sb(nc, ctx, "dst_i", [EH, 2, P], I32)
        src_i = sb(nc, ctx, "src_i", [EH, 2, P], I32)
        rows = sb(nc, ctx, "rows", [EH, 3, 2, P])
        record = sb(nc, ctx, "record", [P, ET, 4])
        coef = record[:, :, :].bitcast(BF16)[:, :, 4:8]
        weights = sb(nc, ctx, "weights", [P, ET])
        rest = sb(nc, ctx, "rest", [P, 2, ET])
        zeros = sb(nc, ctx, "zeros", [P, 128], BF16)
        iota_i = sb(nc, ctx, "iota_i", [P, BLOCKS * WIN], I32)
        iota_h = sb(nc, ctx, "iota_h", [P, BLOCKS * WIN], F16)
        first_i = sb(nc, ctx, "first_i", [EH, BLOCKS + 4], I32)
        first = sb(nc, ctx, "first", [EH, BLOCKS + 4])
        ends = sb(nc, ctx, "ends", [EH, 4])
        touch = sb(nc, ctx, "touch", [EH, 2, BLOCKS])
        marks = sb(nc, ctx, "marks", [EH, 4, BLOCKS])
        most = sb(nc, ctx, "most", [EH, 4, BLOCKS])
        span = sb(nc, ctx, "span", [1, 2, BLOCKS])
        table = sb(nc, ctx, "table", [1, BLOCKS, 2], I32)
        left = sb(nc, ctx, "left", [P, ENDS + MIDDLE, 128], BF16)
        right = sb(nc, ctx, "right", [P, ENDS + MIDDLE, N], BF16)
        block_out = sb(nc, ctx, "block_out", [128, 4, N])
        degrees = sb(nc, ctx, "degrees", [128, BLOCKS])
        parts = sb(nc, ctx, "parts", [128, 2, 3, D])
        counts = sb(nc, ctx, "counts", [128, 2, N])
        mhalf = sb(nc, ctx, "mhalf", [P, TILES])
        held = sb(nc, ctx, "held", [1, 4])
        B = [psum(nc, ctx, f"B{i}", [128, 3 * 512]) for i in range(2)]
        TP = [psum(nc, ctx, f"TP{i}", [128, 512]) for i in range(2)]

        (edges_in, rows_ready, iota_ready, ident_ready, cols_turned, cols_ready, coef_ready, marks_ready,
         most_ready, table_ready, front_free, middle_free, back_free, front_ready, middle_ready, back_ready, block_built, block_copied, w_summed,
         turned, evacuated, loop_link, deg_out, deg_in, dinv_ready, x_in, diag_ready) = sems(
            nc, ctx, "edges_in", "rows_ready", "iota_ready", "ident_ready", "cols_turned", "cols_ready",
            "coef_ready", "marks_ready", "most_ready", "table_ready", "front_free", "middle_free", "back_free",
            "front_ready", "middle_ready", "back_ready",
            "block_built", "block_copied", "w_summed", "turned", "evacuated", "loop_link",
            "deg_out", "deg_in", "dinv_ready", "x_in", "diag_ready")
        moved = [sems(nc, ctx, *(f"moved{par}{q}" for q in range(4))) for par in range(2)]
        dve_link, pool_link = sems(nc, ctx, "dve_link", "pool_link")
        weights_in = sems(nc, ctx, "weights_in")[0]

        def chunk_pairs(eng, body):
            with eng.Fori(0, WCH // 2) as g:
                body(g, True, False)
            body(WCH // 2, False, True)

        def block_range(eng, registers, b):
            eng.load(registers, table[0:1, bass.ds(b, 1), :])
            return (eng.snap(registers[0], min_val=0, max_val=ET - ENDS - 1),
                    eng.snap(registers[1], min_val=ENDS + 1, max_val=ET))

        block = ctx.enter_context(nc.Block())

        @block.sync
        def _(sp):
            for tile, ap in ((dst_i, dst), (src_i, src)):
                sp.dma_start(tile[:, :, :], ap.rearrange("(h q k) -> q h k", h=2, k=P)).then_inc(edges_in, 16)
            sp.dma_start(rows[:, 2], weight.rearrange("(h q k) -> q h k", h=2, k=P)).then_inc(edges_in, 16)

            copied, summed, read = (sp.alloc_register(n) for n in ("copied", "summed", "read"))
            for register, value in ((copied, 3), (summed, 1), (read, 3)):
                sp.reg_mov(register, value)

            def body(g, with_w, last):
                for par in range(2):
                    for q in range(4):
                        sp.wait_ge(block_copied, copied)
                        if q == 0:
                            sp.wait_ge(w_summed, summed)
                            sp.wait_ge(turned, read)
                        lanes = slice(32 * q, 32 * q + 32)
                        sp.dma_start(counts[lanes, par], block_out[0:32, q]).then_inc(moved[par][q], 16)
                        if with_w:
                            for k in range(3):
                                sp.dma_start(parts[lanes, par, k], block_out[32 * k + 32:32 * k + 64, q, 0:D]
                                             ).then_inc(moved[par][q], 16)
                        sp.reg_add(copied, copied, 1)
                        if q == 3:
                            sp.reg_add(summed, summed, 1)
                            sp.reg_add(read, read, 3)

            chunk_pairs(sp, body)
            sp.dma_start(deg_dram.rearrange("(b p) -> p b", p=WIN), degrees[0:32, :],
                         allow_slow_non_contiguous=True).then_inc(deg_out, 16)
            sp.wait_ge(deg_out, 16)
            sp.dma_start(deg[:, :], deg_dram[0:N].rearrange("(t p) -> p t", p=P),
                         allow_slow_non_contiguous=True).then_inc(deg_in, 16)
            sp.wait_ge(deg_in, 16)

        @block.gpsimd
        def _(pool):
            pool.memset(ident[:, :], 0.0).then_inc(pool_link, 1)
            pool.wait_ge(pool_link, 1)
            pool.affine_select(out=ident[:, :], in_=ident[:, :], compare_op=ALU.not_equal, fill=1.0, base=0,
                               pattern=[[-1, 128]], channel_multiplier=1).then_inc(ident_ready, 1)
            pool.iota(iota_i[:, :], [[1, BLOCKS * WIN]], base=0, channel_multiplier=0).then_inc(iota_ready, 1)
            pool.iota(first_i[:, 0:BLOCKS], [[WIN, BLOCKS]], base=0, channel_multiplier=0).then_inc(iota_ready, 1)
            pool.iota(first_i[:, BLOCKS:BLOCKS + 2], [[EH, 2]], base=1, channel_multiplier=1).then_inc(iota_ready, 1)
            pool.iota(first_i[:, BLOCKS + 2:], [[-EH, 2]], base=ET, channel_multiplier=-1).then_inc(iota_ready, 1)
            pool.memset(mhalf[:, :], -0.5).then_inc(iota_ready, 1)
            pool.wait_ge(marks_ready, 1)
            pool.partition_all_reduce(most[:, :, :], marks[:, :, :], EH, RMAX).then_inc(most_ready, 1)

            def hold(k):
                pool.tensor_tensor(held[:, k:k + 1], mhalf[0:1, 0:1], mhalf[0:1, 0:1], ALU.add)

            with pool.Fori(0, WCH // 2) as g:
                for par in range(2):
                    for q in range(4):
                        pool.wait_ge(moved[par][q], 64 * g + 64)
                    hold(2 * par)
                    c = 2 * g + par
                    out = WT[:, bass.ds(c, 1), :].rearrange("p a d -> p (a d)")
                    pool.tensor_tensor(out, parts[:, par, 0], parts[:, par, 1], ALU.add).then_inc(loop_link, 1)
                    pool.wait_ge(loop_link, c + 1)
                    hold(2 * par + 1)
                    pool.tensor_tensor(out, out, parts[:, par, 2], ALU.add).then_inc(w_summed, 1)
            pool.wait_ge(deg_in, 16)
            pool.tensor_scalar(deg[:, :], deg[:, :], 1.0, None, ALU.add).then_inc(pool_link, 1)
            pool.wait_ge(pool_link, 2)
            pool.wait_ge(iota_ready, 5)
            pool.tensor_tensor(dinv[:, :], deg[:, :], mhalf[:, :], ALU.pow).then_inc(dinv_ready, 1)

        @block.vector
        def _(dve):
            link = Link(dve, dve_link)
            dve.wait_ge(edges_in, 48)
            dve.tensor_copy(rows[:, 0], dst_i[:, :, :]).then_inc(rows_ready, 1)
            dve.tensor_copy(rows[:, 1], src_i[:, :, :]).then_inc(rows_ready, 1)
            dve.wait_ge(iota_ready, 4)
            dve.tensor_copy(iota_h[:, :], iota_i[:, :]).then_inc(dve_link, 1)
            link.n += 1
            dve.wait_ge(rows_ready, 1)
            link(dve.tensor_reduce(ends[:, 0:2], rows[:, 0], AX.X, ALU.min))
            link(dve.tensor_reduce(ends[:, 2:4], rows[:, 0], AX.X, ALU.max))
            link(dve.tensor_copy(first[:, :], first_i[:, :]))
            link(dve.tensor_scalar(ends[:, 0:2], ends[:, 0:2], -float(WIN), None, ALU.add))
            for h in range(2):
                link(dve.tensor_scalar(touch[:, h], first[:, 0:BLOCKS], ends[:, h:h + 1], None, ALU.is_gt))
                link(dve.scalar_tensor_tensor(touch[:, h], first[:, 0:BLOCKS], ends[:, 2 + h:3 + h], touch[:, h],
                                              ALU.is_le, ALU.mult))
                link(dve.tensor_scalar(marks[:, h], touch[:, h], first[:, BLOCKS + h:BLOCKS + h + 1], None,
                                       ALU.mult))
                ins = dve.tensor_scalar(marks[:, 2 + h], touch[:, h], first[:, BLOCKS + 2 + h:BLOCKS + 3 + h],
                                        None, ALU.mult)
                if h == 0:
                    link(ins)
            ins.then_inc(marks_ready, 1)
            dve.wait_ge(cols_turned, 1)
            dve.tensor_copy(weights[:, :], TP[0][0:P, 2 * ET:3 * ET]).then_inc(cols_ready, 1)
            for k in range(2):
                dve.tensor_copy(record[:, :, k], TP[0][0:P, k * ET:k * ET + ET]).then_inc(cols_ready, 1)
            dve.memset(coef[:, :, 0], 1.0).then_inc(coef_ready, 1)
            dve.memset(zeros[:, :], 0.0).then_inc(coef_ready, 1)
            dve.wait_ge(cols_ready, 1)
            link(dve.tensor_copy(coef[:, :, 1], weights[:, :]))
            link(dve.tensor_tensor(rest[:, 0], weights[:, :], coef[:, :, 1], ALU.subtract))
            link(dve.tensor_copy(coef[:, :, 2], rest[:, 0]))
            link(dve.tensor_tensor(rest[:, 1], rest[:, 0], coef[:, :, 2], ALU.subtract))
            dve.tensor_copy(coef[:, :, 3], rest[:, 1]).then_inc(coef_ready, 1)
            dve.wait_ge(most_ready, 1)
            link(dve.tensor_tensor(span[:, 1], most[0:1, 0], most[0:1, 1], ALU.max))
            link(dve.tensor_tensor(span[:, 0], most[0:1, 2], most[0:1, 3], ALU.max))
            link(dve.tensor_scalar(span[:, 0], span[:, 0], -1.0, float(ET), ALU.mult, ALU.add))
            link(dve.tensor_scalar(span[:, 0], span[:, 0], float(ET - ENDS - 1), None, ALU.min))
            link(dve.scalar_tensor_tensor(span[:, 1], span[:, 0], float(ENDS + 1), span[:, 1], ALU.add, ALU.max))
            dve.tensor_copy(table[:, :, :].rearrange("a b k -> a k b"), span[:, :, :]).then_inc(table_ready, 1)
            dve.wait_ge(table_ready, 1)
            dve.wait_ge(coef_ready, 3)
            dve.wait_ge(cols_ready, 3)

            bounds = [dve.alloc_register(n) for n in ("made_lo", "made_hi")]
            made = dve.alloc_register("middles_made")
            dve.reg_mov(made, 0)

            def one_hots(b, slot, t):
                dve.scalar_tensor_tensor(
                    left[:, slot, :].rearrange("p a (k d) -> p (a k) d", k=4),
                    iota_h[:, bass.ds(WIN * b, WIN)].unsqueeze(1).broadcast_to([P, 4, WIN]),
                    record[:, bass.ds(t, 1), 0:1].rearrange("p a k -> p (a k)"),
                    coef[:, bass.ds(t, 1), :].rearrange("p a k -> p (a k)").unsqueeze(2).broadcast_to([P, 4, WIN]),
                    ALU.is_equal, ALU.mult)
                return dve.tensor_scalar(right[:, slot, :].rearrange("p a d -> p (a d)"), iota_h[:, 0:N],
                                         record[:, bass.ds(t, 1), 1:2].rearrange("p a k -> p (a k)"), None,
                                         ALU.is_equal)

            def body(g, with_w, last):
                for k in range(8):
                    b = 8 * g + k
                    lo, hi = block_range(dve, bounds, b)
                    dve.wait_ge(front_free, b + 1)
                    one_hots(b, slice(0, 1), lo)
                    one_hots(b, slice(1, 2), lo + 1).then_inc(front_ready, 1)
                    with dve.Fori(lo + 2, hi - 2) as t:
                        n = dve.snap(made, min_val=0, max_val=BLOCKS * ET)
                        dve.wait_ge(middle_free, n + 1)
                        one_hots(b, bass.ds(n % MIDDLE + ENDS, 1), t).then_inc(middle_ready, 1)
                        dve.reg_add(made, made, 1)
                    dve.wait_ge(back_free, b + 1)
                    one_hots(b, slice(2, 3), hi - 2)
                    one_hots(b, slice(3, 4), hi - 1).then_inc(back_ready, 1)

            chunk_pairs(dve, body)
            for j in range(TILES):
                dve.wait_ge(evacuated, 3 * CHUNKS + 2)
                ins = dve.tensor_tensor(CT[0:P, j, P * j:P * j + P], CT[0:P, j, P * j:P * j + P], ident[0:P, 0:P], ALU.add)
            ins.then_inc(diag_ready, 1)
            dve.wait_ge(diag_ready, 1)

        @block.tensor
        def _(pe):
            pe.sem_inc(front_free, 1)
            pe.sem_inc(middle_free, MIDDLE)
            pe.sem_inc(back_free, 1)
            for free in (block_copied, evacuated, w_summed):
                pe.sem_inc(free, 2)
            pe.sem_inc(turned, 6)
            pe.wait_ge(edges_in, 48)
            pe.wait_ge(rows_ready, 2)
            pe.wait_ge(ident_ready, 1)
            for k in range(3):
                for h in range(2):
                    at = (2 * k + h) * EH
                    ins = pe.transpose(TP[0][0:P, at:at + EH], rows[:, k, h], ident[0:EH, 0:EH])
            ins.then_inc(cols_turned, 1)
            pe.wait_ge(cols_ready, 3)
            pe.wait_ge(coef_ready, 2)
            pe.wait_ge(table_ready, 1)
            bounds = [pe.alloc_register(n) for n in ("used_lo", "used_hi")]
            used = pe.alloc_register("middles_used")
            pe.reg_mov(used, 0)

            def products(out, slot, start=False, stop=False):
                lhs = left[:, slot, :].rearrange("p a d -> p (a d)")
                for at in range(0, N, 512):
                    size = min(512, N - at)
                    ins = pe.matmul(out[:, at:at + size], lhs,
                                    right[:, slot, at:at + size].rearrange("p a d -> p (a d)"), start=start, stop=stop)
                return ins

            def build(g, k):
                b, out = 8 * g + k, B[k % 2]
                lo, hi = block_range(pe, bounds, b)
                pe.wait_ge(block_copied, b + 1)
                pe.wait_ge(front_ready, b + 1)
                products(out, slice(0, 1), start=True)
                products(out, slice(1, 2)).then_inc(front_free, 1)
                with pe.Fori(lo + 2, hi - 2):
                    n = pe.snap(used, min_val=0, max_val=BLOCKS * ET)
                    pe.wait_ge(middle_ready, n + 1)
                    products(out, bass.ds(n % MIDDLE + ENDS, 1)).then_inc(middle_free, 1)
                    pe.reg_add(used, used, 1)
                pe.wait_ge(back_ready, b + 1)
                products(out, slice(2, 3))
                products(out, slice(3, 4), stop=True).then_inc(back_free, 1)
                pe.matmul(out[:, 1535:1536], zeros[:, :], zeros[:, 0:1], start=True, stop=True
                          ).then_inc(block_built, 1)

            def turn(g, par, per):
                for q in range(4):
                    pe.wait_ge(moved[par][q], per)
                for k in range(3):
                    pe.wait_ge(evacuated, 6 * g + 3 * par + k + 1)
                    for j in range(4 * k, min(4 * k + 4, TILES)):
                        ins = pe.transpose(TP[(k + par) % 2][0:P, 128 * (j % 4):128 * (j % 4) + 128],
                                           counts[:, par, P * j:P * j + P], ident[:, :])
                    ins.then_inc(turned, 1)

            def body(g, with_w, last):
                got = 64 * g + 64 if with_w else 64 * g + 16
                for k in (2, 3, 4, 5):
                    build(g, k)
                turn(g, 0, got)
                for k in (6, 7) + (() if last else (8, 9)):
                    build(g, k)
                turn(g, 1, got)

            build(0, 0)
            build(0, 1)
            chunk_pairs(pe, body)

        @block.scalar
        def _(act):
            for t in range(TILES):
                act.dma_start(X[:, t], x[P * t:P * t + P, :]).then_inc(x_in, 16)

            def copy(g, k, last_pair=False):
                b, q = 8 * g + k, k % 4
                act.wait_ge(block_built, b + 1)
                if k >= 8:
                    act.wait_ge(moved[1][q], 64 * g + 64)
                elif k >= 4:
                    act.wait_ge(moved[0][q], 64 * g + (64 if not last_pair else 16))
                act.activation(block_out[:, q], B[k % 2][:, 0:N], ACT.Copy,
                               accum_out=degrees[:, bass.ds(b, 1)]).then_inc(block_copied, 1)

            def evacuate(g, par):
                for k in range(3):
                    j, m = 4 * k, min(4, TILES - 4 * k)
                    act.wait_ge(turned, 6 * g + 3 * par + k + 7)
                    act.activation(CT[0:P, j:j + m, bass.ds(128 * (2 * g + par), 128)],
                                   TP[(k + par) % 2][0:P, 0:128 * m].rearrange("p (j d) -> p j d", j=m),
                                   ACT.Copy).then_inc(evacuated, 1)

            def body(g, with_w, last):
                for k in (2, 3, 4, 5):
                    copy(g, k, last)
                evacuate(g, 0)
                for k in (6, 7) + (() if last else (8, 9)):
                    copy(g, k, last)
                evacuate(g, 1)

            copy(0, 0)
            copy(0, 1)
            chunk_pairs(act, body)
            act.wait_ge(x_in, 16 * TILES)


def wait_at(eng, sem, value):
    eng.wait_ge(sem, value)
    if not isinstance(value, int):
        eng.nop(nofuse=True)


class Steps:

    def __init__(self, eng, sem, base):
        self.eng, self.sem, self.base, self.n = eng, sem, base, 0

    def __call__(self, ins):
        ins.then_inc(self.sem, 1)
        self.n += 1
        wait_at(self.eng, self.sem, self.base + self.n)


def tile_of(X, i):
    return X[:, bass.ds(i, 1), :].rearrange("p a d -> p (a d)")


def layer0(nc, weights, X, ident, WT, scale4, shift4, deg, dinv, passes):
    (bias0, enc_W, enc_b, s2c_W, s2c_b, rW1, rb1, rW2, rb2, We1, be1, We2, be2, c2s_W, c2s_b,
     dec_W, dec_b, ln_g, ln_b) = weights
    with ExitStack() as ctx:
        encW = sb(nc, ctx, "encW", [128, KD, H1])
        decW = sb(nc, ctx, "decW", [128, 2, D])
        s2cW = sb(nc, ctx, "s2cW", [128, 2, M1])
        rW1s = sb(nc, ctx, "rW1s", [M1, M1])
        rW2s = sb(nc, ctx, "rW2s", [M1, EX])
        We1s = sb(nc, ctx, "We1s", [M1, EX, 128])
        We2s = sb(nc, ctx, "We2s", [128, EX, M1])
        c2sW = sb(nc, ctx, "c2sW", [M1, H1])
        encb = sb(nc, ctx, "encb", [128, 2])
        s2cb = sb(nc, ctx, "s2cb", [M1, 1])
        rb1s = sb(nc, ctx, "rb1s", [M1, 1])
        be1s = sb(nc, ctx, "be1s", [128, EX])
        c2sb = sb(nc, ctx, "c2sb", [128, 2])
        rb2r = sb(nc, ctx, "rb2r", [P, EX])
        be2r = sb(nc, ctx, "be2r", [P, EX * M1])
        bias0r = sb(nc, ctx, "bias0r", [P, D])
        decbr = sb(nc, ctx, "decbr", [P, D])
        lngr = sb(nc, ctx, "lngr", [P, D])
        lnbr = sb(nc, ctx, "lnbr", [P, D])
        xn1 = sb(nc, ctx, "xn1", [P, 2, D])
        xn2 = sb(nc, ctx, "xn2", [P, 2, D])
        xT1 = sb(nc, ctx, "xT1", [128, KD, PAIR])
        xT2 = sb(nc, ctx, "xT2", [128, KD, PAIR])
        flatT = sb(nc, ctx, "flatT", [128, 2, PAIR])
        contT = sb(nc, ctx, "contT", [M1, PAIR])
        routT = sb(nc, ctx, "routT", [M1, PAIR])
        hT = sb(nc, ctx, "hT", [128, EX, PAIR])
        logits = sb(nc, ctx, "logits", [P, 2, EX])
        top8 = sb(nc, ctx, "top8", [P, 2, EX])
        top_i = sb(nc, ctx, "top_i", [P, 2, EX], U32)
        top_f = sb(nc, ctx, "top_f", [P, 2, EX])
        lead = sb(nc, ctx, "lead", [P, 2, 2])
        share = sb(nc, ctx, "share", [P, 2, 2])
        iota8i = sb(nc, ctx, "iota8i", [P, EX], I32)
        iota8 = sb(nc, ctx, "iota8", [P, EX])
        first = sb(nc, ctx, "first_gate", [P, 2, EX])
        gates = sb(nc, ctx, "gates", [P, 2, EX])
        mixed = sb(nc, ctx, "mixed", [P, 2, EX * M1])
        moe = sb(nc, ctx, "moe", [P, 2, M1])
        moeT = sb(nc, ctx, "moeT", [M1, PAIR])
        spikT = sb(nc, ctx, "spikT", [128, 2, PAIR])
        dec = sb(nc, ctx, "dec", [P, 2, D])
        stats = sb(nc, ctx, "stats", [P, 4, 2, 2, 6])
        mv = sb(nc, ctx, "mv", [P, 4, 2, 2])
        veps = sb(nc, ctx, "veps", [P, 4, 2])
        rstd = sb(nc, ctx, "rstd", [P, 4, 2])
        mhalf = sb(nc, ctx, "mhalf2", [P, 2])
        deg_most = sb(nc, ctx, "deg_most", [P, TILES])
        most = sb(nc, ctx, "most_parts", [1, 1])
        nmean = sb(nc, ctx, "nmean", [P, 2])
        TR = [psum(nc, ctx, f"TR{i}", [128, 512]) for i in range(2)]
        Y = [psum(nc, ctx, f"Y{i}", [128, 512]) for i in range(2)]
        DP = [psum(nc, ctx, f"DP{i}", [128, 512]) for i in range(2)]
        F = [psum(nc, ctx, f"F{i}", [128, 512]) for i in range(2)]
        (w_in, consts, tr_ready, y_ready, y_free, f_ready, lead_ready, share_ready, moe_ready,
         dec_ready, dec_free, dec_done, x_biased, x_shifted, normed, gained, x2_ready, scaled, pool_steps,
         steps_first, steps_loop, steps_last, deg_found, parts_steps, rows_in) = sems(
            nc, ctx, "w_in", "consts", "tr_ready", "y_ready", "y_free", "f_ready", "lead_ready",
            "share_ready", "moe_ready", "dec_ready", "dec_free", "dec_done", "x_biased", "x_shifted", "normed",
            "gained", "x2_ready", "scaled", "pool_steps", "steps_first", "steps_loop", "steps_last",
            "deg_found", "parts_steps", "rows_in")
        f_done = sems(nc, ctx, "f_done0", "f_done1")
        tr_free = sems(nc, ctx, "xn1_turned", "xn2_turned")
        xn_ready = sems(nc, ctx, "xn1_ready", "xn2_ready")
        var_ready = sems(nc, ctx, *(f"var_ready{k}" for k in range(1, 5)))
        rstd_ready = sems(nc, ctx, *(f"rstd_ready{k}" for k in range(1, 5)))
        LAST = PAIRS - 1
        LOADS = 17

        def pairs(eng, prologue, body):
            prologue()
            with eng.Fori(0, LAST - 1) as p:
                body(p, p + 1, p + 2)
            body(LAST - 1, LAST, None)
            body(LAST, None, None)

        def is_first(p):
            return isinstance(p, int) and p == 0

        def fill(p, k):
            return 8 * p + 4 * (k - 1)

        block = ctx.enter_context(nc.Block())

        @block.sync
        def _(sp):
            loads = []

            def load(tile, ap, slow=False, sem=w_in):
                loads.append(1)
                sp.dma_start(tile, ap, allow_slow_non_contiguous=slow).then_inc(sem, 16)

            def row(v, n):
                return v.rearrange("(a n) -> a n", a=1).broadcast_to([P, n])

            load(bias0r[:, :], row(bias0, D), sem=rows_in)
            load(lnbr[:, :], row(ln_b, D), sem=rows_in)
            load(encW[:, :, :], enc_W.rearrange("(k p) m -> p k m", p=128))
            load(encb[:, :], enc_b.rearrange("(c p) -> p c", p=128), True)
            load(s2cW[:, :, :], s2c_W.rearrange("(k p) m -> p k m", p=128))
            load(s2cb[:, :], s2c_b.rearrange("(p a) -> p a", a=1), True)
            load(rW1s[:, :], rW1)
            load(rb1s[:, :], rb1.rearrange("(p a) -> p a", a=1), True)
            load(rW2s[:, :], rW2)
            load(rb2r[:, :], row(rb2, EX))
            load(We1s[:, :, :], We1.rearrange("e m h -> m e h"))
            load(be1s[:, :], be1.rearrange("e h -> h e"), True)
            load(We2s[:, :, :], We2.rearrange("e h m -> h e m"))
            load(be2r[:, :], row(be2.rearrange("e m -> (e m)"), EX * M1))
            load(c2sW[:, :], c2s_W)
            load(c2sb[:, :], c2s_b.rearrange("(c p) -> p c", p=128), True)
            load(decW[:, :, :], dec_W.rearrange("(k p) d -> p k d", p=128))
            load(decbr[:, :], row(dec_b, D))
            load(lngr[:, :], row(ln_g, D))
            assert len(loads) == LOADS + 2
            sp.wait_ge(rows_in, 32)
            sp.wait_ge(w_in, 16 * LOADS)

        @block.tensor
        def _(pe):
            for free, n in ((y_free, 2), (dec_free, 2), (f_done[0], 1), (f_done[1], 1), (f_ready, 12)):
                pe.sem_inc(free, n)

            def turn(p, k):
                xn = (xn1, xn2)[k - 1]
                wait_at(pe, xn_ready[k - 1], p + 1)
                for j in range(4):
                    if j >= 2:
                        wait_at(pe, tr_free[k - 1], 4 * p + j - 1)
                    elif k == 2:
                        wait_at(pe, tr_free[0], 4 * p + j + 3)
                    elif not is_first(p):
                        wait_at(pe, tr_free[1], 4 * p + j - 1)
                    for c in range(2):
                        for s in range(2):
                            at, f = PAIR * c + P * s, 128 * (2 * j + c)
                            ins = pe.transpose(TR[j % 2][:, at:at + P], xn[:, s, f:f + 128], ident[0:P, 0:P])
                    ins.then_inc(tr_ready, 1)

            def gnn(p, part):
                s, half = part // 2, part % 2
                if part == 0:
                    wait_at(pe, tr_free[0], 4 * p + 4)
                wait_at(pe, y_free, 4 * p + part + 1)
                for k in range(KD):
                    ins = pe.matmul(Y[half][0:P, :], xT1[:, k, P * s:P * s + P], WT[:, k, 512 * half:512 * half + 512],
                                    start=(k == 0), stop=(k == KD - 1))
                ins.then_inc(y_ready, 1)

            def use(p, u):
                wait_at(pe, f_done[u % 2], 6 * p + u // 2 + 1)
                return F[u % 2]

            def left_bank(p, u):
                wait_at(pe, f_done[u % 2], 6 * p + u // 2 + 2)

            def prologue():
                turn(0, 1)
                for part in range(4):
                    gnn(0, part)

            def body(p, n, m):
                turn(p, 2)
                if n is not None:
                    turn(n, 1)
                pe.wait_ge(w_in, 16 * LOADS)
                wait_at(pe, tr_free[1], 4 * p + 4)
                f = use(p, 0)
                for m in range(2):
                    for k in range(KD):
                        ins = pe.matmul(f[:, PAIR * m:PAIR * m + PAIR], encW[:, k, 128 * m:128 * m + 128], xT2[:, k, :],
                                        start=(k == 0), stop=(k == KD - 1))
                ins.then_inc(f_ready, 1)
                if n is not None:
                    gnn(n, 0)
                left_bank(p, 0)
                f = use(p, 1)
                for k in range(2):
                    ins = pe.matmul(f[0:M1, 0:PAIR], s2cW[:, k, :], flatT[:, k, :], start=(k == 0), stop=(k == 1))
                ins.then_inc(f_ready, 1)
                if n is not None:
                    gnn(n, 1)
                left_bank(p, 1)
                f = use(p, 2)
                pe.matmul(f[0:M1, 0:PAIR], rW1s[:, :], contT[:, :], start=True, stop=True).then_inc(f_ready, 1)
                for u in range(4):
                    f = use(p, 3 + u)
                    for e in range(2):
                        ins = pe.matmul(f[:, PAIR * e:PAIR * e + PAIR], We1s[:, 2 * u + e, :], contT[:, :],
                                        start=True, stop=True)
                    ins.then_inc(f_ready, 1)
                left_bank(p, 2)
                f = use(p, 7)
                for s in range(2):
                    ins = pe.matmul(f[0:P, EX * s:EX * s + EX], routT[:, P * s:P * s + P], rW2s[:, :],
                                    start=True, stop=True)
                ins.then_inc(f_ready, 1)
                left_bank(p, 5)
                left_bank(p, 6)
                for s in range(2):
                    f = use(p, 8 + s)
                    for e in range(EX):
                        ins = pe.matmul(f[0:P, M1 * e:M1 * e + M1], hT[:, e, P * s:P * s + P], We2s[:, e, :],
                                        start=True, stop=True)
                    ins.then_inc(f_ready, 1)
                if n is not None:
                    gnn(n, 2)
                wait_at(pe, moe_ready, 2 * p + 2)
                f = use(p, 10)
                for s in range(2):
                    ins = pe.transpose(f[0:M1, P * s:P * s + P], moe[:, s, :], ident[0:P, 0:P])
                ins.then_inc(f_ready, 1)
                if n is not None:
                    gnn(n, 3)
                left_bank(p, 10)
                f = use(p, 11)
                for m in range(2):
                    ins = pe.matmul(f[:, PAIR * m:PAIR * m + PAIR], c2sW[:, 128 * m:128 * m + 128], moeT[:, :],
                                    start=True, stop=True)
                ins.then_inc(f_ready, 1)
                left_bank(p, 11)
                for part in range(4):
                    s, half = part // 2, part % 2
                    wait_at(pe, dec_free, 4 * p + part + 1)
                    for k in range(2):
                        ins = pe.matmul(DP[half][0:P, :], spikT[:, k, P * s:P * s + P],
                                        decW[:, k, 512 * half:512 * half + 512], start=(k == 0), stop=(k == 1))
                    ins.then_inc(dec_ready, 1)

            pairs(pe, prologue, body)

        @block.scalar
        def _(act):

            def evacuate_xn1(p):
                if not is_first(p):
                    wait_at(act, y_ready, 4 * p)
                for j in range(4):
                    wait_at(act, tr_ready, fill(p, 1) + j + 1)
                    act.activation(xT1[:, 2 * j:2 * j + 2, :].rearrange("p a n -> p (a n)"),
                                   TR[j % 2][:, 0:2 * PAIR], ACT.Copy).then_inc(tr_free[0], 1)

            def computed(p, u):
                wait_at(act, f_ready, 12 * p + u + 13)
                return F[u % 2]

            def prologue():
                evacuate_xn1(0)

            def body(p, n, m):
                if n is not None:
                    evacuate_xn1(n)
                act.wait_ge(w_in, 16 * LOADS)
                f = computed(p, 0)
                for m in range(2):
                    ins = act.activation(flatT[:, m, :], f[:, PAIR * m:PAIR * m + PAIR], ACT.Sigmoid,
                                         bias=encb[:, m:m + 1])
                ins.then_inc(f_done[0], 1)
                f = computed(p, 1)
                act.activation(contT[:, :], f[0:M1, 0:PAIR], ACT.Identity, bias=s2cb[:, :]).then_inc(f_done[1], 1)
                f = computed(p, 2)
                act.activation(routT[:, :], f[0:M1, 0:PAIR], ACT.Tanh, bias=rb1s[:, :]).then_inc(f_done[0], 1)
                for u in range(4):
                    f = computed(p, 3 + u)
                    for e in range(2):
                        ins = act.activation(hT[:, 2 * u + e, :], f[:, PAIR * e:PAIR * e + PAIR], ACT.Relu,
                                             bias=be1s[:, 2 * u + e:2 * u + e + 1])
                    ins.then_inc(f_done[(3 + u) % 2], 1)
                wait_at(act, lead_ready, p + 1)
                act.activation(share[:, :, :], lead[:, :, :], ACT.Sigmoid).then_inc(share_ready, 1)
                f = computed(p, 11)
                for m in range(2):
                    ins = act.activation(spikT[:, m, :], f[:, PAIR * m:PAIR * m + PAIR], ACT.Sigmoid,
                                         bias=c2sb[:, m:m + 1])
                ins.then_inc(f_done[1], 1)
                for part in range(4):
                    wait_at(act, dec_free, 4 * p + part + 3)
                    at = dec[:, part // 2, 512 * (part % 2):512 * (part % 2) + 512]
                    act.activation(at, at, ACT.Sigmoid).then_inc(dec_done, 1)

            pairs(act, prologue, body)

        @block.gpsimd
        def _(pool):
            pool.memset(mhalf[:, :], -0.5).then_inc(consts, 1)
            pool.iota(iota8i[:, :], [[1, EX]], base=0, channel_multiplier=0).then_inc(consts, 1)
            pool.partition_all_reduce(deg_most[:, :], deg[:, :], P, RMAX).then_inc(deg_found, 1)
            pool.wait_ge(consts, 2)

            def inverse_root(p, k):
                wait_at(pool, var_ready[k - 1], p + 1)
                return pool.tensor_tensor(rstd[:, k - 1], veps[:, k - 1], mhalf[:, :], ALU.pow)

            def first_norm(p, k):
                vector, added = ((bias0r, x_biased), (lnbr, x_shifted))[k - 1]
                inverse_root(p, k).then_inc(rstd_ready[k - 1], 1)
                wait_at(pool, xn_ready[k - 1], p + 1)
                if is_first(p):
                    pool.wait_ge(rows_in, 32)
                for s in range(2):
                    t = tile_of(X, 2 * p + s)
                    ins = pool.tensor_tensor(t, t, vector[:, :], ALU.add)
                ins.then_inc(added, 1)

            def prologue():
                first_norm(0, 1)
                first_norm(1, 1)
                first_norm(0, 2)

            def body(p, n, m):
                if m is not None:
                    first_norm(m, 1)
                if n is not None:
                    first_norm(n, 2)
                inverse_root(p, 3).then_inc(rstd_ready[2], 1)
                pool.wait_ge(w_in, 16 * LOADS)
                wait_at(pool, normed, p + 1)
                for s in range(2):
                    ins = pool.tensor_tensor(dec[:, s, :], dec[:, s, :], lngr[:, :], ALU.mult)
                ins.then_inc(gained, 1)
                inverse_root(p, 4).then_inc(pool_steps, 1)
                pool.tensor_scalar(nmean[:, :], mv[:, 3, :, 0], -1.0, None, ALU.mult).then_inc(pool_steps, 1)
                wait_at(pool, pool_steps, 3 * p + 2)
                pool.tensor_tensor(scale4[:, bass.ds(2 * p, 2)], rstd[:, 3], dinv[:, bass.ds(2 * p, 2)], ALU.mult
                                   ).then_inc(pool_steps, 1)
                wait_at(pool, pool_steps, 3 * p + 3)
                pool.tensor_tensor(shift4[:, bass.ds(2 * p, 2)], nmean[:, :], scale4[:, bass.ds(2 * p, 2)], ALU.mult
                                   ).then_inc(scaled, 1)

            pairs(pool, prologue, body)

        @block.vector
        def _(dve):
            dve.wait_ge(consts, 2)
            dve.tensor_copy(iota8[:, :], iota8i[:, :]).then_inc(consts, 1)
            dve.wait_ge(consts, 3)

            def norm(step, p, k, rows):
                k -= 1
                for s in range(2):
                    for half in range(2):
                        ins = dve.bn_stats(stats[:, k, s, half], rows(s)[:, 512 * half:512 * half + 512])
                step(ins)
                for s in range(2):
                    ins = dve.bn_aggr(mv[:, k, s], stats[:, k, s].rearrange("p a b -> p (a b)"))
                step(ins)
                dve.tensor_scalar(veps[:, k], mv[:, k, :, 1], EPS, None, ALU.add).then_inc(var_ready[k], 1)

            def apply(p, k, s, out, rows):
                return dve.tensor_scalar(out, rows, mv[:, k - 1, s, 0:1], rstd[:, k - 1, s:s + 1],
                                         ALU.subtract, ALU.mult)

            def normalise(step, p, k):
                xn = (xn1, xn2)[k - 1]
                norm(step, p, k, lambda s: tile_of(X, 2 * p + s))
                if not is_first(p):
                    wait_at(dve, tr_ready, fill(p, k) - 4)
                wait_at(dve, rstd_ready[k - 1], p + 1)
                for s in range(2):
                    ins = apply(p, k, s, xn[:, s, :], tile_of(X, 2 * p + s))
                ins.then_inc(xn_ready[k - 1], 1)

            def add_gnn(p, part):
                s, half = part // 2, part % 2
                wait_at(dve, y_ready, 4 * p + part + 1)
                if part == 0:
                    wait_at(dve, x_biased, p + 1)
                t = tile_of(X, 2 * p + s)[:, 512 * half:512 * half + 512]
                return dve.tensor_tensor(t, Y[half][0:P, :], t, ALU.add).then_inc(y_free, 1)

            def added(p):
                wait_at(dve, y_free, 4 * p + 4 + 2)

            def computed(p, u):
                wait_at(dve, f_ready, 12 * p + u + 13)
                return F[u % 2]

            def evacuate_xn2(p):
                wait_at(dve, f_ready, 12 * p + 1)
                for j in range(4):
                    wait_at(dve, tr_ready, fill(p, 2) + j + 1)
                    dve.tensor_copy(xT2[:, 2 * j:2 * j + 2, :].rearrange("p a n -> p (a n)"),
                                    TR[j % 2][:, 0:2 * PAIR]).then_inc(tr_free[1], 1)

            def prologue():
                step = Steps(dve, steps_first, 0)
                normalise(step, 0, 1)
                normalise(step, 1, 1)
                for part in range(4):
                    add_gnn(0, part)
                added(0)
                normalise(step, 0, 2)
                evacuate_xn2(0)

            def body(p, n, m):
                step = last_step if m is None else Steps(dve, steps_loop, STEPS * p)
                if n is not None:
                    add_gnn(n, 0)
                if m is not None:
                    normalise(step, m, 1)
                if n is not None:
                    add_gnn(n, 1)
                dve.wait_ge(w_in, 16 * LOADS)
                f = computed(p, 7)
                dve.tensor_tensor(logits[:, :, :], f[0:P, 0:2 * EX].rearrange("p (s e) -> p s e", s=2),
                                  rb2r[:, :].unsqueeze(1).broadcast_to([P, 2, EX]), ALU.add).then_inc(f_done[1], 1)
                wait_at(dve, f_done[1], 6 * p + 3 + 2)
                for s in range(2):
                    ins = dve.max(top8[:, s], logits[:, s])
                step(ins)
                for s in range(2):
                    last_index = dve.max_index(top_i[:, s], top8[:, s], logits[:, s])
                step(last_index)
                dve.tensor_tensor(lead[:, :, 0], top8[:, :, 0], top8[:, :, 1], ALU.subtract)
                dve.tensor_tensor(lead[:, :, 1], top8[:, :, 1], top8[:, :, 0], ALU.subtract).then_inc(lead_ready, 1)
                step(dve.tensor_copy(top_f[:, :, :], top_i[:, :, :]))
                wait_at(dve, share_ready, p + 1)
                for s in range(2):
                    for out, k in ((first, 0), (gates, 1)):
                        ins = dve.tensor_scalar(out[:, s], iota8[:, :], top_f[:, s, k:k + 1], share[:, s, k:k + 1],
                                                ALU.is_equal, ALU.mult)
                step(ins)
                step(dve.tensor_tensor(gates[:, :, :], gates[:, :, :], first[:, :, :], ALU.add))
                for s in range(2):
                    f = computed(p, 8 + s)
                    ins = dve.tensor_tensor(mixed[:, s], f[0:P, :], be2r[:, :], ALU.add).then_inc(f_done[s], 1)
                wait_at(dve, f_done[0], 6 * p + 4 + 2)
                wait_at(dve, f_done[1], 6 * p + 4 + 2)
                for s in range(2):
                    mix = mixed[:, s].rearrange("p (e m) -> p e m", e=EX)
                    ins = dve.tensor_tensor(mix, mix, gates[:, s].unsqueeze(2).broadcast_to([P, EX, M1]), ALU.mult)
                step(ins)
                for s in range(2):
                    dve.tensor_reduce(moe[:, s], mixed[:, s].rearrange("p (e m) -> p m e", e=EX), AX.X, ALU.add
                                      ).then_inc(moe_ready, 1)
                if n is not None:
                    add_gnn(n, 2)
                f = computed(p, 10)
                dve.tensor_copy(moeT[:, :], f[0:M1, 0:PAIR]).then_inc(f_done[0], 1)
                if n is not None:
                    add_gnn(n, 3)
                    added(n)
                    normalise(step, n, 2)
                for part in range(4):
                    s, half = part // 2, part % 2
                    wait_at(dve, dec_ready, 4 * p + part + 1)
                    dve.tensor_tensor(dec[:, s, 512 * half:512 * half + 512], DP[half][0:P, :],
                                      decbr[:, 512 * half:512 * half + 512], ALU.add).then_inc(dec_free, 1)
                if n is not None:
                    evacuate_xn2(n)
                wait_at(dve, dec_done, 4 * p + 4)
                norm(step, p, 3, lambda s: dec[:, s, :])
                wait_at(dve, rstd_ready[2], p + 1)
                for s in range(2):
                    ins = apply(p, 3, s, dec[:, s, :], dec[:, s, :])
                ins.then_inc(normed, 1)
                wait_at(dve, gained, p + 1)
                wait_at(dve, x_shifted, p + 1)
                for s in range(2):
                    t = tile_of(X, 2 * p + s)
                    ins = dve.tensor_tensor(t, t, dec[:, s, :], ALU.add)
                step(ins)
                norm(step, p, 4, lambda s: tile_of(X, 2 * p + s))
                assert m is None or step.n == STEPS, step.n

            last_step = Steps(dve, steps_last, 0)
            pairs(dve, prologue, body)
            dve.wait_ge(deg_found, 1)
            parts = Steps(dve, parts_steps, 0)
            parts(dve.tensor_reduce(most[:, :], deg_most[0:1, :], AX.X, ALU.max))
            parts(dve.tensor_scalar(most[:, :], most[:, :], 0.5 + float(COUNT_PART), None, ALU.is_gt))
            parts(dve.tensor_scalar(most[:, :], most[:, :], 1.0, None, ALU.add))
            parts(dve.tensor_copy(passes[:, :], most[:, :]))
            dve.wait_ge(scaled, PAIRS)


def quant_view(CT):
    return CT[:, :, :].rearrange("p t d -> p (t d)").bitcast(F32)[:, 0:2 * QC * D].rearrange("p (m d) -> p m d", d=D)


class Dequantise:

    def __init__(self, nc, ctx, name, blocks):
        self.buf = sb(nc, ctx, name, [128, 3, blocks])
        self.shape = [128, blocks, 32]
        self.scales_ready, self.divided, self.rounded, self.ready = sems(
            nc, ctx, *(name + n for n in ("_scales", "_divided", "_rounded", "_ready")))

    def scales(self, dve, step, w, n):
        if not isinstance(n, int) or n > 0:
            wait_at(dve, self.ready, n)
        step(dve.tensor_reduce(self.buf[:, 0], w, AX.X, ALU.max, apply_absolute_value=True))
        step(dve.tensor_scalar(self.buf[:, 1], self.buf[:, 0], 1.0 / 7.0, 1e-12, ALU.mult, ALU.max))
        dve.reciprocal(self.buf[:, 2], self.buf[:, 1]).then_inc(self.scales_ready, 1)

    def divide(self, pool, w, n):
        wait_at(pool, self.scales_ready, n + 1)
        pool.tensor_tensor(w, w, self.buf[:, 2].unsqueeze(2).broadcast_to(self.shape), ALU.mult
                           ).then_inc(self.divided, 1)

    def round(self, dve, step, w, n):
        wait_at(dve, self.divided, n + 1)
        step(dve.tensor_scalar(w, w, MAGIC, None, ALU.add))
        dve.tensor_scalar(w, w, -MAGIC, 7.0, ALU.add, ALU.min).then_inc(self.rounded, 1)

    def multiply(self, pool, w, n):
        wait_at(pool, self.rounded, n + 1)
        pool.tensor_tensor(w, w, self.buf[:, 1].unsqueeze(2).broadcast_to(self.shape), ALU.mult
                           ).then_inc(self.ready, 1)


def chunk_products(pe, out, high, low, counts, before=None):
    for i in range(TILES):
        if before is not None:
            before(i)
        for part in (high, low):
            for at in range(0, N, 512):
                size = min(512, N - at)
                ins = pe.matmul(out[:, at:at + size], part[:, i, :], counts[:, i, at:at + size],
                                start=(i == 0 and part is high), stop=(i == TILES - 1 and part is low))
    return ins


def aggregate_rest(nc, X, CT, AG, CTf, high, low, A, value, scale4, shift4, passes):
    with ExitStack() as ctx:
        rest_steps, rest_staged, rest_done = sems(nc, ctx, "rest_steps", "rest_staged", "rest_done")
        block = ctx.enter_context(nc.Block())

        def if_needed(eng):
            needed = eng.alloc_register("passes_needed")
            eng.reg_load(needed, passes[0:1, 0:1])
            return eng.If_ne(needed, 1)

        @block.vector
        def _(dve):
            with if_needed(dve):
                step = Steps(dve, rest_steps, 0)
                for i in range(TILES):
                    step(dve.tensor_copy(CTf[:, i, :], CT[0:P, i, 0:N]))
                    step(dve.tensor_tensor(CTf[:, i, :], CT[0:P, i, 0:N], CTf[:, i, :].bitcast(F32), ALU.subtract))
                with dve.Fori(0, KD) as f:
                    step = Steps(dve, rest_steps, 2 * TILES + 4 * f)
                    step(dve.tensor_tensor(value, X[:, :, bass.ds(128 * f, 128)],
                                           scale4[:, :].unsqueeze(2).broadcast_to([P, TILES, 128]), ALU.mult))
                    step(dve.tensor_tensor(value, value, shift4[:, :].unsqueeze(2).broadcast_to([P, TILES, 128]),
                                           ALU.add))
                    step(dve.tensor_copy(high[:, 0], value))
                    step(dve.tensor_tensor(low[:, 0], value, high[:, 0].bitcast(F32), ALU.subtract))
                    dve.sem_inc(rest_staged, 1)
                    wait_at(dve, rest_done, 2 * f + 1)
                    dve.tensor_copy(AG[:, bass.ds(f, 1), :].rearrange("p a n -> p (a n)"), A[0][:, 0:N]
                                    ).then_inc(rest_done, 1)
                    wait_at(dve, rest_done, 2 * f + 2)

        @block.tensor
        def _(pe):
            with if_needed(pe):
                with pe.Fori(0, KD) as f:
                    wait_at(pe, rest_staged, f + 1)
                    chunk_products(pe, A[0], high[:, 0], low[:, 0], CTf).then_inc(rest_done, 1)


def aggregate(nc, X, CT, w1raw, AG, scale4, shift4, passes, w_layer1, w_gate, w_up):
    with ExitStack() as ctx:
        CTf = sb(nc, ctx, "CTf", [P, TILES, N], F32R)
        high = sb(nc, ctx, "high", [P, 2, TILES, 128], F32R)
        low = sb(nc, ctx, "low", [P, 2, TILES, 128], F32R)
        values = sb(nc, ctx, "values", [P, 2, TILES, 128])
        A = [psum(nc, ctx, f"A{i}", [128, 3 * 512]) for i in range(2)]
        aggregate_rest(nc, X, CT, AG, CTf, high, low, A, values[:, 0], scale4, shift4, passes)
        (w1_in, quant_in, counts_even, counts_odd, zeroed, staged_ready, agg_ready, agg_done, valued,
         high_ready, zero_steps) = sems(
            nc, ctx, "w1_in", "quant_in", "counts_even", "counts_odd", "zeroed4", "staged_ready", "agg_ready",
            "agg_done", "valued", "high_ready", "zero_steps")
        GU = quant_view(CT)
        block = ctx.enter_context(nc.Block())

        @block.sync
        def _(sp):
            sp.dma_start(w1raw[:, :, :], w_layer1.rearrange("(k p) d -> p k d", p=128)[:, 0:RAW]).then_inc(w1_in, 16)
            sp.wait_ge(counts_even, TILES // 2)
            sp.wait_ge(counts_odd, TILES // 2)
            sp.dma_start(GU[:, 0:QC], w_gate.rearrange("(m p) d -> p m d", p=128)).then_inc(quant_in, 16)
            sp.dma_start(GU[:, QC:2 * QC], w_up.rearrange("(m p) d -> p m d", p=128)).then_inc(quant_in, 16)
            sp.wait_ge(w1_in, 16)
            sp.wait_ge(quant_in, 32)

        @block.gpsimd
        def _(pool):
            for i in range(1, TILES, 2):
                pool.tensor_copy(CTf[:, i, :], CT[0:P, i, 0:N]).then_inc(counts_odd, 1)
            needed = pool.alloc_register("passes_needed")
            pool.reg_load(needed, passes[0:1, 0:1])
            with pool.If_eq(needed, 1):
                pool.memset(AG[:, :, :].rearrange("p k n -> p (k n)"), 0.0).then_inc(zero_steps, 1)
                pool.wait_ge(zero_steps, 1)
            pool.sem_inc(zeroed, 1)

        @block.scalar
        def _(act):
            def value(f, par):
                wait_at(act, staged_ready, f + 1)
                for i in range(TILES):
                    ins = act.activation(values[:, par, i, :], X[:, i, bass.ds(128 * f, 128)], ACT.Identity,
                                         scale=scale4[:, i:i + 1], bias=shift4[:, i:i + 1])
                ins.then_inc(valued, 1)
                wait_at(act, valued, f + 1)
                wait_at(act, agg_ready, f + 1)
                act.activation(high[:, par], values[:, par], ACT.Copy).then_inc(high_ready, 1)

            with act.Fori(0, KD // 2) as g:
                for par in range(2):
                    value(2 * g + par, par)

        @block.vector
        def _(dve):
            def counts(i):
                dve.tensor_copy(CTf[:, i, :], CT[0:P, i, 0:N]).then_inc(counts_even, 1)

            def remainder(f, par):
                wait_at(dve, agg_ready, f + 1)
                wait_at(dve, high_ready, f + 1)
                dve.tensor_tensor(low[:, par], values[:, par], high[:, par].bitcast(F32), ALU.subtract
                                  ).then_inc(staged_ready, 1)

            def add(f, par):
                wait_at(dve, agg_ready, f + 3)
                at = AG[:, bass.ds(f, 1), :].rearrange("p a n -> p (a n)")
                dve.tensor_tensor(at, A[par][:, 0:N], at, ALU.add).then_inc(agg_done, 1)

            for i in (0, 2, 4):
                counts(i)
            remainder(0, 0)
            for i in (6, 8):
                counts(i)
            remainder(1, 1)
            dve.wait_ge(zeroed, 1)
            with dve.Fori(0, KD // 2 - 1) as g:
                for par in range(2):
                    add(2 * g + par, par)
                    remainder(2 * g + par + 2, par)
            add(KD - 2, 0)
            add(KD - 1, 1)
            dve.wait_ge(agg_done, KD + 2)

        @block.tensor
        def _(pe):
            def products(f, par, before=None):
                wait_at(pe, staged_ready, f + 1 + 2)
                wait_at(pe, agg_done, f + 1)
                chunk_products(pe, A[par], high[:, par], low[:, par], CTf, before).then_inc(agg_ready, 1)

            def tile_ready(i):
                pe.wait_ge((counts_even, counts_odd)[i % 2], i // 2 + 1)

            for free in (agg_ready, agg_done, staged_ready):
                pe.sem_inc(free, 2)
            products(0, 0, tile_ready)
            products(1, 1)
            with pe.Fori(1, KD // 2) as g:
                for par in range(2):
                    products(2 * g + par, par)


def layer1_gnn(nc, X, GU, w1raw, AG, dinv, scale5, shift5, largest, w_layer1, bias1):
    with ExitStack() as ctx:
        W1h = sb(nc, ctx, "W1h", [128, KD, D], F32R)
        W1l = sb(nc, ctx, "W1l", [128, KD, D], F32R)
        agh = sb(nc, ctx, "agh", [128, 2, KD, P], F32R)
        agl = sb(nc, ctx, "agl", [128, 2, KD, P], F32R)
        biasr = sb(nc, ctx, "biasr", [P, D])
        z = sb(nc, ctx, "z", [P, 2, D])
        stats = sb(nc, ctx, "stats5", [P, 2, 2, 6])
        mv = sb(nc, ctx, "mv5", [P, 2, 2])
        veps = sb(nc, ctx, "veps5", [P, 2])
        rstd = sb(nc, ctx, "rstd5", [P, 2])
        nmean = sb(nc, ctx, "nmean5", [P, 2])
        mhalf = sb(nc, ctx, "mhalf5", [P, 2])
        Z = [psum(nc, ctx, f"Z{i}", [128, 512]) for i in range(4)]
        raw_in = sems(nc, ctx, *(f"raw_in{k}" for k in range(RAW)))
        (bias_in, w1_high, w1_split, ag_high, ag_split, z_ready, z_free, zeroed, var_ready, rstd_ready,
         pool_steps, first_steps, loop_steps, last_steps) = sems(
            nc, ctx, "bias_in", "w1_high", "w1_split", "ag_high", "ag_split", "z_ready", "z_free",
            "zeroed", "var_ready5", "rstd_ready5", "pool_steps5", "first_steps5", "loop_steps5", "last_steps5")
        quant = Dequantise(nc, ctx, "gu_quant", D // 32)
        LAST = PAIRS - 1
        X3_STEPS = 8
        block = ctx.enter_context(nc.Block())

        def columns(i):
            return AG[:, :, bass.ds(P * i, P)]

        def weights_of(m):
            return GU[:, bass.ds(m, 1), :].rearrange("p m (b k) -> p (m b) k", k=32)

        @block.sync
        def _(sp):
            sp.dma_start(biasr[:, :], bias1.rearrange("(a n) -> a n", a=1).broadcast_to([P, D])).then_inc(bias_in, 16)
            w1 = w_layer1.rearrange("(k p) d -> p k d", p=128)
            for k in range(RAW, KD):
                sp.wait_ge(w1_split, k - RAW + 1)
                sp.dma_start(w1raw[:, k % RAW], w1[:, k]).then_inc(raw_in[k % RAW], 16)
            for buffer, sem in enumerate(raw_in):
                sp.wait_ge(sem, 16 * len(range(RAW + buffer, KD, RAW)))
            sp.wait_ge(bias_in, 16)

        @block.gpsimd
        def _(pool):
            pool.memset(mhalf[:, :], -0.5).then_inc(zeroed, 1)
            pool.memset(largest[:, :], 0.0).then_inc(zeroed, 1)
            pool.wait_ge(zeroed, 2)
            quant.divide(pool, weights_of(2 * QC - 1), 0)
            quant.multiply(pool, weights_of(2 * QC - 1), 0)
            with pool.Fori(0, PAIRS) as g:
                quant.divide(pool, weights_of(g), g + 1)
                wait_at(pool, var_ready, g + 1)
                pool.tensor_tensor(rstd[:, :], veps[:, :], mhalf[:, :], ALU.pow).then_inc(rstd_ready, 1)
                pool.tensor_scalar(nmean[:, :], mv[:, :, 0], -1.0, None, ALU.mult).then_inc(pool_steps, 1)
                wait_at(pool, rstd_ready, g + 1)
                wait_at(pool, pool_steps, 2 * g + 1)
                pool.tensor_copy(scale5[:, bass.ds(2 * g, 2)], rstd[:, :])
                pool.tensor_tensor(shift5[:, bass.ds(2 * g, 2)], nmean[:, :], rstd[:, :], ALU.mult
                                   ).then_inc(pool_steps, 1)
                quant.multiply(pool, weights_of(g), g + 1)

        @block.tensor
        def _(pe):
            pe.sem_inc(z_free, 4)

            def products(part, k):
                s, half = part // 2, part % 2
                for n, (a, b) in enumerate(PARTS):
                    ins = pe.matmul(Z[part][0:P, :], (agh, agl)[a][:, s, k, :],
                                    (W1h, W1l)[b][:, k, 512 * half:512 * half + 512],
                                    start=(k == 0 and n == 0), stop=(k == KD - 1 and n == 2))
                return ins

            pe.wait_ge(ag_split, 2)
            for k in range(KD):
                pe.wait_ge(w1_split, k + 1)
                for part in range(4):
                    ins = products(part, k)
                    if k == KD - 1:
                        ins.then_inc(z_ready, 1)
            with pe.Fori(1, PAIRS) as g:
                for part in range(4):
                    wait_at(pe, ag_split, 2 * g + part // 2 + 1)
                    wait_at(pe, z_free, 4 * g + part + 1)
                    for k in range(KD):
                        ins = products(part, k)
                    ins.then_inc(z_ready, 1)

        @block.scalar
        def _(act):
            def high(i, s):
                act.activation(agh[:, s], columns(i), ACT.Copy).then_inc(ag_high, 1)

            high(0, 0)
            high(1, 1)
            for k in range(KD):
                if k >= RAW:
                    act.wait_ge(raw_in[k % RAW], 16 * (k // RAW))
                act.activation(W1h[:, k], w1raw[:, k % RAW], ACT.Copy).then_inc(w1_high, 1)
            with act.Fori(0, LAST) as g:
                for s in range(2):
                    wait_at(act, z_ready, 4 * g + 2 * s + 2)
                    high(2 * g + 2 + s, s)

        @block.vector
        def _(dve):
            def low(i, s):
                wait_at(dve, ag_high, i + 1)
                dve.tensor_tensor(agl[:, s], columns(i), agh[:, s].bitcast(F32), ALU.subtract).then_inc(ag_split, 1)

            def dense(g, s):
                for half in range(2):
                    part = 2 * s + half
                    wait_at(dve, z_ready, 4 * g + part + 1)
                    at = slice(512 * half, 512 * half + 512)
                    dve.scalar_tensor_tensor(z[:, s, at], Z[part][0:P, :], dinv[:, bass.ds(2 * g + s, 1)],
                                             biasr[:, at], ALU.mult, ALU.add).then_inc(z_free, 1)

            def body(step, g, more):
                quant.scales(dve, step, weights_of(g), g + 1)
                for s in range(2):
                    dense(g, s)
                    if more:
                        low(2 * g + 2 + s, s)
                wait_at(dve, z_free, 4 * g + 8)
                for s in range(2):
                    t = tile_of(X, 2 * g + s)
                    ins = dve.scalar_tensor_tensor(t, z[:, s], 0.0, t, ALU.max, ALU.add)
                step(ins)
                for s in range(2):
                    for half in range(2):
                        ins = dve.bn_stats(stats[:, s, half], tile_of(X, 2 * g + s)[:, 512 * half:512 * half + 512])
                step(ins)
                if more is None or not isinstance(g, int):
                    wait_at(dve, pool_steps, 2 * g)
                for s in range(2):
                    ins = dve.bn_aggr(mv[:, s], stats[:, s].rearrange("p a b -> p (a b)"))
                step(ins)
                dve.tensor_scalar(veps[:, :], mv[:, :, 1], EPS, None, ALU.add).then_inc(var_ready, 1)
                quant.round(dve, step, weights_of(g), g + 1)
                wait_at(dve, rstd_ready, g + 1)
                for s in range(2):
                    ins = dve.tensor_scalar(z[:, s], tile_of(X, 2 * g + s), mv[:, s, 0:1], rstd[:, s:s + 1],
                                            ALU.subtract, ALU.mult)
                step(ins)
                ins = dve.tensor_reduce(largest[0:P, bass.ds(2 * g, 2)], z[:, :, :], AX.X, ALU.max,
                                        apply_absolute_value=True)
                step(ins)
                assert step.n == X3_STEPS, step.n

            low(0, 0)
            low(1, 1)
            for k in range(KD):
                dve.wait_ge(w1_high, k + 1)
                dve.tensor_tensor(W1l[:, k], w1raw[:, k % RAW], W1h[:, k].bitcast(F32), ALU.subtract
                                  ).then_inc(w1_split, 1)
            step = Steps(dve, first_steps, 0)
            quant.scales(dve, step, weights_of(2 * QC - 1), 0)
            quant.round(dve, step, weights_of(2 * QC - 1), 0)
            dve.wait_ge(bias_in, 16)
            dve.wait_ge(zeroed, 2)
            with dve.Fori(0, LAST) as g:
                body(Steps(dve, loop_steps, X3_STEPS * g), g, True)
            body(Steps(dve, last_steps, 0), LAST, False)
            dve.wait_ge(quant.ready, PAIRS + 1)


def quantised_ffn(nc, X, GU, AG, ident, scale5, shift5, largest, w_down, out):
    with ExitStack() as ctx:
        guT = [sb(nc, ctx, n, [128, KD, 2 * QI], F32R) for n in ("guT_high", "guT_low")]
        wd = GU[:, 0:QC, :].rearrange("p m d -> p (m d)").rearrange("p (c k) -> p c k", k=QI)
        wdT = [w[:, 0:QC * D // (2 * QI), :].rearrange("p k n -> p (k n)").rearrange("p (k n) -> p k n", n=D)
               for w in guT]
        q = sb(nc, ctx, "q", [P, 2, D])
        qT = [sb(nc, ctx, n, [128, 2, KD, PAIR], F32R) for n in ("qT_high", "qT_low")]
        o_magic = sb(nc, ctx, "o_magic", [128, 2, QC, P])
        oq = sb(nc, ctx, "oq", [128, 2, QC, P])
        oq_parts = [sb(nc, ctx, n, [128, 2, QC, P], F32R) for n in ("oq_high", "oq_low")]
        magic = sb(nc, ctx, "magic", [128, 1])
        big = sb(nc, ctx, "big", [128, 16])
        red = sb(nc, ctx, "red", [128, 16])
        sc = sb(nc, ctx, "sc", [128, 16])
        coef = sb(nc, ctx, "coef5", [P, 2, TILES])
        big2 = sb(nc, ctx, "big2", [128, 2, PAIRS])
        big3 = sb(nc, ctx, "big3", [128, 2, QC])
        TQ = [psum(nc, ctx, f"TQ{i}", [128, 512]) for i in range(2)]
        H = [psum(nc, ctx, f"H{i}", [128, 512]) for i in range(3)]
        O = [psum(nc, ctx, f"O{i}", [128, 512]) for i in range(2)]
        (wd_in, steps, reduced, magic_set, q_ready, w_ready, w_high, w_done, tq_ready, tq_high, tq_done, oq_steps, u_ready, h_ready, h_done, g_scaled, g_ready, u_scaled,
         sigmoid_done, s_scaled, gated, g2_scaled, o_scaled, oq_ready, o_ready, o_done, stored, q_steps,
         coef_ready, measured, found) = sems(
            nc, ctx, "wd_in", "steps6", "reduced", "magic_set", "q_ready", "w_ready6", "w_high", "w_done", "tq_ready",
            "tq_high", "tq_done", "oq_steps", "u_ready", "h_ready6",
            "h_done", "g_scaled", "g_ready", "u_scaled", "sigmoid_done", "s_scaled", "gated", "g2_scaled",
            "o_scaled", "oq_ready", "o_ready", "o_done", "stored", "q_steps", "coef_ready", "measured", "found")
        quant = Dequantise(nc, ctx, "wd_quant", KD * QI // 32)
        wd_blocks = wd.rearrange("p c k -> p (c k)").rearrange("p (b k) -> p b k", k=32)
        G, U = AG[:, 0:QC], AG[:, QC:2 * QC]
        S = AG[:, 2 * QC:2 * QC + 2]
        W_FILLS, D_FILLS, Q_FILLS = 4 * QC, KD, 4
        WB = TQ + O
        block = ctx.enter_context(nc.Block())

        def weight_fill(fill):
            if fill < W_FILLS:
                m, j = fill // 2, fill % 2
                return [w[:, 4 * j:4 * j + 4, 128 * m:128 * m + 128] for w in guT], 4
            c = fill - W_FILLS
            return [w[:, :, 128 * c:128 * c + 128] for w in wdT], QC

        def turned(fill, chunks):
            return WB[fill % len(WB)][:, 0:128 * chunks].rearrange("p (k n) -> p k n", k=chunks)

        def pair_fill(par, j):
            return [t[:, bass.ds(par, 1), 2 * j:2 * j + 2, :].rearrange("p b a n -> p (b a n)") for t in qT]

        def scales(dve, step, a, n):
            step(dve.tensor_scalar(sc[:, a:a + n], red[:, a:a + n], 1.0 / 32767.0, 1e-12, ALU.mult, ALU.max))
            step(dve.reciprocal(sc[:, a + 8:a + 8 + n], sc[:, a:a + n]))

        @block.gpsimd
        def _(pool):
            pool.memset(magic[:, :], MAGIC).then_inc(magic_set, 1)

            def reduce(n, a, k):
                pool.wait_ge(found, n + 1)
                pool.partition_all_reduce(red[:, a:a + k], big[:, a:a + k], 128, RMAX).then_inc(reduced, 1)

            reduce(0, 0, 1)
            quant.divide(pool, wd_blocks, 0)
            quant.multiply(pool, wd_blocks, 0)
            reduce(1, 1, 2)
            reduce(2, 3, 1)
            for c in range(QC):
                pool.wait_ge(u_scaled, c + 1)
                pool.tensor_scalar(U[:, c], U[:, c], -MAGIC, 32767.0, ALU.add, ALU.min).then_inc(u_ready, 1)
            reduce(3, 4, 1)

        @block.vector
        def _(dve):
            step = Steps(dve, steps, 0)

            def low_weights(fills):
                for fill in fills:
                    (high, low), chunks = weight_fill(fill)
                    dve.wait_ge(w_high, fill + 1)
                    dve.tensor_tensor(low, turned(fill, chunks), high.bitcast(F32), ALU.subtract).then_inc(w_done, 1)

            def low_pair(g, par):
                for j in range(Q_FILLS):
                    high, low = pair_fill(par, j)
                    wait_at(dve, tq_high, Q_FILLS * g + j + 1)
                    dve.tensor_tensor(low, TQ[j % 2][:, 0:2 * PAIR], high.bitcast(F32), ALU.subtract
                                      ).then_inc(tq_done, 1)

            def integers(g, between=()):
                if not isinstance(g, int) or g > 0:
                    wait_at(dve, tq_ready, Q_FILLS * g)
                lstep = Steps(dve, q_steps, 2 * g)
                for s in range(2):
                    ins = dve.tensor_scalar(q[:, s], tile_of(X, 2 * g + s), coef[:, 0, bass.ds(2 * g + s, 1)],
                                            coef[:, 1, bass.ds(2 * g + s, 1)], ALU.mult, ALU.add)
                lstep(ins)
                low_weights(between[0:2])
                for s in range(2):
                    ins = dve.tensor_scalar(q[:, s], q[:, s], MAGIC, None, ALU.add)
                lstep(ins)
                low_weights(between[2:4])
                dve.tensor_scalar(q[:, :, :].rearrange("p s d -> p (s d)"), q[:, :, :].rearrange("p s d -> p (s d)"),
                                  -MAGIC, 32767.0, ALU.add, ALU.min).then_inc(q_ready, 1)

            def measure(g):
                wait_at(dve, h_done, 3 * g + 6)
                dve.tensor_reduce(big2[:, :, bass.ds(g, 1)],
                                  AG[:, 0:2 * QC, bass.ds(PAIR * g, PAIR)].rearrange("p (a m) n -> p a m n", a=2),
                                  AX.XY, ALU.max, apply_absolute_value=True).then_inc(measured, 1)

            dve.tensor_reduce(big[:, 0:1], largest[:, :], AX.X, ALU.max).then_inc(found, 1)
            low_weights(range(0, 3))
            dve.wait_ge(reduced, 1)
            scales(dve, step, 0, 1)
            for k, c in ((0, scale5), (1, shift5)):
                ins = dve.tensor_scalar(coef[:, k], c[:, :], sc[0:P, 8:9], None, ALU.mult)
            ins.then_inc(coef_ready, 1)
            dve.wait_ge(coef_ready, 1)
            integers(0, range(3, 7))
            low_weights(range(7, W_FILLS))
            low_pair(0, 0)
            integers(1)
            low_pair(1, 1)
            integers(2)
            with dve.Fori(1, PAIRS - 2) as g:
                low_pair(g + 1, (g + 1) % 2)
                integers(g + 2)
                measure(g - 1)
            low_pair(PAIRS - 1, (PAIRS - 1) % 2)
            dve.wait_ge(wd_in, 16)
            quant.scales(dve, step, wd_blocks, 0)
            measure(PAIRS - 3)
            quant.round(dve, step, wd_blocks, 0)
            measure(PAIRS - 2)
            measure(PAIRS - 1)
            dve.wait_ge(measured, PAIRS)
            dve.tensor_reduce(big[:, 1:3], big2[:, :, :], AX.X, ALU.max).then_inc(found, 1)
            dve.wait_ge(reduced, 2)
            scales(dve, step, 1, 2)
            dve.sem_inc(coef_ready, 1)

            def gate_integers(c):
                dve.wait_ge(g_scaled, c + 1)
                dve.tensor_scalar(G[:, c], G[:, c], -MAGIC, 32767.0, ALU.add, ALU.min).then_inc(g_ready, 1)

            gate_integers(0)
            gate_integers(1)
            low_weights(range(W_FILLS, W_FILLS + D_FILLS // 2))
            for c in range(QC):
                dve.wait_ge(s_scaled, c + 1)
                s = S[:, c % 2]
                step(dve.tensor_scalar(s, s, -MAGIC, 65535.0, ALU.add, ALU.min))
                dve.scalar_tensor_tensor(G[:, c], s, 1.0 / 65536.0, G[:, c], ALU.mult, ALU.mult).then_inc(gated, 1)
                if c + 2 < QC:
                    gate_integers(c + 2)
                dve.wait_ge(gated, c + 1)
                step(dve.tensor_reduce(big3[:, 0, c:c + 1], G[:, c], AX.X, ALU.max, apply_absolute_value=True))
            step(dve.tensor_reduce(big[:, 6:7], big3[:, 0], AX.X, ALU.max))
            dve.tensor_tensor(big[:, 3:4], big[:, 6:7], sc[:, 1:2], ALU.mult).then_inc(found, 1)
            low_weights(range(W_FILLS + D_FILLS // 2, W_FILLS + D_FILLS))
            dve.wait_ge(reduced, 3)
            scales(dve, step, 3, 1)
            dve.tensor_tensor(sc[:, 7:8], sc[:, 1:2], sc[:, 11:12], ALU.mult).then_inc(coef_ready, 1)
            step(dve.tensor_tensor(sc[:, 5:6], sc[:, 3:4], sc[:, 2:3], ALU.mult))
            for c in range(QC):
                dve.wait_ge(g2_scaled, c + 1)
                step(dve.tensor_scalar(G[:, c], G[:, c], -MAGIC, 32767.0, ALU.add, ALU.min))
                dve.wait_ge(u_ready, c + 1)
                step(dve.tensor_tensor(G[:, c], G[:, c], U[:, c], ALU.mult))
                step(dve.tensor_reduce(big3[:, 1, c:c + 1], G[:, c], AX.X, ALU.max, apply_absolute_value=True))
            step(dve.tensor_reduce(big[:, 5:6], big3[:, 1], AX.X, ALU.max))
            dve.tensor_tensor(big[:, 4:5], big[:, 5:6], sc[:, 5:6], ALU.mult).then_inc(found, 1)
            dve.wait_ge(reduced, 4)
            scales(dve, step, 4, 1)
            dve.tensor_tensor(sc[:, 6:7], sc[:, 5:6], sc[:, 12:13], ALU.mult).then_inc(coef_ready, 1)

            def quantised(i, s):
                wait_at(dve, o_scaled, i + 1)
                wait_at(dve, o_ready, 2 * i + 2)
                part = Steps(dve, oq_steps, 2 * i)
                part(dve.tensor_scalar(oq[:, s], o_magic[:, s], -MAGIC, 32767.0, ALU.add, ALU.min))
                part(dve.tensor_copy(oq_parts[0][:, s], oq[:, s]))
                dve.tensor_tensor(oq_parts[1][:, s], oq[:, s], oq_parts[0][:, s].bitcast(F32), ALU.subtract
                                  ).then_inc(oq_ready, 1)

            def add_down(i):
                for half in range(2):
                    wait_at(dve, o_ready, 2 * i + half + 1 + 4)
                    t = tile_of(X, i)[:, 512 * half:512 * half + 512]
                    dve.scalar_tensor_tensor(t, O[half][0:P, :], sc[0:P, 4:5], t, ALU.mult, ALU.add
                                             ).then_inc(o_done, 1)

            quantised(0, 0)
            quantised(1, 1)
            with dve.Fori(0, PAIRS - 1) as g:
                for s in range(2):
                    add_down(2 * g + s)
                    quantised(2 * g + 2 + s, s)
            add_down(TILES - 2)
            add_down(TILES - 1)

        @block.scalar
        def _(act):
            def high_weights(fill):
                (high, low), chunks = weight_fill(fill)
                act.wait_ge(w_ready, fill + 1)
                act.activation(high, turned(fill, chunks), ACT.Copy).then_inc(w_high, 1)

            def evacuate(g, par, banks):
                if not isinstance(g, int):
                    wait_at(act, h_ready, 3 * g)
                for j in banks:
                    wait_at(act, tq_ready, Q_FILLS * g + j + 1)
                    act.activation(pair_fill(par, j)[0], TQ[j % 2][:, 0:2 * PAIR], ACT.Copy).then_inc(tq_high, 1)

            def products_out(g, j):
                wait_at(act, h_ready, 3 * g + j + 1 + 3)
                act.activation(AG[:, 2 * j:2 * j + 2, bass.ds(PAIR * g, PAIR)],
                               H[j][:, 0:2 * PAIR].rearrange("p (a n) -> p a n", a=2), ACT.Copy,
                               scale=sc[:, 0:1]).then_inc(h_done, 1)

            def in_steps(out, value, factor):
                return act.activation(out, value, ACT.Identity, scale=factor, bias=magic[:, :])

            for fill in range(W_FILLS):
                high_weights(fill)
            act.wait_ge(coef_ready, 1)
            evacuate(0, 0, range(Q_FILLS))
            with act.Fori(0, PAIRS - 1) as g:
                products_out(g, 0)
                evacuate(g + 1, (g + 1) % 2, (0, 1))
                products_out(g, 1)
                evacuate(g + 1, (g + 1) % 2, (2, 3))
                products_out(g, 2)
            for j in range(QC):
                products_out(PAIRS - 1, j)
            act.wait_ge(magic_set, 1)
            act.wait_ge(coef_ready, 2)

            def gate_steps(c):
                in_steps(G[:, c], G[:, c], sc[:, 9:10]).then_inc(g_scaled, 1)

            gate_steps(0)
            gate_steps(1)
            for fill in range(W_FILLS, W_FILLS + 2):
                high_weights(fill)
            for c in range(QC):
                act.wait_ge(g_ready, c + 1)
                if c >= 2:
                    act.wait_ge(gated, c - 1)
                act.activation(S[:, c % 2], G[:, c], ACT.Sigmoid, scale=sc[:, 1:2]).then_inc(sigmoid_done, 1)
                if c + 2 < QC:
                    gate_steps(c + 2)
                act.wait_ge(sigmoid_done, c + 1)
                in_steps(S[:, c % 2], S[:, c % 2], 65536.0).then_inc(s_scaled, 1)
                for fill in range(W_FILLS + 2 + 2 * c, W_FILLS + 4 + 2 * c):
                    high_weights(fill)
            for c in range(QC):
                in_steps(U[:, c], U[:, c], sc[:, 10:11]).then_inc(u_scaled, 1)
            act.wait_ge(coef_ready, 3)
            for c in range(QC):
                in_steps(G[:, c], G[:, c], sc[:, 7:8]).then_inc(g2_scaled, 1)
            act.wait_ge(coef_ready, 4)

            def down_steps(i, s):
                if not isinstance(i, int):
                    wait_at(act, oq_ready, i - 1)
                in_steps(o_magic[:, s], G[:, :, bass.ds(P * i, P)], sc[:, 6:7]).then_inc(o_scaled, 1)

            down_steps(0, 0)
            down_steps(1, 1)
            with act.Fori(1, PAIRS) as g:
                for s in range(2):
                    down_steps(2 * g + s, s)

        @block.tensor
        def _(pe):
            for free, n in ((w_done, len(WB)), (tq_done, 2), (h_done, 3), (h_ready, 3), (o_done, 2), (o_ready, 4)):
                pe.sem_inc(free, n)

            def turn_weights(w, at, fill, chunks):
                pe.wait_ge(w_done, fill + 1)
                for k in range(chunks):
                    ins = pe.transpose(WB[fill % len(WB)][:, 128 * k:128 * k + 128], w[:, at + 128 * k:at + 128 * k + 128],
                                       ident[:, :])
                ins.then_inc(w_ready, 1)

            def turn(g, banks):
                wait_at(pe, q_ready, g + 1)
                for j in banks:
                    wait_at(pe, tq_done, Q_FILLS * g + j + 1)
                    for c in range(2):
                        for s in range(2):
                            at, f = PAIR * c + P * s, 128 * (2 * j + c)
                            ins = pe.transpose(TQ[j % 2][:, at:at + P], q[:, s, f:f + 128], ident[0:P, 0:P])
                    ins.then_inc(tq_ready, 1)

            def products(g, par, more):
                wait_at(pe, tq_done, Q_FILLS * g + Q_FILLS + 2)
                for j in range(QC):
                    if more and j > 0:
                        turn(g + 1, (2 * j - 2, 2 * j - 1))
                    wait_at(pe, h_done, 3 * g + j + 1)
                    for m in range(2):
                        for k in range(KD):
                            for n, (a, b) in enumerate(PARTS):
                                w = guT[a][:, k, 128 * (2 * j + m):128 * (2 * j + m) + 128]
                                ins = pe.matmul(H[j][:, PAIR * m:PAIR * m + PAIR], w,
                                                qT[b][:, bass.ds(par, 1), k, :].rearrange("p a n -> p (a n)"),
                                                start=(k == 0 and n == 0), stop=(k == KD - 1 and n == 2))
                    ins.then_inc(h_ready, 1)

            for m in range(2 * QC):
                for j in range(2):
                    turn_weights(GU[:, m], 512 * j, 2 * m + j, 4)
            pe.wait_ge(w_done, W_FILLS + len(WB))
            turn(0, range(Q_FILLS))
            with pe.Fori(0, PAIRS - 1) as g:
                products(g, g % 2, True)
            products(PAIRS - 1, (PAIRS - 1) % 2, False)
            pe.wait_ge(quant.ready, 1)
            pe.wait_ge(tq_done, Q_FILLS * PAIRS + 2)
            for c in range(D_FILLS):
                turn_weights(wd[:, c], 0, W_FILLS + c, QC)
            pe.wait_ge(w_done, W_FILLS + D_FILLS + len(WB))
            with pe.Fori(0, PAIRS) as g:
                for s in range(2):
                    wait_at(pe, oq_ready, 2 * g + s + 1)
                    for half in range(2):
                        wait_at(pe, o_done, 4 * g + 2 * s + half + 1)
                        for k in range(QC):
                            for n, (a, b) in enumerate(PARTS):
                                ins = pe.matmul(O[half][0:P, :], oq_parts[a][:, s, k, :],
                                                wdT[b][:, k, 512 * half:512 * half + 512],
                                                start=(k == 0 and n == 0), stop=(k == QC - 1 and n == 2))
                        ins.then_inc(o_ready, 1)

        @block.sync
        def _(sp):
            sp.wait_ge(w_ready, W_FILLS)
            sp.dma_start(wd, w_down.rearrange("(c p) k -> p c k", p=128)).then_inc(wd_in, 16)
            with sp.Fori(0, PAIRS) as g:
                for s in range(2):
                    sp.wait_ge(o_done, 4 * g + 2 * s + 2 + 2)
                    sp.nop(nofuse=True)
                    sp.dma_start(out.rearrange("(t p) d -> p t d", p=P)[:, bass.ds(2 * g + s, 1), :],
                                 X[:, bass.ds(2 * g + s, 1), :]).then_inc(stored, 16)
            sp.wait_ge(stored, 16 * TILES)


def program(nc, a, out):
    with ExitStack() as top:
        ident = sb(nc, top, "ident", [128, 128])
        X = sb(nc, top, "X", [P, TILES, D])
        CT = sb(nc, top, "CT", [128, TILES, BLOCKS * WIN], I16)
        dinv, scale4, shift4, scale5, shift5 = (
            sb(nc, top, n, [P, TILES]) for n in ("dinv", "scale4", "shift4", "scale5", "shift5"))
        largest = sb(nc, top, "largest", [128, TILES])
        deg = sb(nc, top, "deg", [P, TILES])
        passes = sb(nc, top, "passes", [1, 1], I32)
        with ExitStack() as ctx:
            WT = sb(nc, ctx, "WT", [128, WCH, D])
            deg_dram = nc.dram_tensor("deg_dram", (BLOCKS * WIN,), F32).ap()
            build_matrices(nc, a["src"], a["dst"], a["edge_weight"], a["x"], X, ident, WT, CT, deg, dinv, deg_dram)
            layer0(nc, [a["L0_" + n] for n in LAYER0], X, ident, WT, scale4, shift4, deg, dinv, passes)
        AG = sb(nc, top, "AG", [128, KD, N])
        with ExitStack() as ctx:
            w1raw = sb(nc, ctx, "w1raw", [128, RAW, D])
            aggregate(nc, X, CT, w1raw, AG, scale4, shift4, passes, a["L1_gnn_W"], a["L1_ffn_w_gate"],
                      a["L1_ffn_w_up"])
            layer1_gnn(nc, X, quant_view(CT), w1raw, AG, dinv, scale5, shift5, largest, a["L1_gnn_W"], a["L1_gnn_b"])
        quantised_ffn(nc, X, quant_view(CT), AG, ident, scale5, shift5, largest, a["L1_ffn_w_down"], out)


def kernel(**inputs):
    import concourse.bacc as bacc
    from concourse.bass_utils import run_bass_kernel_spmd

    nc = bacc.Bacc("TRN2", target_bir_lowering=False, num_devices=1)
    arrays = {k: np.ascontiguousarray(v) for k, v in inputs.items()}
    args = {k: nc.dram_tensor(f"in_{k}", v.shape, mybir.dt.from_np(v.dtype), kind="ExternalInput").ap()
            for k, v in arrays.items()}
    out = nc.dram_tensor("out", (N, D), F32, kind="ExternalOutput").ap()
    program(nc, args, out)
    r = run_bass_kernel_spmd(nc, [{f"in_{k}": v for k, v in arrays.items()}], core_ids=[0])
    return r.results[0]["out"]
```

```python
from contextlib import ExitStack

import concourse.bass as bass
import numpy as np
from concourse import mybir

F32 = mybir.dt.float32
F32R = mybir.dt.float32r
BF16 = mybir.dt.bfloat16
F16 = mybir.dt.float16
I16 = mybir.dt.int16
U32 = mybir.dt.uint32
I32 = mybir.dt.int32
ALU = mybir.AluOpType
ACT = mybir.ActivationFunctionType
AX = mybir.AxisListType
RMAX = bass.bass_isa.ReduceOp.max

N = 1250
D = 1024
E = 21250
P = 125
TILES = N // P
PAIRS = TILES // 2
ET = E // P
EH = ET // 2
WIN = 32
BLOCKS = 40
CHUNKS = 10
WCH = D // 128
KD = D // 128
ENDS = 4
MIDDLE = 2
H1 = 256
M1 = 64
EX = 8
QI = 384
QC = QI // 128
PAIR = 2 * P
EPS = 1e-5
RAW = 2
LAYER0 = ("gnn_bias", "ffn_enc_W", "ffn_enc_b", "ffn_s2c_W", "ffn_s2c_b", "ffn_rW1", "ffn_rb1", "ffn_rW2",
          "ffn_rb2", "ffn_We1", "ffn_be1", "ffn_We2", "ffn_be2", "ffn_c2s_W", "ffn_c2s_b", "ffn_dec_W",
          "ffn_dec_b", "ffn_ln_g", "ffn_ln_b")
STEPS = 16
COUNT_PART = 4096
PARTS = ((0, 0), (1, 0), (0, 1))
MAGIC = 12582912.0


def wait_at(eng, sem, value):
    eng.wait_ge(sem, value)
    if not isinstance(value, int):
        eng.nop(nofuse=True)


class Steps:

    def __init__(self, eng, sem, base):
        self.eng, self.sem, self.base, self.n = eng, sem, base, 0

    def __call__(self, ins):
        ins.then_inc(self.sem, 1)
        self.n += 1
        wait_at(self.eng, self.sem, self.base + self.n)


def sb(nc, ctx, name, shape, dt=F32):
    return ctx.enter_context(nc.sbuf_tensor(name, shape, dt))


def psum(nc, ctx, name, shape, dt=F32):
    return ctx.enter_context(nc.psum_tensor(name, shape, dt))


def sems(nc, ctx, *names):
    return [ctx.enter_context(nc.semaphore(n)) for n in names]


def build_matrices(nc, src, dst, weight, x, X, ident, WT, ct_dram, deg, dinv, deg_dram):
    with ExitStack() as ctx:
        dst_i = sb(nc, ctx, "dst_i", [EH, 2, P], I32)
        src_i = sb(nc, ctx, "src_i", [EH, 2, P], I32)
        rows = sb(nc, ctx, "rows", [EH, 3, 2, P])
        record = sb(nc, ctx, "record", [P, ET, 4])
        coef = record[:, :, :].bitcast(BF16)[:, :, 4:8]
        weights = sb(nc, ctx, "weights", [P, ET])
        rest = sb(nc, ctx, "rest", [P, 2, ET])
        zeros = sb(nc, ctx, "zeros", [P, 128], BF16)
        iota_i = sb(nc, ctx, "iota_i", [P, BLOCKS * WIN], I32)
        iota_h = sb(nc, ctx, "iota_h", [P, BLOCKS * WIN], F16)
        first_i = sb(nc, ctx, "first_i", [EH, BLOCKS + 4], I32)
        first = sb(nc, ctx, "first", [EH, BLOCKS + 4])
        ends = sb(nc, ctx, "ends", [EH, 4])
        touch = sb(nc, ctx, "touch", [EH, 2, BLOCKS])
        marks = sb(nc, ctx, "marks", [EH, 4, BLOCKS])
        most = sb(nc, ctx, "most", [EH, 4, BLOCKS])
        span = sb(nc, ctx, "span", [1, 2, BLOCKS])
        table = sb(nc, ctx, "table", [1, BLOCKS, 2], I32)
        left = sb(nc, ctx, "left", [P, ENDS + MIDDLE, 128], BF16)
        right = sb(nc, ctx, "right", [P, ENDS + MIDDLE, N], BF16)
        block_out = sb(nc, ctx, "block_out", [128, 4, N])
        degrees = sb(nc, ctx, "degrees", [128, BLOCKS])
        parts = sb(nc, ctx, "parts", [128, 2, 3, D])
        counts = sb(nc, ctx, "counts", [128, 2, N])
        ct_stage = sb(nc, ctx, "ct_stage", [P, 2, TILES, 128], I16)
        eye = sb(nc, ctx, "eye", [WIN, 128], BF16)
        mhalf = sb(nc, ctx, "mhalf", [P, TILES])
        B = [psum(nc, ctx, f"B{i}", [128, 3 * 512]) for i in range(2)]
        TP = [psum(nc, ctx, f"TP{i}", [128, 512]) for i in range(2)]

        (edges_in, rows_ready, iota_ready, ident_ready, cols_turned, cols_ready, coef_ready, marks_ready,
         most_ready, table_ready, front_free, middle_free, back_free, front_ready, middle_ready,
         back_ready, block_built, block_copied, w_summed, w_high, w_split,
         turned, evacuated, loop_link, deg_out, deg_in, x_in) = sems(
            nc, ctx, "edges_in", "rows_ready", "iota_ready", "ident_ready", "cols_turned", "cols_ready",
            "coef_ready", "marks_ready", "most_ready", "table_ready", "front_free", "middle_free", "back_free",
            "front_ready", "middle_ready", "back_ready",
            "block_built", "block_copied", "w_summed", "w_high0", "w_split", "turned", "evacuated", "loop_link",
            "deg_out", "deg_in", "x_in")
        moved = [sems(nc, ctx, *(f"moved{par}{q}" for q in range(4))) for par in range(2)]
        dve_link, pool_link = sems(nc, ctx, "dve_link", "pool_link")
        ct_out = sems(nc, ctx, "ct_out0", "ct_out1")

        def chunk_pairs(eng, body):
            with eng.Fori(0, WCH // 2) as g:
                body(g, True, False)
            body(WCH // 2, False, True)

        def block_range(eng, registers, b):
            eng.load(registers, table[0:1, bass.ds(b, 1), :])
            return (eng.snap(registers[0], min_val=0, max_val=ET - ENDS - 1),
                    eng.snap(registers[1], min_val=ENDS + 1, max_val=ET))

        block = ctx.enter_context(nc.Block())

        @block.sync
        def _(sp):
            for tile, ap in ((dst_i, dst), (src_i, src)):
                sp.dma_start(tile[:, :, :], ap.rearrange("(h q k) -> q h k", h=2, k=P)).then_inc(edges_in, 16)
            sp.dma_start(rows[:, 2], weight.rearrange("(h q k) -> q h k", h=2, k=P)).then_inc(edges_in, 16)

            copied, split, read = (sp.alloc_register(n) for n in ("copied", "split", "read"))
            for register, value in ((copied, 3), (split, 1), (read, 3)):
                sp.reg_mov(register, value)

            def body(g, with_w, last):
                for par in range(2):
                    for q in range(4):
                        sp.wait_ge(block_copied, copied)
                        if q == 0:
                            sp.wait_ge(w_split, split)
                            sp.wait_ge(turned, read)
                        lanes = slice(32 * q, 32 * q + 32)
                        sp.dma_start(counts[lanes, par], block_out[0:32, q]).then_inc(moved[par][q], 16)
                        if with_w:
                            for k in range(3):
                                sp.dma_start(parts[lanes, par, k], block_out[32 * k + 32:32 * k + 64, q, 0:D]
                                             ).then_inc(moved[par][q], 16)
                        sp.reg_add(copied, copied, 1)
                        if q == 3:
                            sp.reg_add(split, split, 1)
                            sp.reg_add(read, read, 3)

            chunk_pairs(sp, body)
            sp.dma_start(deg_dram.rearrange("(b p) -> p b", p=WIN), degrees[0:32, :],
                         allow_slow_non_contiguous=True).then_inc(deg_out, 16)
            sp.wait_ge(deg_out, 16)
            sp.dma_start(deg[:, :], deg_dram[0:N].rearrange("(t p) -> p t", p=P),
                         allow_slow_non_contiguous=True).then_inc(deg_in, 16)
            sp.wait_ge(deg_in, 16)

        @block.gpsimd
        def _(pool):
            pool.memset(ident[:, :], 0.0).then_inc(pool_link, 1)
            pool.wait_ge(pool_link, 1)
            pool.affine_select(out=ident[:, :], in_=ident[:, :], compare_op=ALU.not_equal, fill=1.0, base=0,
                               pattern=[[-1, 128]], channel_multiplier=1).then_inc(ident_ready, 1)
            pool.iota(iota_i[:, :], [[1, BLOCKS * WIN]], base=0, channel_multiplier=0).then_inc(iota_ready, 1)
            pool.iota(first_i[:, 0:BLOCKS], [[WIN, BLOCKS]], base=0, channel_multiplier=0).then_inc(iota_ready, 1)
            pool.iota(first_i[:, BLOCKS:BLOCKS + 2], [[EH, 2]], base=1, channel_multiplier=1).then_inc(iota_ready, 1)
            pool.iota(first_i[:, BLOCKS + 2:], [[-EH, 2]], base=ET, channel_multiplier=-1).then_inc(iota_ready, 1)
            pool.memset(mhalf[:, :], -0.5).then_inc(iota_ready, 1)
            pool.wait_ge(marks_ready, 1)
            pool.partition_all_reduce(most[:, :, :], marks[:, :, :], EH, RMAX).then_inc(most_ready, 1)

            with pool.Fori(0, WCH // 2) as g:
                for par in range(2):
                    for q in range(4):
                        pool.wait_ge(moved[par][q], 64 * g + 64)
                    total = parts[:, par, 0]
                    pool.tensor_tensor(total, total, parts[:, par, 1], ALU.add).then_inc(loop_link, 1)
                    pool.wait_ge(loop_link, 2 * g + par + 1)
                    pool.tensor_tensor(total, total, parts[:, par, 2], ALU.add).then_inc(w_summed, 1)
            pool.wait_ge(deg_in, 16)
            pool.wait_ge(iota_ready, 5)
            pool.tensor_tensor(dinv[:, :], deg[:, :], mhalf[:, :], ALU.pow)

        @block.vector
        def _(dve):
            link = Steps(dve, dve_link, 0)
            dve.wait_ge(edges_in, 48)
            dve.tensor_copy(rows[:, 0], dst_i[:, :, :]).then_inc(rows_ready, 1)
            dve.tensor_copy(rows[:, 1], src_i[:, :, :]).then_inc(rows_ready, 1)
            dve.wait_ge(iota_ready, 4)
            dve.tensor_copy(iota_h[:, :], iota_i[:, :]).then_inc(dve_link, 1)
            link.n += 1
            dve.wait_ge(rows_ready, 1)
            link(dve.tensor_reduce(ends[:, 0:2], rows[:, 0], AX.X, ALU.min))
            link(dve.tensor_reduce(ends[:, 2:4], rows[:, 0], AX.X, ALU.max))
            link(dve.tensor_copy(first[:, :], first_i[:, :]))
            link(dve.tensor_scalar(ends[:, 0:2], ends[:, 0:2], -float(WIN), None, ALU.add))
            for h in range(2):
                link(dve.tensor_scalar(touch[:, h], first[:, 0:BLOCKS], ends[:, h:h + 1], None, ALU.is_gt))
                link(dve.scalar_tensor_tensor(touch[:, h], first[:, 0:BLOCKS], ends[:, 2 + h:3 + h], touch[:, h],
                                              ALU.is_le, ALU.mult))
                link(dve.tensor_scalar(marks[:, h], touch[:, h], first[:, BLOCKS + h:BLOCKS + h + 1], None,
                                       ALU.mult))
                ins = dve.tensor_scalar(marks[:, 2 + h], touch[:, h], first[:, BLOCKS + 2 + h:BLOCKS + 3 + h],
                                        None, ALU.mult)
                if h == 0:
                    link(ins)
            ins.then_inc(marks_ready, 1)
            dve.wait_ge(cols_turned, 1)
            dve.tensor_copy(weights[:, :], TP[0][0:P, 2 * ET:3 * ET]).then_inc(cols_ready, 1)
            for k in range(2):
                dve.tensor_copy(record[:, :, k], TP[0][0:P, k * ET:k * ET + ET]).then_inc(cols_ready, 1)
            dve.memset(coef[:, :, 0], 1.0).then_inc(coef_ready, 1)
            dve.memset(zeros[:, :], 0.0).then_inc(coef_ready, 1)
            dve.wait_ge(ident_ready, 1)
            dve.tensor_copy(eye[:, :], ident[0:WIN, :]).then_inc(coef_ready, 1)
            dve.wait_ge(cols_ready, 1)
            link(dve.tensor_copy(coef[:, :, 1], weights[:, :]))
            link(dve.tensor_tensor(rest[:, 0], weights[:, :], coef[:, :, 1], ALU.subtract))
            link(dve.tensor_copy(coef[:, :, 2], rest[:, 0]))
            link(dve.tensor_tensor(rest[:, 1], rest[:, 0], coef[:, :, 2], ALU.subtract))
            dve.tensor_copy(coef[:, :, 3], rest[:, 1]).then_inc(coef_ready, 1)
            dve.wait_ge(most_ready, 1)
            link(dve.tensor_tensor(span[:, 1], most[0:1, 0], most[0:1, 1], ALU.max))
            link(dve.tensor_tensor(span[:, 0], most[0:1, 2], most[0:1, 3], ALU.max))
            link(dve.tensor_scalar(span[:, 0], span[:, 0], -1.0, float(ET), ALU.mult, ALU.add))
            link(dve.tensor_scalar(span[:, 0], span[:, 0], float(ET - ENDS - 1), None, ALU.min))
            link(dve.scalar_tensor_tensor(span[:, 1], span[:, 0], float(ENDS + 1), span[:, 1], ALU.add, ALU.max))
            dve.tensor_copy(table[:, :, :].rearrange("a b k -> a k b"), span[:, :, :]).then_inc(table_ready, 1)
            dve.wait_ge(table_ready, 1)
            dve.wait_ge(coef_ready, 4)
            dve.wait_ge(cols_ready, 3)

            bounds = [dve.alloc_register(n) for n in ("made_lo", "made_hi")]
            made = dve.alloc_register("middles_made")
            dve.reg_mov(made, 0)

            def one_hots(b, slot, t):
                dve.scalar_tensor_tensor(
                    left[:, slot, :].rearrange("p a (k d) -> p (a k) d", k=4),
                    iota_h[:, bass.ds(WIN * b, WIN)].unsqueeze(1).broadcast_to([P, 4, WIN]),
                    record[:, bass.ds(t, 1), 0:1].rearrange("p a k -> p (a k)"),
                    coef[:, bass.ds(t, 1), :].rearrange("p a k -> p (a k)").unsqueeze(2).broadcast_to([P, 4, WIN]),
                    ALU.is_equal, ALU.mult)
                return dve.tensor_scalar(right[:, slot, :].rearrange("p a d -> p (a d)"), iota_h[:, 0:N],
                                         record[:, bass.ds(t, 1), 1:2].rearrange("p a k -> p (a k)"), None,
                                         ALU.is_equal)

            def one_hots_of(b):
                lo, hi = block_range(dve, bounds, b)
                dve.wait_ge(front_free, b + 1)
                one_hots(b, slice(0, 1), lo)
                one_hots(b, slice(1, 2), lo + 1).then_inc(front_ready, 1)
                with dve.Fori(lo + 2, hi - 2) as t:
                    n = dve.snap(made, min_val=0, max_val=BLOCKS * ET)
                    dve.wait_ge(middle_free, n + 1)
                    one_hots(b, bass.ds(n % MIDDLE + ENDS, 1), t).then_inc(middle_ready, 1)
                    dve.reg_add(made, made, 1)
                dve.wait_ge(back_free, b + 1)
                one_hots(b, slice(2, 3), hi - 2)
                one_hots(b, slice(3, 4), hi - 1).then_inc(back_ready, 1)

            for b in range(4):
                one_hots_of(b)
            with dve.Fori(0, WCH // 2) as g:
                for par in range(2):
                    for k in range(4):
                        one_hots_of(8 * g + 4 * par + 4 + k)
                    c = 2 * g + par
                    wait_at(dve, w_high, c + 1)
                    low, high = (w[:, bass.ds(c, 1), :].rearrange("p a d -> p (a d)") for w in (WT[1], WT[0]))
                    dve.tensor_tensor(low, parts[:, par, 0], high.bitcast(F32), ALU.subtract).then_inc(w_split, 1)
            for b in range(BLOCKS - 4, BLOCKS):
                one_hots_of(b)

        @block.tensor
        def _(pe):
            pe.sem_inc(front_free, 1)
            pe.sem_inc(middle_free, MIDDLE)
            pe.sem_inc(back_free, 1)
            for free in (block_copied, evacuated, w_split):
                pe.sem_inc(free, 2)
            for free in ct_out:
                pe.sem_inc(free, 16)
            pe.sem_inc(turned, 6)
            pe.wait_ge(edges_in, 48)
            pe.wait_ge(rows_ready, 2)
            pe.wait_ge(ident_ready, 1)
            for k in range(3):
                for h in range(2):
                    at = (2 * k + h) * EH
                    ins = pe.transpose(TP[0][0:P, at:at + EH], rows[:, k, h], ident[0:EH, 0:EH])
            ins.then_inc(cols_turned, 1)
            pe.wait_ge(cols_ready, 3)
            pe.wait_ge(coef_ready, 3)
            pe.wait_ge(table_ready, 1)
            bounds = [pe.alloc_register(n) for n in ("used_lo", "used_hi")]
            used = pe.alloc_register("middles_used")
            pe.reg_mov(used, 0)

            def products(out, slot, start=False, stop=False):
                lhs = left[:, slot, :].rearrange("p a d -> p (a d)")
                for at in range(0, N, 512):
                    size = min(512, N - at)
                    ins = pe.matmul(out[:, at:at + size], lhs,
                                    right[:, slot, at:at + size].rearrange("p a d -> p (a d)"), start=start, stop=stop)
                return ins

            def build(g, k):
                b, out = 8 * g + k, B[k % 2]
                lo, hi = block_range(pe, bounds, b)
                pe.wait_ge(block_copied, b + 1)
                pe.wait_ge(front_ready, b + 1)
                products(out, slice(0, 1), start=True)
                products(out, slice(1, 2)).then_inc(front_free, 1)
                width = min(WIN, N - WIN * b) if isinstance(b, int) else WIN
                pe.matmul(out[:, bass.ds(WIN * b, width)], eye[:, :], eye[:, 0:width], start=False, stop=False)
                with pe.Fori(lo + 2, hi - 2):
                    n = pe.snap(used, min_val=0, max_val=BLOCKS * ET)
                    pe.wait_ge(middle_ready, n + 1)
                    products(out, bass.ds(n % MIDDLE + ENDS, 1)).then_inc(middle_free, 1)
                    pe.reg_add(used, used, 1)
                pe.wait_ge(back_ready, b + 1)
                products(out, slice(2, 3))
                products(out, slice(3, 4), stop=True).then_inc(back_free, 1)
                pe.matmul(out[:, 1535:1536], zeros[:, :], zeros[:, 0:1], start=True, stop=True
                          ).then_inc(block_built, 1)

            def turn(g, par, per):
                for q in range(4):
                    pe.wait_ge(moved[par][q], per)
                for k in range(3):
                    pe.wait_ge(evacuated, 6 * g + 3 * par + k + 1)
                    for j in range(4 * k, min(4 * k + 4, TILES)):
                        ins = pe.transpose(TP[(k + par) % 2][0:P, 128 * (j % 4):128 * (j % 4) + 128],
                                           counts[:, par, P * j:P * j + P], ident[:, :])
                    ins.then_inc(turned, 1)

            def body(g, with_w, last):
                got = 64 * g + 64 if with_w else 64 * g + 16
                for k in (2, 3, 4, 5):
                    build(g, k)
                turn(g, 0, got)
                for k in (6, 7) + (() if last else (8, 9)):
                    build(g, k)
                turn(g, 1, got)

            build(0, 0)
            build(0, 1)
            chunk_pairs(pe, body)

        @block.scalar
        def _(act):
            for t in range(TILES):
                act.dma_start(X[:, t], x[P * t:P * t + P, :]).then_inc(x_in, 16)

            def copy(g, k, last_pair=False):
                b, q = 8 * g + k, k % 4
                act.wait_ge(block_built, b + 1)
                if k >= 8:
                    act.wait_ge(moved[1][q], 64 * g + 64)
                elif k >= 4:
                    act.wait_ge(moved[0][q], 64 * g + (64 if not last_pair else 16))
                act.activation(block_out[:, q], B[k % 2][:, 0:N], ACT.Identity,
                               accum_out=degrees[:, bass.ds(b, 1)]).then_inc(block_copied, 1)

            def evacuate(g, par):
                act.wait_ge(ct_out[par], 16 * g + 16)
                for k in range(3):
                    j, m = 4 * k, min(4, TILES - 4 * k)
                    act.wait_ge(turned, 6 * g + 3 * par + k + 7)
                    act.activation(ct_stage[:, par, j:j + m, :],
                                   TP[(k + par) % 2][0:P, 0:128 * m].rearrange("p (j d) -> p j d", j=m),
                                   ACT.Identity).then_inc(evacuated, 1)
                wait_at(act, evacuated, 6 * g + 3 * par + 5)
                act.dma_start(ct_dram[:, bass.ds(2 * g + par, 1), :],
                              ct_stage[:, par, :, :].rearrange("p (a j) d -> p a (j d)", a=1)).then_inc(ct_out[par], 16)

            def round_weights(g, par):
                c = 2 * g + par
                wait_at(act, w_summed, c + 1)
                act.activation(WT[0][:, bass.ds(c, 1), :].rearrange("p a d -> p (a d)"), parts[:, par, 0], ACT.Identity
                               ).then_inc(w_high, 1)

            def body(g, with_w, last):
                for k in (2, 3, 4, 5):
                    copy(g, k, last)
                evacuate(g, 0)
                if with_w:
                    round_weights(g, 0)
                for k in (6, 7) + (() if last else (8, 9)):
                    copy(g, k, last)
                evacuate(g, 1)
                if with_w:
                    round_weights(g, 1)

            copy(0, 0)
            copy(0, 1)
            chunk_pairs(act, body)
            act.wait_ge(x_in, 16 * TILES)
            for sem in ct_out:
                act.wait_ge(sem, 16 * (CHUNKS // 2) + 16)


def tile_of(X, i):
    return X[:, bass.ds(i, 1), :].rearrange("p a d -> p (a d)")


def layer0(nc, weights, X, ident, WT, scale4, shift4, deg, dinv, passes):
    (bias0, enc_W, enc_b, s2c_W, s2c_b, rW1, rb1, rW2, rb2, We1, be1, We2, be2, c2s_W, c2s_b,
     dec_W, dec_b, ln_g, ln_b) = weights
    with ExitStack() as ctx:
        encW = sb(nc, ctx, "encW", [128, KD, H1])
        decW = sb(nc, ctx, "decW", [128, 2, D])
        s2cW = sb(nc, ctx, "s2cW", [128, 2, M1])
        rW1s = sb(nc, ctx, "rW1s", [M1, M1])
        rW2s = sb(nc, ctx, "rW2s", [M1, EX])
        We1s = sb(nc, ctx, "We1s", [M1, EX, 128])
        We2s = sb(nc, ctx, "We2s", [128, EX, M1])
        c2sW = sb(nc, ctx, "c2sW", [M1, H1])
        encb = sb(nc, ctx, "encb", [128, 2])
        s2cb = sb(nc, ctx, "s2cb", [M1, 1])
        rb1s = sb(nc, ctx, "rb1s", [M1, 1])
        be1s = sb(nc, ctx, "be1s", [128, EX])
        c2sb = sb(nc, ctx, "c2sb", [128, 2])
        rb2r = sb(nc, ctx, "rb2r", [P, EX])
        be2r = sb(nc, ctx, "be2r", [P, EX * M1])
        bias0r = sb(nc, ctx, "bias0r", [P, D])
        decbr = sb(nc, ctx, "decbr", [P, D])
        lngr = sb(nc, ctx, "lngr", [P, D])
        lnbr = sb(nc, ctx, "lnbr", [P, D])
        xn1 = sb(nc, ctx, "xn1", [P, 2, D])
        xn2 = sb(nc, ctx, "xn2", [P, 2, D])
        xT1 = [sb(nc, ctx, n, [128, KD, PAIR], F32R) for n in ("xT1_high", "xT1_low")]
        xT2 = sb(nc, ctx, "xT2", [128, KD, PAIR])
        flatT = sb(nc, ctx, "flatT", [128, 2, PAIR])
        contT = sb(nc, ctx, "contT", [M1, PAIR])
        routT = sb(nc, ctx, "routT", [M1, PAIR])
        hT = sb(nc, ctx, "hT", [128, EX, PAIR])
        logits = sb(nc, ctx, "logits", [P, 2, EX])
        top8 = sb(nc, ctx, "top8", [P, 2, EX])
        top_i = sb(nc, ctx, "top_i", [P, 2, EX], U32)
        top_f = sb(nc, ctx, "top_f", [P, 2, EX])
        lead = sb(nc, ctx, "lead", [P, 2, 2])
        share = sb(nc, ctx, "share", [P, 2, 2])
        iota8i = sb(nc, ctx, "iota8i", [P, EX], I32)
        iota8 = sb(nc, ctx, "iota8", [P, EX])
        first = sb(nc, ctx, "first_gate", [P, 2, EX])
        gates = sb(nc, ctx, "gates", [P, 2, EX])
        moe = sb(nc, ctx, "moe", [P, 2, M1])
        dec = sb(nc, ctx, "dec", [P, 2, D])
        mixed, moeT, spikT = dec[:, :, 0:EX * M1], contT, flatT
        stats = sb(nc, ctx, "stats", [P, 4, 2, 2, 6])
        mv = sb(nc, ctx, "mv", [P, 4, 2, 2])
        veps = sb(nc, ctx, "veps", [P, 4, 2])
        rstd = sb(nc, ctx, "rstd", [P, 4, 2])
        mhalf = sb(nc, ctx, "mhalf2", [P, 2])
        deg_most = sb(nc, ctx, "deg_most", [P, TILES])
        most = sb(nc, ctx, "most_parts", [1, 1])
        nmean = sb(nc, ctx, "nmean", [P, 2])
        spare = sb(nc, ctx, "spare", [1, 2])
        TR = [psum(nc, ctx, f"TR{i}", [128, 512]) for i in range(2)]
        Y = [psum(nc, ctx, f"Y{i}", [128, 512]) for i in range(2)]
        DP = [psum(nc, ctx, f"DP{i}", [128, 512]) for i in range(2)]
        F = [psum(nc, ctx, f"F{i}", [128, 512]) for i in range(2)]
        (w_in, consts, tr_ready, y_ready, y_free, f_ready, lead_ready, share_ready, moe_ready,
         dec_ready, dec_free, dec_done, x_biased, x_shifted, scaled, pool_steps,
         steps_first, steps_loop, steps_last, deg_found, parts_steps, rows_in) = sems(
            nc, ctx, "w_in", "consts", "tr_ready", "y_ready", "y_free", "f_ready", "lead_ready",
            "share_ready", "moe_ready", "dec_ready", "dec_free", "dec_done", "x_biased", "x_shifted", "scaled",
            "pool_steps", "steps_first", "steps_loop", "steps_last",
            "deg_found", "parts_steps", "rows_in")
        f_done = sems(nc, ctx, "f_done0", "f_done1")
        xn1_high = sems(nc, ctx, "xn1_high")[0]
        tr_free = sems(nc, ctx, "xn1_turned", "xn2_turned")
        xn_ready = sems(nc, ctx, "xn1_ready", "xn2_ready")
        var_ready = sems(nc, ctx, *(f"var_ready{k}" for k in range(1, 5)))
        rstd_ready = sems(nc, ctx, *(f"rstd_ready{k}" for k in range(1, 5)))
        LAST = PAIRS - 1
        LOADS = 17

        def pairs(eng, prologue, body):
            prologue()
            with eng.Fori(0, LAST - 1) as p:
                body(p, p + 1, p + 2)
            body(LAST - 1, LAST, None)
            body(LAST, None, None)

        def is_first(p):
            return isinstance(p, int) and p == 0

        def fill(p, k):
            return 8 * p + 4 * (k - 1)

        block = ctx.enter_context(nc.Block())

        @block.sync
        def _(sp):
            loads = []

            def load(tile, ap, slow=False, sem=w_in):
                loads.append(1)
                sp.dma_start(tile, ap, allow_slow_non_contiguous=slow).then_inc(sem, 16)

            def row(v, n):
                return v.rearrange("(a n) -> a n", a=1).broadcast_to([P, n])

            load(bias0r[:, :], row(bias0, D), sem=rows_in)
            load(lnbr[:, :], row(ln_b, D), sem=rows_in)
            load(encW[:, :, :], enc_W.rearrange("(k p) m -> p k m", p=128))
            load(encb[:, :], enc_b.rearrange("(c p) -> p c", p=128), True)
            load(s2cW[:, :, :], s2c_W.rearrange("(k p) m -> p k m", p=128))
            load(s2cb[:, :], s2c_b.rearrange("(p a) -> p a", a=1), True)
            load(rW1s[:, :], rW1)
            load(rb1s[:, :], rb1.rearrange("(p a) -> p a", a=1), True)
            load(rW2s[:, :], rW2)
            load(rb2r[:, :], row(rb2, EX))
            load(We1s[:, :, :], We1.rearrange("e m h -> m e h"))
            load(be1s[:, :], be1.rearrange("e h -> h e"), True)
            load(We2s[:, :, :], We2.rearrange("e h m -> h e m"))
            load(be2r[:, :], row(be2.rearrange("e m -> (e m)"), EX * M1))
            load(c2sW[:, :], c2s_W)
            load(c2sb[:, :], c2s_b.rearrange("(c p) -> p c", p=128), True)
            load(decW[:, :, :], dec_W.rearrange("(k p) d -> p k d", p=128))
            load(decbr[:, :], row(dec_b, D))
            load(lngr[:, :], row(ln_g, D))
            assert len(loads) == LOADS + 2
            sp.wait_ge(rows_in, 32)
            sp.wait_ge(w_in, 16 * LOADS)

        @block.tensor
        def _(pe):
            for free, n in ((y_free, 2), (dec_free, 2), (f_done[0], 1), (f_done[1], 1), (f_ready, 12)):
                pe.sem_inc(free, n)

            def turn(p, k, banks=range(4)):
                xn = (xn1, xn2)[k - 1]
                wait_at(pe, xn_ready[k - 1], p + 1)
                for j in banks:
                    if j >= 2:
                        wait_at(pe, tr_free[k - 1], 4 * p + j - 1)
                    elif k == 2:
                        wait_at(pe, tr_free[0], 4 * p + j + 3)
                    elif not is_first(p):
                        wait_at(pe, tr_free[1], 4 * p + j - 1)
                    for c in range(2):
                        for s in range(2):
                            at, f = PAIR * c + P * s, 128 * (2 * j + c)
                            ins = pe.transpose(TR[j % 2][:, at:at + P], xn[:, s, f:f + 128], ident[0:P, 0:P])
                    ins.then_inc(tr_ready, 1)

            def gnn(p, part):
                s, half = part // 2, part % 2
                if part == 0:
                    wait_at(pe, tr_free[0], 4 * p + 4)
                wait_at(pe, y_free, 4 * p + part + 1)
                for k in range(KD):
                    for m, (a, b) in enumerate(PARTS):
                        ins = pe.matmul(Y[half][0:P, :], xT1[a][:, k, P * s:P * s + P],
                                        WT[b][:, k, 512 * half:512 * half + 512],
                                        start=(k == 0 and m == 0), stop=(k == KD - 1 and m == 2))
                ins.then_inc(y_ready, 1)

            def use(p, u):
                wait_at(pe, f_done[u % 2], 6 * p + u // 2 + 1)
                return F[u % 2]

            def left_bank(p, u):
                wait_at(pe, f_done[u % 2], 6 * p + u // 2 + 2)

            def prologue():
                turn(0, 1)
                for part in range(4):
                    gnn(0, part)

            def body(p, n, m):
                turn(p, 2)
                if n is not None:
                    turn(n, 1, (0, 1))
                pe.wait_ge(w_in, 16 * LOADS)
                wait_at(pe, tr_free[1], 4 * p + 4)
                f = use(p, 0)
                for m in range(2):
                    if m == 1 and n is not None:
                        turn(n, 1, (2, 3))
                    for k in range(KD):
                        ins = pe.matmul(f[:, PAIR * m:PAIR * m + PAIR], encW[:, k, 128 * m:128 * m + 128], xT2[:, k, :],
                                        start=(k == 0), stop=(k == KD - 1))
                ins.then_inc(f_ready, 1)
                if n is not None:
                    gnn(n, 0)
                left_bank(p, 0)
                f = use(p, 1)
                for k in range(2):
                    ins = pe.matmul(f[0:M1, 0:PAIR], s2cW[:, k, :], flatT[:, k, :], start=(k == 0), stop=(k == 1))
                ins.then_inc(f_ready, 1)
                if n is not None:
                    gnn(n, 1)
                left_bank(p, 1)
                f = use(p, 2)
                pe.matmul(f[0:M1, 0:PAIR], rW1s[:, :], contT[:, :], start=True, stop=True).then_inc(f_ready, 1)
                for u in range(4):
                    f = use(p, 3 + u)
                    for e in range(2):
                        ins = pe.matmul(f[:, PAIR * e:PAIR * e + PAIR], We1s[:, 2 * u + e, :], contT[:, :],
                                        start=True, stop=True)
                    ins.then_inc(f_ready, 1)
                left_bank(p, 2)
                f = use(p, 7)
                for s in range(2):
                    ins = pe.matmul(f[0:P, EX * s:EX * s + EX], routT[:, P * s:P * s + P], rW2s[:, :],
                                    start=True, stop=True)
                ins.then_inc(f_ready, 1)
                left_bank(p, 5)
                left_bank(p, 6)
                for s in range(2):
                    f = use(p, 8 + s)
                    for e in range(EX):
                        ins = pe.matmul(f[0:P, M1 * e:M1 * e + M1], hT[:, e, P * s:P * s + P], We2s[:, e, :],
                                        start=True, stop=True)
                    ins.then_inc(f_ready, 1)
                if n is not None:
                    gnn(n, 2)
                wait_at(pe, moe_ready, 2 * p + 2)
                f = use(p, 10)
                for s in range(2):
                    ins = pe.transpose(f[0:M1, P * s:P * s + P], moe[:, s, :], ident[0:P, 0:P])
                ins.then_inc(f_ready, 1)
                if n is not None:
                    gnn(n, 3)
                left_bank(p, 10)
                f = use(p, 11)
                for m in range(2):
                    ins = pe.matmul(f[:, PAIR * m:PAIR * m + PAIR], c2sW[:, 128 * m:128 * m + 128], moeT[:, :],
                                    start=True, stop=True)
                ins.then_inc(f_ready, 1)
                left_bank(p, 11)
                for part in range(4):
                    s, half = part // 2, part % 2
                    wait_at(pe, dec_free, 4 * p + part + 1)
                    for k in range(2):
                        ins = pe.matmul(DP[half][0:P, :], spikT[:, k, P * s:P * s + P],
                                        decW[:, k, 512 * half:512 * half + 512], start=(k == 0), stop=(k == 1))
                    ins.then_inc(dec_ready, 1)

            pairs(pe, prologue, body)

        @block.scalar
        def _(act):

            def round_xn1(p):
                if not is_first(p):
                    wait_at(act, y_ready, 4 * p)
                for j in range(4):
                    wait_at(act, tr_ready, fill(p, 1) + j + 1)
                    act.activation(xT1[0][:, 2 * j:2 * j + 2, :].rearrange("p a n -> p (a n)"),
                                   TR[j % 2][:, 0:2 * PAIR], ACT.Identity).then_inc(xn1_high, 1)

            def computed(p, u):
                wait_at(act, f_ready, 12 * p + u + 13)
                return F[u % 2]

            def take_sigmoids():
                act.activation(spare[:, 1:2], spare[:, 0:1], ACT.Sigmoid)

            def prologue():
                act.wait_ge(consts, 2)
                take_sigmoids()
                round_xn1(0)

            def body(p, n, m):
                take_sigmoids()
                if n is not None:
                    round_xn1(n)
                act.wait_ge(w_in, 16 * LOADS)
                f = computed(p, 0)
                for m in range(2):
                    ins = act.activation(flatT[:, m, :], f[:, PAIR * m:PAIR * m + PAIR], ACT.Sigmoid,
                                         bias=encb[:, m:m + 1])
                ins.then_inc(f_done[0], 1)
                f = computed(p, 1)
                act.activation(contT[:, :], f[0:M1, 0:PAIR], ACT.Identity, bias=s2cb[:, :]).then_inc(f_done[1], 1)
                f = computed(p, 2)
                act.activation(routT[:, :], f[0:M1, 0:PAIR], ACT.Tanh, bias=rb1s[:, :]).then_inc(f_done[0], 1)
                for u in range(4):
                    f = computed(p, 3 + u)
                    for e in range(2):
                        ins = act.activation(hT[:, 2 * u + e, :], f[:, PAIR * e:PAIR * e + PAIR], ACT.Relu,
                                             bias=be1s[:, 2 * u + e:2 * u + e + 1])
                    ins.then_inc(f_done[(3 + u) % 2], 1)
                wait_at(act, lead_ready, p + 1)
                act.activation(share[:, :, :], lead[:, :, :], ACT.Sigmoid).then_inc(share_ready, 1)
                f = computed(p, 11)
                for m in range(2):
                    ins = act.activation(spikT[:, m, :], f[:, PAIR * m:PAIR * m + PAIR], ACT.Sigmoid,
                                         bias=c2sb[:, m:m + 1])
                ins.then_inc(f_done[1], 1)
                for part in range(4):
                    wait_at(act, dec_free, 4 * p + part + 3)
                    at = dec[:, part // 2, 512 * (part % 2):512 * (part % 2) + 512]
                    act.activation(at, at, ACT.Sigmoid).then_inc(dec_done, 1)

            pairs(act, prologue, body)

        @block.gpsimd
        def _(pool):
            pool.memset(mhalf[:, :], -0.5).then_inc(consts, 1)
            pool.memset(spare[:, 0:1], 0.0)
            pool.iota(iota8i[:, :], [[1, EX]], base=0, channel_multiplier=0).then_inc(consts, 1)
            pool.partition_all_reduce(deg_most[:, :], deg[:, :], P, RMAX).then_inc(deg_found, 1)
            pool.wait_ge(consts, 2)

            def inverse_root(p, k):
                wait_at(pool, var_ready[k - 1], p + 1)
                return pool.tensor_tensor(rstd[:, k - 1], veps[:, k - 1], mhalf[:, :], ALU.pow)

            def first_norm(p, k):
                vector, added = ((bias0r, x_biased), (lnbr, x_shifted))[k - 1]
                inverse_root(p, k).then_inc(rstd_ready[k - 1], 1)
                wait_at(pool, xn_ready[k - 1], p + 1)
                if is_first(p):
                    pool.wait_ge(rows_in, 32)
                for s in range(2):
                    t = tile_of(X, 2 * p + s)
                    ins = pool.tensor_tensor(t, t, vector[:, :], ALU.add)
                ins.then_inc(added, 1)

            def prologue():
                first_norm(0, 1)
                first_norm(1, 1)
                first_norm(0, 2)

            def body(p, n, m):
                if m is not None:
                    first_norm(m, 1)
                if n is not None:
                    first_norm(n, 2)
                inverse_root(p, 3).then_inc(rstd_ready[2], 1)
                inverse_root(p, 4).then_inc(pool_steps, 1)
                pool.tensor_scalar(nmean[:, :], mv[:, 3, :, 0], -1.0, None, ALU.mult).then_inc(pool_steps, 1)
                wait_at(pool, pool_steps, 3 * p + 2)
                pool.tensor_tensor(scale4[:, bass.ds(2 * p, 2)], rstd[:, 3], dinv[:, bass.ds(2 * p, 2)], ALU.mult
                                   ).then_inc(pool_steps, 1)
                wait_at(pool, pool_steps, 3 * p + 3)
                pool.tensor_tensor(shift4[:, bass.ds(2 * p, 2)], nmean[:, :], scale4[:, bass.ds(2 * p, 2)], ALU.mult
                                   ).then_inc(scaled, 1)

            pairs(pool, prologue, body)

        @block.vector
        def _(dve):
            dve.wait_ge(consts, 2)
            dve.tensor_copy(iota8[:, :], iota8i[:, :]).then_inc(consts, 1)
            dve.wait_ge(consts, 3)

            def norm(step, p, k, rows, ready=None):
                k -= 1
                for s in range(2):
                    if ready is not None:
                        ready(s)
                    for half in range(2):
                        ins = dve.bn_stats(stats[:, k, s, half], rows(s)[:, 512 * half:512 * half + 512])
                step(ins)
                for s in range(2):
                    ins = dve.bn_aggr(mv[:, k, s], stats[:, k, s].rearrange("p a b -> p (a b)"))
                step(ins)
                dve.tensor_scalar(veps[:, k], mv[:, k, :, 1], EPS, None, ALU.add).then_inc(var_ready[k], 1)

            def apply(p, k, s, out, rows):
                return dve.tensor_scalar(out, rows, mv[:, k - 1, s, 0:1], rstd[:, k - 1, s:s + 1],
                                         ALU.subtract, ALU.mult)

            def normalise(step, p, k, meanwhile=None):
                xn = (xn1, xn2)[k - 1]
                norm(step, p, k, lambda s: tile_of(X, 2 * p + s))
                if meanwhile is not None:
                    meanwhile()
                if not is_first(p):
                    wait_at(dve, tr_ready, fill(p, k) - 4)
                wait_at(dve, rstd_ready[k - 1], p + 1)
                for s in range(2):
                    ins = apply(p, k, s, xn[:, s, :], tile_of(X, 2 * p + s))
                ins.then_inc(xn_ready[k - 1], 1)

            def add_gnn(p, part):
                s, half = part // 2, part % 2
                wait_at(dve, y_ready, 4 * p + part + 1)
                if part == 0:
                    wait_at(dve, x_biased, p + 1)
                t = tile_of(X, 2 * p + s)[:, 512 * half:512 * half + 512]
                return dve.tensor_tensor(t, Y[half][0:P, :], t, ALU.add).then_inc(y_free, 1)

            def added(p):
                wait_at(dve, y_free, 4 * p + 4 + 2)

            def computed(p, u):
                wait_at(dve, f_ready, 12 * p + u + 13)
                return F[u % 2]

            def remainder_xn1(p):
                for j in range(4):
                    high, low = (t[:, 2 * j:2 * j + 2, :].rearrange("p a n -> p (a n)") for t in xT1)
                    wait_at(dve, xn1_high, 4 * p + j + 1)
                    dve.tensor_tensor(low, TR[j % 2][:, 0:2 * PAIR], high.bitcast(F32), ALU.subtract
                                      ).then_inc(tr_free[0], 1)

            def evacuate_xn2(p):
                wait_at(dve, f_ready, 12 * p + 1)
                for j in range(4):
                    wait_at(dve, tr_ready, fill(p, 2) + j + 1)
                    dve.tensor_copy(xT2[:, 2 * j:2 * j + 2, :].rearrange("p a n -> p (a n)"),
                                    TR[j % 2][:, 0:2 * PAIR]).then_inc(tr_free[1], 1)

            def prologue():
                step = Steps(dve, steps_first, 0)
                normalise(step, 0, 1)
                remainder_xn1(0)
                normalise(step, 1, 1)
                for part in range(4):
                    add_gnn(0, part)
                added(0)
                normalise(step, 0, 2)
                evacuate_xn2(0)
                remainder_xn1(1)

            def decoded(p, quarters):
                for part in quarters:
                    s, half = part // 2, part % 2
                    wait_at(dve, dec_ready, 4 * p + part + 1)
                    dve.tensor_tensor(dec[:, s, 512 * half:512 * half + 512], DP[half][0:P, :],
                                      decbr[:, 512 * half:512 * half + 512], ALU.add).then_inc(dec_free, 1)

            def body(p, n, m):
                step = last_step if m is None else Steps(dve, steps_loop, STEPS * p)
                if n is not None:
                    add_gnn(n, 0)
                if m is not None:
                    normalise(step, m, 1)
                if n is not None:
                    add_gnn(n, 1)
                dve.wait_ge(w_in, 16 * LOADS)
                f = computed(p, 7)
                dve.tensor_tensor(logits[:, :, :], f[0:P, 0:2 * EX].rearrange("p (s e) -> p s e", s=2),
                                  rb2r[:, :].unsqueeze(1).broadcast_to([P, 2, EX]), ALU.add).then_inc(f_done[1], 1)
                wait_at(dve, f_done[1], 6 * p + 3 + 2)
                for s in range(2):
                    ins = dve.max(top8[:, s], logits[:, s])
                step(ins)
                for s in range(2):
                    last_index = dve.max_index(top_i[:, s], top8[:, s], logits[:, s])
                step(last_index)
                dve.tensor_tensor(lead[:, :, 0], top8[:, :, 0], top8[:, :, 1], ALU.subtract)
                dve.tensor_tensor(lead[:, :, 1], top8[:, :, 1], top8[:, :, 0], ALU.subtract).then_inc(lead_ready, 1)
                step(dve.tensor_copy(top_f[:, :, :], top_i[:, :, :]))
                wait_at(dve, share_ready, p + 1)
                for s in range(2):
                    for out, k in ((first, 0), (gates, 1)):
                        ins = dve.tensor_scalar(out[:, s], iota8[:, :], top_f[:, s, k:k + 1], share[:, s, k:k + 1],
                                                ALU.is_equal, ALU.mult)
                step(ins)
                step(dve.tensor_tensor(gates[:, :, :], gates[:, :, :], first[:, :, :], ALU.add))
                for s in range(2):
                    f = computed(p, 8 + s)
                    ins = dve.tensor_tensor(mixed[:, s], f[0:P, :], be2r[:, :], ALU.add).then_inc(f_done[s], 1)
                wait_at(dve, f_done[0], 6 * p + 4 + 2)
                wait_at(dve, f_done[1], 6 * p + 4 + 2)
                for s in range(2):
                    mix = mixed[:, s].rearrange("p (e m) -> p e m", e=EX)
                    ins = dve.tensor_tensor(mix, mix, gates[:, s].unsqueeze(2).broadcast_to([P, EX, M1]), ALU.mult)
                step(ins)
                for s in range(2):
                    dve.tensor_reduce(moe[:, s], mixed[:, s].rearrange("p (e m) -> p m e", e=EX), AX.X, ALU.add
                                      ).then_inc(moe_ready, 1)
                if n is not None:
                    add_gnn(n, 2)
                f = computed(p, 10)
                dve.tensor_copy(moeT[:, :], f[0:M1, 0:PAIR]).then_inc(f_done[0], 1)
                if n is not None:
                    add_gnn(n, 3)
                    added(n)
                    normalise(step, n, 2, lambda: decoded(p, (0, 1)))
                else:
                    decoded(p, (0, 1))
                decoded(p, (2, 3))
                if n is not None:
                    evacuate_xn2(n)
                if m is not None:
                    remainder_xn1(m)
                norm(step, p, 3, lambda s: dec[:, s, :], lambda s: wait_at(dve, dec_done, 4 * p + 2 * s + 2))
                for s in range(2):
                    ins = dve.scalar_tensor_tensor(dec[:, s, :], dec[:, s, :], mv[:, 2, s, 0:1], lngr[:, :],
                                                   ALU.subtract, ALU.mult)
                step(ins)
                wait_at(dve, rstd_ready[2], p + 1)
                wait_at(dve, x_shifted, p + 1)
                for s in range(2):
                    t = tile_of(X, 2 * p + s)
                    ins = dve.scalar_tensor_tensor(t, dec[:, s, :], rstd[:, 2, s:s + 1], t, ALU.mult, ALU.add)
                step(ins)
                norm(step, p, 4, lambda s: tile_of(X, 2 * p + s))
                assert m is None or step.n == STEPS, step.n

            last_step = Steps(dve, steps_last, 0)
            pairs(dve, prologue, body)
            dve.wait_ge(deg_found, 1)
            parts = Steps(dve, parts_steps, 0)
            parts(dve.tensor_reduce(most[:, :], deg_most[0:1, :], AX.X, ALU.max))
            parts(dve.tensor_scalar(most[:, :], most[:, :], 0.5 + float(COUNT_PART), None, ALU.is_gt))
            parts(dve.tensor_scalar(most[:, :], most[:, :], 1.0, None, ALU.add))
            parts(dve.tensor_copy(passes[:, :], most[:, :]))
            dve.wait_ge(scaled, PAIRS)


def quant_view(CT):
    place = CT[:, :, :, :].rearrange("p c t d -> p (c t d)").bitcast(F32)
    return place[:, 0:2 * QC * D].rearrange("p (m d) -> p m d", d=D)


class Dequantise:

    def __init__(self, nc, ctx, name, blocks):
        self.buf = sb(nc, ctx, name, [128, 3, blocks])
        self.shape = [128, blocks, 32]
        self.scales_ready, self.divided, self.rounded, self.ready = sems(
            nc, ctx, *(name + n for n in ("_scales", "_divided", "_rounded", "_ready")))

    def scales(self, dve, step, w, n):
        if not isinstance(n, int) or n > 0:
            wait_at(dve, self.ready, n)
        step(dve.tensor_reduce(self.buf[:, 0], w, AX.X, ALU.max, apply_absolute_value=True))
        step(dve.tensor_scalar(self.buf[:, 1], self.buf[:, 0], 1.0 / 7.0, 1e-12, ALU.mult, ALU.max))
        dve.reciprocal(self.buf[:, 2], self.buf[:, 1]).then_inc(self.scales_ready, 1)

    def divide(self, pool, w, n):
        wait_at(pool, self.scales_ready, n + 1)
        pool.tensor_tensor(w, w, self.buf[:, 2].unsqueeze(2).broadcast_to(self.shape), ALU.mult
                           ).then_inc(self.divided, 1)

    def round(self, dve, step, w, n):
        wait_at(dve, self.divided, n + 1)
        step(dve.tensor_scalar(w, w, MAGIC, None, ALU.add))
        dve.tensor_scalar(w, w, -MAGIC, 7.0, ALU.add, ALU.min).then_inc(self.rounded, 1)

    def multiply(self, pool, w, n):
        wait_at(pool, self.rounded, n + 1)
        pool.tensor_tensor(w, w, self.buf[:, 1].unsqueeze(2).broadcast_to(self.shape), ALU.mult
                           ).then_inc(self.ready, 1)


def counts_of(CT, i):
    return CT[0:P, :, i, :]


def chunk_products(pe, out, high, low, counts, before=None):
    for i in range(TILES):
        if before is not None:
            before(i)
        row = counts[:, i, :, :].rearrange("p c d -> p (c d)")
        for part in (high, low):
            for at in range(0, N, 512):
                size = min(512, N - at)
                ins = pe.matmul(out[:, at:at + size], part[:, i, :], row[:, at:at + size],
                                start=(i == 0 and part is high), stop=(i == TILES - 1 and part is low))
    return ins


def aggregate_rest(nc, X, CT, ct_dram, AG, CTf, high, low, A, value, scale4, shift4, passes):
    with ExitStack() as ctx:
        rest_in, rest_steps, rest_staged, rest_done = sems(nc, ctx, "rest_in", "rest_steps", "rest_staged", "rest_done")
        block = ctx.enter_context(nc.Block())

        def if_needed(eng):
            needed = eng.alloc_register("passes_needed")
            eng.reg_load(needed, passes[0:1, 0:1])
            return eng.If_ne(needed, 1)

        @block.sync
        def _(sp):
            with if_needed(sp):
                sp.dma_start(CT[0:P, :, :, :].rearrange("p c t d -> p c (t d)"), ct_dram).then_inc(rest_in, 16)
                sp.wait_ge(rest_in, 16)

        @block.vector
        def _(dve):
            with if_needed(dve):
                dve.wait_ge(rest_in, 16)
                step = Steps(dve, rest_steps, 0)
                for i in range(TILES):
                    step(dve.tensor_copy(CTf[:, i], counts_of(CT, i)))
                    step(dve.tensor_tensor(CTf[:, i], counts_of(CT, i), CTf[:, i].bitcast(F32), ALU.subtract))
                with dve.Fori(0, KD) as f:
                    step = Steps(dve, rest_steps, 2 * TILES + 4 * f)
                    step(dve.tensor_tensor(value, X[:, :, bass.ds(128 * f, 128)],
                                           scale4[:, :].unsqueeze(2).broadcast_to([P, TILES, 128]), ALU.mult))
                    step(dve.tensor_tensor(value, value, shift4[:, :].unsqueeze(2).broadcast_to([P, TILES, 128]),
                                           ALU.add))
                    step(dve.tensor_copy(high[:, 0], value))
                    step(dve.tensor_tensor(low[:, 0], value, high[:, 0].bitcast(F32), ALU.subtract))
                    dve.sem_inc(rest_staged, 1)
                    wait_at(dve, rest_done, 2 * f + 1)
                    dve.tensor_copy(AG[:, bass.ds(f, 1), :].rearrange("p a n -> p (a n)"), A[0][:, 0:N]
                                    ).then_inc(rest_done, 1)
                    wait_at(dve, rest_done, 2 * f + 2)

        @block.tensor
        def _(pe):
            with if_needed(pe):
                with pe.Fori(0, KD) as f:
                    wait_at(pe, rest_staged, f + 1)
                    chunk_products(pe, A[0], high[:, 0], low[:, 0], CTf).then_inc(rest_done, 1)


def aggregate(nc, X, CT, ct_dram, w1raw, AG, scale4, shift4, passes, w_layer1, w_gate, w_up):
    with ExitStack() as ctx:
        CTf = sb(nc, ctx, "CTf", [P, TILES, CHUNKS, 128], F32R)
        high = sb(nc, ctx, "high", [P, 2, TILES, 128], F32R)
        low = sb(nc, ctx, "low", [P, 2, TILES, 128], F32R)
        values = sb(nc, ctx, "values", [P, 2, TILES, 128])
        A = [psum(nc, ctx, f"A{i}", [128, 3 * 512]) for i in range(2)]
        aggregate_rest(nc, X, CT, ct_dram, AG, CTf, high, low, A, values[:, 0], scale4, shift4, passes)
        LOADED = (0, 2, 6, TILES)
        counts_in = sems(nc, ctx, "counts_in0", "counts_in1", "counts_in2")
        (w1_in, quant_in, counts_ready, zeroed, staged_ready, agg_ready, agg_done, valued,
         high_ready, zero_steps) = sems(
            nc, ctx, "w1_in", "quant_in", "counts_ready", "zeroed4", "staged_ready", "agg_ready",
            "agg_done", "valued", "high_ready", "zero_steps")
        GU = quant_view(CT)
        block = ctx.enter_context(nc.Block())

        @block.sync
        def _(sp):
            for sem, first, last in zip(counts_in, LOADED, LOADED[1:]):
                sp.dma_start(CT[0:P, :, first:last, :],
                             ct_dram.rearrange("p c (t d) -> p c t d", t=TILES)[:, :, first:last, :]).then_inc(sem, 16)
            sp.dma_start(w1raw[:, :, :], w_layer1.rearrange("(k p) d -> p k d", p=128)[:, 0:RAW]).then_inc(w1_in, 16)
            sp.wait_ge(counts_ready, TILES)
            sp.dma_start(GU[:, 0:QC], w_gate.rearrange("(m p) d -> p m d", p=128)).then_inc(quant_in, 16)
            sp.dma_start(GU[:, QC:2 * QC], w_up.rearrange("(m p) d -> p m d", p=128)).then_inc(quant_in, 16)
            sp.wait_ge(w1_in, 16)
            sp.wait_ge(quant_in, 32)

        @block.gpsimd
        def _(pool):
            needed = pool.alloc_register("passes_needed")
            pool.reg_load(needed, passes[0:1, 0:1])
            with pool.If_eq(needed, 1):
                pool.memset(AG[:, :, :].rearrange("p k n -> p (k n)"), 0.0).then_inc(zero_steps, 1)
                pool.wait_ge(zero_steps, 1)
            pool.sem_inc(zeroed, 1)

        @block.scalar
        def _(act):
            def value(f, par):
                wait_at(act, staged_ready, f + 1)
                for i in range(TILES):
                    ins = act.activation(values[:, par, i, :], X[:, i, bass.ds(128 * f, 128)], ACT.Identity,
                                         scale=scale4[:, i:i + 1], bias=shift4[:, i:i + 1])
                ins.then_inc(valued, 1)
                wait_at(act, valued, f + 1)
                wait_at(act, agg_ready, f + 1)
                act.activation(high[:, par], values[:, par], ACT.Identity).then_inc(high_ready, 1)

            with act.Fori(0, KD // 2) as g:
                for par in range(2):
                    value(2 * g + par, par)

        @block.vector
        def _(dve):
            def counts(i):
                if i in LOADED:
                    dve.wait_ge(counts_in[LOADED.index(i)], 16)
                dve.tensor_copy(CTf[:, i], counts_of(CT, i)).then_inc(counts_ready, 1)

            def remainder(f, par):
                wait_at(dve, agg_ready, f + 1)
                wait_at(dve, high_ready, f + 1)
                dve.tensor_tensor(low[:, par], values[:, par], high[:, par].bitcast(F32), ALU.subtract
                                  ).then_inc(staged_ready, 1)

            def add(f, par):
                wait_at(dve, agg_ready, f + 3)
                at = AG[:, bass.ds(f, 1), :].rearrange("p a n -> p (a n)")
                dve.tensor_tensor(at, A[par][:, 0:N], at, ALU.add).then_inc(agg_done, 1)

            counts(0)
            counts(1)
            remainder(0, 0)
            for i in range(2, TILES):
                counts(i)
            remainder(1, 1)
            dve.wait_ge(zeroed, 1)
            with dve.Fori(0, KD // 2 - 1) as g:
                for par in range(2):
                    add(2 * g + par, par)
                    remainder(2 * g + par + 2, par)
            add(KD - 2, 0)
            add(KD - 1, 1)
            dve.wait_ge(agg_done, KD + 2)

        @block.tensor
        def _(pe):
            def products(f, par, before=None):
                wait_at(pe, staged_ready, f + 1 + 2)
                wait_at(pe, agg_done, f + 1)
                chunk_products(pe, A[par], high[:, par], low[:, par], CTf, before).then_inc(agg_ready, 1)

            def tile_ready(i):
                pe.wait_ge(counts_ready, i + 1)

            for free in (agg_ready, agg_done, staged_ready):
                pe.sem_inc(free, 2)
            products(0, 0, tile_ready)
            products(1, 1)
            with pe.Fori(1, KD // 2) as g:
                for par in range(2):
                    products(2 * g + par, par)


def layer1_gnn(nc, X, GU, w1raw, AG, dinv, scale5, shift5, largest, w_layer1, bias1):
    with ExitStack() as ctx:
        W1h = sb(nc, ctx, "W1h", [128, KD, D], F32R)
        W1l = sb(nc, ctx, "W1l", [128, KD, D], F32R)
        agh = sb(nc, ctx, "agh", [128, 2, KD, P], F32R)
        agl = sb(nc, ctx, "agl", [128, 2, KD, P], F32R)
        biasr = sb(nc, ctx, "biasr", [P, D])
        z = sb(nc, ctx, "z", [P, 2, D])
        stats = sb(nc, ctx, "stats5", [P, 2, 2, 6])
        mv = sb(nc, ctx, "mv5", [P, 2, 2])
        veps = sb(nc, ctx, "veps5", [P, 2])
        rstd = sb(nc, ctx, "rstd5", [P, 2])
        nmean = sb(nc, ctx, "nmean5", [P, 2])
        mhalf = sb(nc, ctx, "mhalf5", [P, 2])
        Z = [psum(nc, ctx, f"Z{i}", [128, 512]) for i in range(4)]
        raw_in = sems(nc, ctx, *(f"raw_in{k}" for k in range(RAW)))
        (bias_in, w1_high, w1_split, ag_high, ag_split, z_ready, z_free, zeroed, var_ready, rstd_ready,
         pool_steps, first_steps, loop_steps, last_steps) = sems(
            nc, ctx, "bias_in", "w1_high", "w1_split", "ag_high", "ag_split", "z_ready", "z_free",
            "zeroed", "var_ready5", "rstd_ready5", "pool_steps5", "first_steps5", "loop_steps5", "last_steps5")
        quant = Dequantise(nc, ctx, "gu_quant", D // 32)
        LAST = PAIRS - 1
        X3_STEPS = 13
        block = ctx.enter_context(nc.Block())

        def columns(i):
            return AG[:, :, bass.ds(P * i, P)]

        def weights_of(m):
            return GU[:, bass.ds(m, 1), :].rearrange("p m (b k) -> p (m b) k", k=32)

        @block.sync
        def _(sp):
            sp.dma_start(biasr[:, :], bias1.rearrange("(a n) -> a n", a=1).broadcast_to([P, D])).then_inc(bias_in, 16)
            w1 = w_layer1.rearrange("(k p) d -> p k d", p=128)
            for k in range(RAW, KD):
                sp.wait_ge(w1_split, k - RAW + 1)
                sp.dma_start(w1raw[:, k % RAW], w1[:, k]).then_inc(raw_in[k % RAW], 16)
            for buffer, sem in enumerate(raw_in):
                sp.wait_ge(sem, 16 * len(range(RAW + buffer, KD, RAW)))
            sp.wait_ge(bias_in, 16)

        @block.gpsimd
        def _(pool):
            pool.memset(mhalf[:, :], -0.5).then_inc(zeroed, 1)
            pool.memset(largest[:, :], 0.0).then_inc(zeroed, 1)
            pool.wait_ge(zeroed, 2)
            quant.divide(pool, weights_of(2 * QC - 1), 0)
            quant.multiply(pool, weights_of(2 * QC - 1), 0)
            with pool.Fori(0, PAIRS) as g:
                for s in range(2):
                    i = 2 * g + s
                    wait_at(pool, var_ready, i + 1)
                    pool.tensor_tensor(rstd[:, s:s + 1], veps[:, s:s + 1], mhalf[:, 0:1], ALU.pow
                                       ).then_inc(rstd_ready, 1)
                    pool.tensor_scalar(nmean[:, s:s + 1], mv[:, s, 0:1], -1.0, None, ALU.mult).then_inc(pool_steps, 1)
                    wait_at(pool, rstd_ready, i + 1)
                    wait_at(pool, pool_steps, 2 * i + 1 + 4)
                    pool.tensor_copy(scale5[:, bass.ds(i, 1)], rstd[:, s:s + 1])
                    pool.tensor_tensor(shift5[:, bass.ds(i, 1)], nmean[:, s:s + 1], rstd[:, s:s + 1], ALU.mult
                                       ).then_inc(pool_steps, 1)
                    if s == 0:
                        quant.divide(pool, weights_of(g), g + 1)
                quant.multiply(pool, weights_of(g), g + 1)

        @block.tensor
        def _(pe):
            pe.sem_inc(z_free, 4)
            pe.sem_inc(pool_steps, 4)

            def products(part, k):
                s, half = part // 2, part % 2
                for n, (a, b) in enumerate(PARTS):
                    ins = pe.matmul(Z[part][0:P, :], (agh, agl)[a][:, s, k, :],
                                    (W1h, W1l)[b][:, k, 512 * half:512 * half + 512],
                                    start=(k == 0 and n == 0), stop=(k == KD - 1 and n == 2))
                return ins

            pe.wait_ge(ag_split, 2)
            for k in range(KD):
                pe.wait_ge(w1_split, k + 1)
                for part in range(4):
                    ins = products(part, k)
                    if k == KD - 1:
                        ins.then_inc(z_ready, 1)
            with pe.Fori(1, PAIRS) as g:
                for part in range(4):
                    wait_at(pe, ag_split, 2 * g + part // 2 + 1)
                    wait_at(pe, z_free, 4 * g + part + 1)
                    for k in range(KD):
                        ins = products(part, k)
                    ins.then_inc(z_ready, 1)

        @block.scalar
        def _(act):
            def high(i, s):
                act.activation(agh[:, s], columns(i), ACT.Identity).then_inc(ag_high, 1)

            high(0, 0)
            high(1, 1)
            for k in range(KD):
                if k >= RAW:
                    act.wait_ge(raw_in[k % RAW], 16 * (k // RAW))
                act.activation(W1h[:, k], w1raw[:, k % RAW], ACT.Identity).then_inc(w1_high, 1)
            with act.Fori(0, LAST) as g:
                for s in range(2):
                    wait_at(act, z_ready, 4 * g + 2 * s + 2)
                    high(2 * g + 2 + s, s)

        @block.vector
        def _(dve):
            def low(i, s):
                wait_at(dve, ag_high, i + 1)
                dve.tensor_tensor(agl[:, s], columns(i), agh[:, s].bitcast(F32), ALU.subtract).then_inc(ag_split, 1)

            def dense(g, s):
                for half in range(2):
                    part = 2 * s + half
                    wait_at(dve, z_ready, 4 * g + part + 1)
                    at = slice(512 * half, 512 * half + 512)
                    dve.scalar_tensor_tensor(z[:, s, at], Z[part][0:P, :], dinv[:, bass.ds(2 * g + s, 1)],
                                             biasr[:, at], ALU.mult, ALU.add).then_inc(z_free, 1)

            def body(step, g, more):
                for s in range(2):
                    i = 2 * g + s
                    t = tile_of(X, i)
                    dense(g, s)
                    if more:
                        low(i + 2, s)
                    wait_at(dve, z_free, 4 * g + 2 * s + 2 + 4)
                    step(dve.scalar_tensor_tensor(t, z[:, s], 0.0, t, ALU.max, ALU.add))
                    for half in range(2):
                        ins = dve.bn_stats(stats[:, s, half], t[:, 512 * half:512 * half + 512])
                    step(ins)
                    wait_at(dve, pool_steps, 4 * g + 2 * s + 2)
                    step(dve.bn_aggr(mv[:, s], stats[:, s].rearrange("p a b -> p (a b)")))
                    dve.tensor_scalar(veps[:, s:s + 1], mv[:, s, 1:2], EPS, None, ALU.add).then_inc(var_ready, 1)
                    if s == 0:
                        quant.scales(dve, step, weights_of(g), g + 1)
                    else:
                        quant.round(dve, step, weights_of(g), g + 1)
                    wait_at(dve, rstd_ready, i + 1)
                    step(dve.tensor_scalar(z[:, s], t, mv[:, s, 0:1], rstd[:, s:s + 1], ALU.subtract, ALU.mult))
                    step(dve.tensor_reduce(largest[0:P, bass.ds(i, 1)], z[:, s], AX.X, ALU.max,
                                           apply_absolute_value=True))
                assert step.n == X3_STEPS, step.n

            low(0, 0)
            low(1, 1)
            for k in range(KD):
                dve.wait_ge(w1_high, k + 1)
                dve.tensor_tensor(W1l[:, k], w1raw[:, k % RAW], W1h[:, k].bitcast(F32), ALU.subtract
                                  ).then_inc(w1_split, 1)
            step = Steps(dve, first_steps, 0)
            quant.scales(dve, step, weights_of(2 * QC - 1), 0)
            quant.round(dve, step, weights_of(2 * QC - 1), 0)
            dve.wait_ge(bias_in, 16)
            dve.wait_ge(zeroed, 2)
            with dve.Fori(0, LAST) as g:
                body(Steps(dve, loop_steps, X3_STEPS * g), g, True)
            body(Steps(dve, last_steps, 0), LAST, False)
            dve.wait_ge(quant.ready, PAIRS + 1)


def quantised_ffn(nc, X, GU, AG, ident, scale5, shift5, largest, w_down, out):
    with ExitStack() as ctx:
        guT = [sb(nc, ctx, n, [128, KD, 2 * QI], F32R) for n in ("guT_high", "guT_low")]
        wd = GU[:, 0:QC, :].rearrange("p m d -> p (m d)").rearrange("p (c k) -> p c k", k=QI)
        wdT = [w[:, 0:QC * D // (2 * QI), :].rearrange("p k n -> p (k n)").rearrange("p (k n) -> p k n", n=D)
               for w in guT]
        q = sb(nc, ctx, "q", [P, 2, D])
        qT = [sb(nc, ctx, n, [128, 2, KD, PAIR], F32R) for n in ("qT_high", "qT_low")]
        o_magic = sb(nc, ctx, "o_magic", [128, 2, QC, P])
        oq = sb(nc, ctx, "oq", [128, 2, QC, P])
        oq_parts = [sb(nc, ctx, n, [128, 2, QC, P], F32R) for n in ("oq_high", "oq_low")]
        magic = sb(nc, ctx, "magic", [128, 2])
        big = sb(nc, ctx, "big", [128, 16])
        red = sb(nc, ctx, "red", [128, 16])
        sc = sb(nc, ctx, "sc", [128, 16])
        coef = sb(nc, ctx, "coef5", [P, 2, TILES])
        big2 = sb(nc, ctx, "big2", [128, 2, PAIRS])
        big3 = sb(nc, ctx, "big3", [128, 2, QC])
        TQ = [psum(nc, ctx, f"TQ{i}", [128, 512]) for i in range(2)]
        H = [psum(nc, ctx, f"H{i}", [128, 512]) for i in range(3)]
        O = [psum(nc, ctx, f"O{i}", [128, 512]) for i in range(2)]
        (wd_in, steps, reduced, magic_set, q_ready, w_ready, w_high, w_done, tq_ready, tq_high, tq_done,
         oq_steps, u_ready, h_ready, h_done, g_scaled, g_ready, u_scaled,
         sigmoid_done, s_scaled, gated, g2_magic, g2_scaled, o_scaled, oq_ready, o_ready, o_done, stored, q_steps,
         coef_ready, measured, found) = sems(
            nc, ctx, "wd_in", "steps6", "reduced", "magic_set", "q_ready", "w_ready6", "w_high", "w_done", "tq_ready",
            "tq_high", "tq_done", "oq_steps", "u_ready", "h_ready6",
            "h_done", "g_scaled", "g_ready", "u_scaled", "sigmoid_done", "s_scaled", "gated", "g2_magic", "g2_scaled",
            "o_scaled", "oq_ready", "o_ready", "o_done", "stored", "q_steps", "coef_ready", "measured", "found")
        quant = Dequantise(nc, ctx, "wd_quant", KD * QI // 32)
        wd_blocks = wd.rearrange("p c k -> p (c k)").rearrange("p (b k) -> p b k", k=32)
        G, U = AG[:, 0:QC], AG[:, QC:2 * QC]
        S = AG[:, 2 * QC:2 * QC + 2]
        W_FILLS, D_FILLS, Q_FILLS = 4 * QC, KD, 4
        WB = TQ + O
        block = ctx.enter_context(nc.Block())

        def weight_fill(fill):
            if fill < W_FILLS:
                m, j = fill // 2, fill % 2
                return [w[:, 4 * j:4 * j + 4, 128 * m:128 * m + 128] for w in guT], 4
            c = fill - W_FILLS
            return [w[:, :, 128 * c:128 * c + 128] for w in wdT], QC

        def turned(fill, chunks):
            return WB[fill % len(WB)][:, 0:128 * chunks].rearrange("p (k n) -> p k n", k=chunks)

        def pair_fill(par, j):
            return [t[:, bass.ds(par, 1), 2 * j:2 * j + 2, :].rearrange("p b a n -> p (b a n)") for t in qT]

        def scales(dve, step, a, n):
            step(dve.tensor_scalar(sc[:, a:a + n], red[:, a:a + n], 1.0 / 32767.0, 1e-12, ALU.mult, ALU.max))
            step(dve.reciprocal(sc[:, a + 8:a + 8 + n], sc[:, a:a + n]))

        @block.gpsimd
        def _(pool):
            pool.memset(magic[:, 0:1], MAGIC).then_inc(magic_set, 1)
            pool.memset(magic[:, 1:2], -MAGIC).then_inc(magic_set, 1)

            def reduce(n, a, k):
                pool.wait_ge(found, n + 1)
                pool.partition_all_reduce(red[:, a:a + k], big[:, a:a + k], 128, RMAX).then_inc(reduced, 1)

            reduce(0, 0, 1)
            quant.divide(pool, wd_blocks, 0)
            quant.multiply(pool, wd_blocks, 0)
            reduce(1, 1, 2)
            pool.wait_ge(coef_ready, 2)
            for c in range(QC):
                pool.tensor_scalar(U[:, c], U[:, c], sc[:, 10:11], MAGIC, ALU.mult, ALU.add).then_inc(u_scaled, 1)
            for c in range(QC):
                pool.wait_ge(u_scaled, c + 1)
                pool.tensor_scalar(U[:, c], U[:, c], -MAGIC, 32767.0, ALU.add, ALU.min).then_inc(u_ready, 1)
            reduce(2, 3, 1)
            reduce(3, 4, 1)

        @block.vector
        def _(dve):
            step = Steps(dve, steps, 0)

            def low_weights(fills):
                for fill in fills:
                    (high, low), chunks = weight_fill(fill)
                    dve.wait_ge(w_high, fill + 1)
                    dve.tensor_tensor(low, turned(fill, chunks), high.bitcast(F32), ALU.subtract).then_inc(w_done, 1)

            def low_pair(g, par):
                for j in range(Q_FILLS):
                    high, low = pair_fill(par, j)
                    wait_at(dve, tq_high, Q_FILLS * g + j + 1)
                    dve.tensor_tensor(low, TQ[j % 2][:, 0:2 * PAIR], high.bitcast(F32), ALU.subtract
                                      ).then_inc(tq_done, 1)

            def integers(g, between=()):
                if not isinstance(g, int) or g > 0:
                    wait_at(dve, tq_ready, Q_FILLS * g)
                lstep = Steps(dve, q_steps, 2 * g)
                for s in range(2):
                    ins = dve.tensor_scalar(q[:, s], tile_of(X, 2 * g + s), coef[:, 0, bass.ds(2 * g + s, 1)],
                                            coef[:, 1, bass.ds(2 * g + s, 1)], ALU.mult, ALU.add)
                lstep(ins)
                low_weights(between[0:2])
                for s in range(2):
                    ins = dve.tensor_scalar(q[:, s], q[:, s], MAGIC, None, ALU.add)
                lstep(ins)
                low_weights(between[2:4])
                dve.tensor_scalar(q[:, :, :].rearrange("p s d -> p (s d)"), q[:, :, :].rearrange("p s d -> p (s d)"),
                                  -MAGIC, 32767.0, ALU.add, ALU.min).then_inc(q_ready, 1)

            def measure(g):
                wait_at(dve, h_done, 3 * g + 6)
                dve.tensor_reduce(big2[:, :, bass.ds(g, 1)],
                                  AG[:, 0:2 * QC, bass.ds(PAIR * g, PAIR)].rearrange("p (a m) n -> p a m n", a=2),
                                  AX.XY, ALU.max, apply_absolute_value=True).then_inc(measured, 1)

            dve.tensor_reduce(big[:, 0:1], largest[:, :], AX.X, ALU.max).then_inc(found, 1)
            low_weights(range(0, 3))
            dve.wait_ge(reduced, 1)
            scales(dve, step, 0, 1)
            for k, c in ((0, scale5), (1, shift5)):
                ins = dve.tensor_scalar(coef[:, k], c[:, :], sc[0:P, 8:9], None, ALU.mult)
            ins.then_inc(coef_ready, 1)
            dve.wait_ge(coef_ready, 1)
            integers(0, range(3, 7))
            low_weights(range(7, W_FILLS))
            low_pair(0, 0)
            integers(1)
            low_pair(1, 1)
            integers(2)
            with dve.Fori(1, PAIRS - 2) as g:
                low_pair(g + 1, (g + 1) % 2)
                integers(g + 2)
                measure(g - 1)
            low_pair(PAIRS - 1, (PAIRS - 1) % 2)
            dve.wait_ge(wd_in, 16)
            quant.scales(dve, step, wd_blocks, 0)
            measure(PAIRS - 3)
            quant.round(dve, step, wd_blocks, 0)
            measure(PAIRS - 2)
            measure(PAIRS - 1)
            dve.wait_ge(measured, PAIRS)
            dve.tensor_reduce(big[:, 1:3], big2[:, :, :], AX.X, ALU.max).then_inc(found, 1)
            dve.wait_ge(reduced, 2)
            scales(dve, step, 1, 2)
            dve.sem_inc(coef_ready, 1)

            def gate_integers(c):
                dve.wait_ge(g_scaled, c + 1)
                dve.tensor_scalar(G[:, c], G[:, c], -MAGIC, 32767.0, ALU.add, ALU.min).then_inc(g_ready, 1)

            gate_integers(0)
            gate_integers(1)
            low_weights(range(W_FILLS, W_FILLS + D_FILLS // 2))
            for c in range(QC):
                dve.wait_ge(s_scaled, c + 1)
                s = S[:, c % 2]
                step(dve.tensor_scalar(s, s, -MAGIC, 65535.0, ALU.add, ALU.min))
                dve.scalar_tensor_tensor(G[:, c], s, 1.0 / 65536.0, G[:, c], ALU.mult, ALU.mult).then_inc(gated, 1)
                if c + 2 < QC:
                    gate_integers(c + 2)
                dve.wait_ge(gated, c + 1)
                step(dve.tensor_reduce(big3[:, 0, c:c + 1], G[:, c], AX.X, ALU.max, apply_absolute_value=True))
            step(dve.tensor_reduce(big[:, 6:7], big3[:, 0], AX.X, ALU.max))
            dve.tensor_tensor(big[:, 3:4], big[:, 6:7], sc[:, 1:2], ALU.mult).then_inc(found, 1)
            low_weights(range(W_FILLS + D_FILLS // 2, W_FILLS + D_FILLS))
            dve.wait_ge(reduced, 3)
            scales(dve, step, 3, 1)
            dve.tensor_tensor(sc[:, 7:8], sc[:, 1:2], sc[:, 11:12], ALU.mult).then_inc(coef_ready, 1)
            step(dve.tensor_tensor(sc[:, 5:6], sc[:, 3:4], sc[:, 2:3], ALU.mult))
            for c in range(QC):
                dve.wait_ge(g2_scaled, c + 1)
                dve.wait_ge(u_ready, c + 1)
                step(dve.scalar_tensor_tensor(G[:, c], G[:, c], 32767.0, U[:, c], ALU.min, ALU.mult))
                step(dve.tensor_reduce(big3[:, 1, c:c + 1], G[:, c], AX.X, ALU.max, apply_absolute_value=True))
            step(dve.tensor_reduce(big[:, 5:6], big3[:, 1], AX.X, ALU.max))
            dve.tensor_tensor(big[:, 4:5], big[:, 5:6], sc[:, 5:6], ALU.mult).then_inc(found, 1)
            dve.wait_ge(reduced, 4)
            scales(dve, step, 4, 1)
            dve.tensor_tensor(sc[:, 6:7], sc[:, 5:6], sc[:, 12:13], ALU.mult).then_inc(coef_ready, 1)

            def quantised(i, s):
                wait_at(dve, o_scaled, i + 1)
                wait_at(dve, o_ready, 2 * i + 2)
                part = Steps(dve, oq_steps, 2 * i)
                part(dve.tensor_scalar(oq[:, s], o_magic[:, s], -MAGIC, 32767.0, ALU.add, ALU.min))
                part(dve.tensor_copy(oq_parts[0][:, s], oq[:, s]))
                dve.tensor_tensor(oq_parts[1][:, s], oq[:, s], oq_parts[0][:, s].bitcast(F32), ALU.subtract
                                  ).then_inc(oq_ready, 1)

            def add_down(i):
                for half in range(2):
                    wait_at(dve, o_ready, 2 * i + half + 1 + 4)
                    t = tile_of(X, i)[:, 512 * half:512 * half + 512]
                    dve.scalar_tensor_tensor(t, O[half][0:P, :], sc[0:P, 4:5], t, ALU.mult, ALU.add
                                             ).then_inc(o_done, 1)

            quantised(0, 0)
            quantised(1, 1)
            with dve.Fori(0, PAIRS - 1) as g:
                for s in range(2):
                    add_down(2 * g + s)
                    quantised(2 * g + 2 + s, s)
            add_down(TILES - 2)
            add_down(TILES - 1)

        @block.scalar
        def _(act):
            def high_weights(fill):
                (high, low), chunks = weight_fill(fill)
                act.wait_ge(w_ready, fill + 1)
                act.activation(high, turned(fill, chunks), ACT.Identity).then_inc(w_high, 1)

            def evacuate(g, par, banks):
                if not isinstance(g, int):
                    wait_at(act, h_ready, 3 * g)
                for j in banks:
                    wait_at(act, tq_ready, Q_FILLS * g + j + 1)
                    act.activation(pair_fill(par, j)[0], TQ[j % 2][:, 0:2 * PAIR], ACT.Identity).then_inc(tq_high, 1)

            def products_out(g, j):
                wait_at(act, h_ready, 3 * g + j + 1 + 3)
                act.activation(AG[:, 2 * j:2 * j + 2, bass.ds(PAIR * g, PAIR)],
                               H[j][:, 0:2 * PAIR].rearrange("p (a n) -> p a n", a=2), ACT.Identity,
                               scale=sc[:, 0:1]).then_inc(h_done, 1)

            def in_steps(out, value, factor):
                return act.activation(out, value, ACT.Identity, scale=factor, bias=magic[:, 0:1])

            for fill in range(W_FILLS):
                high_weights(fill)
            act.wait_ge(coef_ready, 1)
            evacuate(0, 0, range(Q_FILLS))
            with act.Fori(0, PAIRS - 1) as g:
                products_out(g, 0)
                evacuate(g + 1, (g + 1) % 2, (0, 1))
                products_out(g, 1)
                evacuate(g + 1, (g + 1) % 2, (2, 3))
                products_out(g, 2)
            for j in range(QC):
                products_out(PAIRS - 1, j)
            for fill in range(W_FILLS, W_FILLS + D_FILLS // 2):
                high_weights(fill)
            act.wait_ge(magic_set, 2)
            act.wait_ge(coef_ready, 2)

            def gate_steps(c):
                in_steps(G[:, c], G[:, c], sc[:, 9:10]).then_inc(g_scaled, 1)

            gate_steps(0)
            gate_steps(1)
            for c in range(QC):
                act.wait_ge(g_ready, c + 1)
                if c >= 2:
                    act.wait_ge(gated, c - 1)
                act.activation(S[:, c % 2], G[:, c], ACT.Sigmoid, scale=sc[:, 1:2]).then_inc(sigmoid_done, 1)
                if c + 2 < QC:
                    gate_steps(c + 2)
                act.wait_ge(sigmoid_done, c + 1)
                in_steps(S[:, c % 2], S[:, c % 2], 65536.0).then_inc(s_scaled, 1)
            for fill in range(W_FILLS + D_FILLS // 2, W_FILLS + D_FILLS):
                high_weights(fill)
            act.wait_ge(coef_ready, 3)
            for c in range(QC):
                in_steps(G[:, c], G[:, c], sc[:, 7:8]).then_inc(g2_magic, 1)
                act.wait_ge(g2_magic, c + 1)
                act.activation(G[:, c], G[:, c], ACT.Identity, bias=magic[:, 1:2]).then_inc(g2_scaled, 1)
            act.wait_ge(coef_ready, 4)

            def down_steps(i, s):
                if not isinstance(i, int):
                    wait_at(act, oq_ready, i - 1)
                in_steps(o_magic[:, s], G[:, :, bass.ds(P * i, P)], sc[:, 6:7]).then_inc(o_scaled, 1)

            down_steps(0, 0)
            down_steps(1, 1)
            with act.Fori(1, PAIRS) as g:
                for s in range(2):
                    down_steps(2 * g + s, s)

        @block.tensor
        def _(pe):
            for free, n in ((w_done, len(WB)), (tq_done, 2), (h_done, 3), (h_ready, 3), (o_done, 2), (o_ready, 4)):
                pe.sem_inc(free, n)

            def turn_weights(w, at, fill, chunks):
                pe.wait_ge(w_done, fill + 1)
                for k in range(chunks):
                    ins = pe.transpose(WB[fill % len(WB)][:, 128 * k:128 * k + 128],
                                       w[:, at + 128 * k:at + 128 * k + 128], ident[:, :])
                ins.then_inc(w_ready, 1)

            def turn(g, banks):
                wait_at(pe, q_ready, g + 1)
                for j in banks:
                    wait_at(pe, tq_done, Q_FILLS * g + j + 1)
                    for c in range(2):
                        for s in range(2):
                            at, f = PAIR * c + P * s, 128 * (2 * j + c)
                            ins = pe.transpose(TQ[j % 2][:, at:at + P], q[:, s, f:f + 128], ident[0:P, 0:P])
                    ins.then_inc(tq_ready, 1)

            def products(g, par, more):
                wait_at(pe, tq_done, Q_FILLS * g + Q_FILLS + 2)
                for j in range(QC):
                    if more and j > 0:
                        turn(g + 1, (2 * j - 2, 2 * j - 1))
                    wait_at(pe, h_done, 3 * g + j + 1)
                    for m in range(2):
                        for k in range(KD):
                            for n, (a, b) in enumerate(PARTS):
                                w = guT[a][:, k, 128 * (2 * j + m):128 * (2 * j + m) + 128]
                                ins = pe.matmul(H[j][:, PAIR * m:PAIR * m + PAIR], w,
                                                qT[b][:, bass.ds(par, 1), k, :].rearrange("p a n -> p (a n)"),
                                                start=(k == 0 and n == 0), stop=(k == KD - 1 and n == 2))
                    ins.then_inc(h_ready, 1)

            for m in range(2 * QC):
                for j in range(2):
                    turn_weights(GU[:, m], 512 * j, 2 * m + j, 4)
            pe.wait_ge(w_done, W_FILLS + len(WB))
            turn(0, range(Q_FILLS))
            with pe.Fori(0, PAIRS - 1) as g:
                products(g, g % 2, True)
            products(PAIRS - 1, (PAIRS - 1) % 2, False)
            pe.wait_ge(quant.ready, 1)
            pe.wait_ge(tq_done, Q_FILLS * PAIRS + 2)
            for c in range(D_FILLS):
                turn_weights(wd[:, c], 0, W_FILLS + c, QC)
            pe.wait_ge(w_done, W_FILLS + D_FILLS + len(WB))
            with pe.Fori(0, PAIRS) as g:
                for s in range(2):
                    wait_at(pe, oq_ready, 2 * g + s + 1)
                    for half in range(2):
                        wait_at(pe, o_done, 4 * g + 2 * s + half + 1)
                        for k in range(QC):
                            for n, (a, b) in enumerate(PARTS):
                                ins = pe.matmul(O[half][0:P, :], oq_parts[a][:, s, k, :],
                                                wdT[b][:, k, 512 * half:512 * half + 512],
                                                start=(k == 0 and n == 0), stop=(k == QC - 1 and n == 2))
                        ins.then_inc(o_ready, 1)

        @block.sync
        def _(sp):
            sp.wait_ge(w_ready, W_FILLS)
            sp.dma_start(wd, w_down.rearrange("(c p) k -> p c k", p=128)).then_inc(wd_in, 16)
            with sp.Fori(0, PAIRS) as g:
                for s in range(2):
                    sp.wait_ge(o_done, 4 * g + 2 * s + 2 + 2)
                    sp.nop(nofuse=True)
                    sp.dma_start(out.rearrange("(t p) d -> p t d", p=P)[:, bass.ds(2 * g + s, 1), :],
                                 X[:, bass.ds(2 * g + s, 1), :]).then_inc(stored, 16)
            sp.wait_ge(stored, 16 * TILES)


def program(nc, a, out):
    with ExitStack() as top:
        ident = sb(nc, top, "ident", [128, 128])
        X = sb(nc, top, "X", [P, TILES, D])
        dinv, scale4, shift4, scale5, shift5 = (
            sb(nc, top, n, [P, TILES]) for n in ("dinv", "scale4", "shift4", "scale5", "shift5"))
        largest = sb(nc, top, "largest", [128, TILES])
        deg = sb(nc, top, "deg", [P, TILES])
        passes = sb(nc, top, "passes", [1, 1], I32)
        ct_dram = nc.dram_tensor("ct_dram", (P, CHUNKS, TILES * 128), I16).ap()
        with ExitStack() as ctx:
            WT = [sb(nc, ctx, n, [128, WCH, D], F32R) for n in ("WT_high", "WT_low")]
            deg_dram = nc.dram_tensor("deg_dram", (BLOCKS * WIN,), F32).ap()
            build_matrices(nc, a["src"], a["dst"], a["edge_weight"], a["x"], X, ident, WT, ct_dram, deg, dinv,
                           deg_dram)
            layer0(nc, [a["L0_" + n] for n in LAYER0], X, ident, WT, scale4, shift4, deg, dinv, passes)
        CT = sb(nc, top, "CT", [128, CHUNKS, TILES, 128], I16)
        AG = sb(nc, top, "AG", [128, KD, N])
        with ExitStack() as ctx:
            w1raw = sb(nc, ctx, "w1raw", [128, RAW, D])
            aggregate(nc, X, CT, ct_dram, w1raw, AG, scale4, shift4, passes, a["L1_gnn_W"], a["L1_ffn_w_gate"],
                      a["L1_ffn_w_up"])
            layer1_gnn(nc, X, quant_view(CT), w1raw, AG, dinv, scale5, shift5, largest, a["L1_gnn_W"], a["L1_gnn_b"])
        quantised_ffn(nc, X, quant_view(CT), AG, ident, scale5, shift5, largest, a["L1_ffn_w_down"], out)


def kernel(**inputs):
    import concourse.bacc as bacc
    from concourse.bass_utils import run_bass_kernel_spmd

    nc = bacc.Bacc("TRN2", target_bir_lowering=False, num_devices=1)
    arrays = {k: np.ascontiguousarray(v) for k, v in inputs.items()}
    args = {k: nc.dram_tensor(f"in_{k}", v.shape, mybir.dt.from_np(v.dtype), kind="ExternalInput").ap()
            for k, v in arrays.items()}
    out = nc.dram_tensor("out", (N, D), F32, kind="ExternalOutput").ap()
    program(nc, args, out)
    r = run_bass_kernel_spmd(nc, [{f"in_{k}": v for k, v in arrays.items()}], core_ids=[0])
    return r.results[0]["out"]
```
